# Optimizing a Trainium2 kernel written in Bass

```python
import numpy as np
import jax
import jax.numpy as jnp

def _softmax(x, axis=-1):
    return jax.nn.softmax(x, axis=axis)

def _gelu(x):
    return jax.nn.gelu(x, approximate=True)

def _silu(x):
    return jax.nn.silu(x)

def _sigmoid(x):
    return jax.nn.sigmoid(x)

def _layernorm(x, axis=-1, eps=1e-05):
    m = jnp.mean(x, axis=axis, keepdims=True)
    v = jnp.var(x, axis=axis, keepdims=True)
    return (x - m) / jnp.sqrt(v + eps)

def _scatter_add(tgt, idx, src, axis=0):
    return tgt.at[idx].add(src)

def _segment_sum(src, seg, n):
    return jax.ops.segment_sum(src, seg, n)
kernel_name = 'mk_decoder_postln_d1_seqx_r8_a633b9'

def setup_inputs(seed: int=0):
    np.random.seed(seed)
    _w = jnp.asarray

    def _rec_inputs():
        import jax
        import jax.numpy as jnp
        _rk = jax.random.key(seed)
        x = -0.000125 + 0.9999 * jax.random.normal(jax.random.fold_in(_rk, 1), (4, 256, 256), jnp.float32)
        _lenS = 256 - jax.random.randint(jax.random.fold_in(_rk, 7), (4,), 0, max(1, 256 // 4) + 1, jnp.int32)
        _lenS2 = 256 - jax.random.randint(jax.random.fold_in(_rk, 8), (4,), 0, max(1, 256 // 4) + 1, jnp.int32)
        fside_BxS2xS2_0 = -3.05549e-07 + 0.0199987 * jax.random.normal(jax.random.fold_in(_rk, 11), (4, 256, 256), jnp.float32)
        _ctx_1024P = jax.random.normal(jax.random.fold_in(_rk, 12), (4, 16, 128), jnp.float32)
        _ctx_1024c = jax.random.dirichlet(jax.random.fold_in(_rk, 512), 0.3 * jnp.ones((16,), jnp.float32), (4, 256))
        _ctx_1024t = jnp.einsum('bsk,bkd->bsd', _ctx_1024c, _ctx_1024P)
        _ctx_1024t = _ctx_1024t * jax.lax.rsqrt(jnp.mean(jnp.square(_ctx_1024t)) + 1e-12) * 0.953939
        ctx_1024 = 6.82029e-06 + 0.0200006 * (_ctx_1024t + 0.3 * jax.random.normal(jax.random.fold_in(_rk, 612), (4, 256, 128), jnp.float32))
        return (x, fside_BxS2xS2_0, ctx_1024)
    x, fside_BxS2xS2_0, ctx_1024 = _rec_inputs()

    def _L0_attn_setup():
        import jax, jax.numpy as jnp
        import numpy as np
        BLOCK = 32
        NUM_HEADS = 16
        HEAD_DIM = 128
        FP4_GRID = jnp.array([0.0, 0.5, 1.0, 1.5, 2.0, 3.0, 4.0, 6.0], dtype=jnp.float32)

        def quantize_to_mxfp4(w, block_size=BLOCK):
            D, F = w.shape
            blocks = w.reshape(D // block_size, block_size, F)
            amax = jnp.max(jnp.abs(blocks), axis=1)
            e = jnp.floor(jnp.log2(jnp.maximum(amax, 1e-12) / 6.0))
            scale = jnp.exp2(e)
            v = blocks / scale[:, None, :]
            idx = jnp.argmin(jnp.abs(jnp.abs(v)[..., None] - FP4_GRID), axis=-1)
            codes = jnp.sign(v) * FP4_GRID[idx]
            return (codes.reshape(D, F).astype(jnp.float32), scale.astype(jnp.float32))

        def _mxfp4_matmul(x, codes, scales, block_size=BLOCK):
            w = codes * jnp.repeat(scales, block_size, axis=0)
            return x @ w
        key = jax.random.key(seed)
        ks = jax.random.split(key, 9)
        B, S, D = (2, 256, 256)
        feat = NUM_HEADS * HEAD_DIM
        x = jax.random.normal(ks[0], (B, S, D), dtype=jnp.float32)

        def make_w(k, din, dout):
            w = jax.random.normal(k, (din, dout), dtype=jnp.float32) * (1.0 / np.sqrt(din))
            return quantize_to_mxfp4(w, BLOCK)
        wq_codes, wq_scales = make_w(ks[1], D, feat)
        wk_codes, wk_scales = make_w(ks[2], D, feat)
        wv_codes, wv_scales = make_w(ks[3], D, feat)
        wo_codes, wo_scales = make_w(ks[4], feat, D)
        bq = jnp.zeros((feat,), jnp.float32)
        bk = jnp.zeros((feat,), jnp.float32)
        bv = jnp.zeros((feat,), jnp.float32)
        bo = jnp.zeros((D,), jnp.float32)
        return {'x': x, 'wq_codes': wq_codes, 'wq_scales': wq_scales, 'bq': bq, 'wk_codes': wk_codes, 'wk_scales': wk_scales, 'bk': bk, 'wv_codes': wv_codes, 'wv_scales': wv_scales, 'bv': bv, 'wo_codes': wo_codes, 'wo_scales': wo_scales, 'bo': bo}
    _L0_attn_all = _L0_attn_setup()
    _L0_attn_in = {k: v for k, v in _L0_attn_all.items() if k in ('wq_codes', 'wq_scales', 'bq', 'wk_codes', 'wk_scales', 'bk', 'wv_codes', 'wv_scales', 'bv', 'wo_codes', 'wo_scales', 'bo')}
    del _L0_attn_all

    def _L0_xattn_setup():
        import jax, jax.numpy as jnp
        import numpy as np
        EPS = 1e-06
        QMAX = 127.0

        def _smooth_quant_linear(x, w):
            amax_x = jnp.max(jnp.abs(x), axis=0)
            amax_w = jnp.max(jnp.abs(w), axis=0)
            s = jnp.sqrt(jnp.maximum(amax_x, EPS) / jnp.maximum(amax_w, EPS))
            s = jnp.maximum(s, EPS)
            xs = x / s
            ws = w * s
            x_scale = jnp.maximum(jnp.max(jnp.abs(xs), axis=-1, keepdims=True), EPS) / QMAX
            w_scale = jnp.maximum(jnp.max(jnp.abs(ws), axis=-1, keepdims=True), EPS) / QMAX
            x_q = jnp.clip(jnp.round(xs / x_scale), -QMAX, QMAX)
            w_q = jnp.clip(jnp.round(ws / w_scale), -QMAX, QMAX)
            return x_q @ w_q.T * x_scale * w_scale.T

        def _expert_forward(xe, guw, dw):
            h = _smooth_quant_linear(xe, guw)
            gate, up = jnp.split(h, 2, axis=-1)
            a = jax.nn.silu(gate) * up
            return _smooth_quant_linear(a, dw)
        key = jax.random.key(seed)
        k1, k2, k3 = jax.random.split(key, 3)
        E, T, D, I = (8, 256, 256, 128)
        x = jax.random.normal(k1, (E, T, D), dtype=jnp.float32)
        gate_up_weight = jax.random.normal(k2, (E, 2 * I, D), dtype=jnp.float32) * 0.02
        down_weight = jax.random.normal(k3, (E, D, I), dtype=jnp.float32) * 0.02
        return {'x': x, 'gate_up_weight': gate_up_weight, 'down_weight': down_weight}
    _L0_xattn_all = _L0_xattn_setup()
    _L0_xattn_in = {k: v for k, v in _L0_xattn_all.items() if k in ()}
    del _L0_xattn_all

    def _L0_ffn_setup():
        import jax, jax.numpy as jnp
        import numpy as np
        TOP_K = 2
        key = jax.random.key(seed)
        ks = jax.random.split(key, 7)
        B, S, H = (2, 256, 256)
        E, A, NS = (8, 64, 2048)
        x = jax.random.normal(ks[0], (B, S, H), jnp.float32)
        gate_w = jax.random.normal(ks[1], (E, H), jnp.float32) * 0.01
        W = jax.random.normal(ks[2], (H, H), jnp.float32) * 0.02
        atoms = jax.random.normal(ks[3], (A, NS), jnp.float32) * 0.02
        expert_atom_weights = jax.random.normal(ks[4], (E, A), jnp.float32) * 0.1
        importance = jax.random.normal(ks[5], (E, NS), jnp.float32) * 0.1
        mask_idx = jax.random.randint(ks[6], (NS,), 0, H * H, jnp.int32)
        return dict(x=x, gate_w=gate_w, W=W, atoms=atoms, expert_atom_weights=expert_atom_weights, importance=importance, mask_idx=mask_idx)
    _L0_ffn_all = _L0_ffn_setup()
    _L0_ffn_in = {k: v for k, v in _L0_ffn_all.items() if k in ('gate_w', 'W', 'atoms', 'expert_atom_weights', 'importance', 'mask_idx')}
    del _L0_ffn_all
    return {'x': x, 'fside_BxS2xS2_0': fside_BxS2xS2_0, 'ctx_1024': ctx_1024, 'L0_attn_wq_codes': _L0_attn_in['wq_codes'], 'L0_attn_wq_scales': _L0_attn_in['wq_scales'], 'L0_attn_bq': _L0_attn_in['bq'], 'L0_attn_wk_codes': _L0_attn_in['wk_codes'], 'L0_attn_wk_scales': _L0_attn_in['wk_scales'], 'L0_attn_bk': _L0_attn_in['bk'], 'L0_attn_wv_codes': _L0_attn_in['wv_codes'], 'L0_attn_wv_scales': _L0_attn_in['wv_scales'], 'L0_attn_bv': _L0_attn_in['bv'], 'L0_attn_wo_codes': _L0_attn_in['wo_codes'], 'L0_attn_wo_scales': _L0_attn_in['wo_scales'], 'L0_attn_bo': _L0_attn_in['bo'], 'L0_ffn_gate_w': _L0_ffn_in['gate_w'], 'L0_ffn_W': _L0_ffn_in['W'], 'L0_ffn_atoms': _L0_ffn_in['atoms'], 'L0_ffn_expert_atom_weights': _L0_ffn_in['expert_atom_weights'], 'L0_ffn_importance': _L0_ffn_in['importance'], 'L0_ffn_mask_idx': _L0_ffn_in['mask_idx']}

def reference(x, fside_BxS2xS2_0, ctx_1024, L0_attn_wq_codes, L0_attn_wq_scales, L0_attn_bq, L0_attn_wk_codes, L0_attn_wk_scales, L0_attn_bk, L0_attn_wv_codes, L0_attn_wv_scales, L0_attn_bv, L0_attn_wo_codes, L0_attn_wo_scales, L0_attn_bo, L0_ffn_gate_w, L0_ffn_W, L0_ffn_atoms, L0_ffn_expert_atom_weights, L0_ffn_importance, L0_ffn_mask_idx):
    import jax
    import jax.numpy as jnp

    def _L0_attn_ref(x, wq_codes, wq_scales, bq, wk_codes, wk_scales, bk, wv_codes, wv_scales, bv, wo_codes, wo_scales, bo):
        import jax, jax.numpy as jnp
        import numpy as np
        BLOCK = 32
        NUM_HEADS = 16
        HEAD_DIM = 128
        FP4_GRID = jnp.array([0.0, 0.5, 1.0, 1.5, 2.0, 3.0, 4.0, 6.0], dtype=jnp.float32)

        def quantize_to_mxfp4(w, block_size=BLOCK):
            D, F = w.shape
            blocks = w.reshape(D // block_size, block_size, F)
            amax = jnp.max(jnp.abs(blocks), axis=1)
            e = jnp.floor(jnp.log2(jnp.maximum(amax, 1e-12) / 6.0))
            scale = jnp.exp2(e)
            v = blocks / scale[:, None, :]
            idx = jnp.argmin(jnp.abs(jnp.abs(v)[..., None] - FP4_GRID), axis=-1)
            codes = jnp.sign(v) * FP4_GRID[idx]
            return (codes.reshape(D, F).astype(jnp.float32), scale.astype(jnp.float32))

        def _mxfp4_matmul(x, codes, scales, block_size=BLOCK):
            w = codes * jnp.repeat(scales, block_size, axis=0)
            return x @ w
        B, S, D = x.shape
        q = _mxfp4_matmul(x, wq_codes, wq_scales) + bq
        k = _mxfp4_matmul(x, wk_codes, wk_scales) + bk
        v = _mxfp4_matmul(x, wv_codes, wv_scales) + bv
        q = q.reshape(B, S, NUM_HEADS, HEAD_DIM)
        k = k.reshape(B, S, NUM_HEADS, HEAD_DIM)
        v = v.reshape(B, S, NUM_HEADS, HEAD_DIM)
        scores = jnp.einsum('bqhd,bkhd->bhqk', q, k) / jnp.sqrt(jnp.float32(HEAD_DIM))
        attn = jax.nn.softmax(scores, axis=-1)
        out = jnp.einsum('bhqk,bkhd->bqhd', attn, v).reshape(B, S, NUM_HEADS * HEAD_DIM)
        return _mxfp4_matmul(out, wo_codes, wo_scales) + bo

    def _L0_xattn_ref(x, gate_up_weight, down_weight):
        import jax, jax.numpy as jnp
        import numpy as np
        EPS = 1e-06
        QMAX = 127.0

        def _smooth_quant_linear(x, w):
            amax_x = jnp.max(jnp.abs(x), axis=0)
            amax_w = jnp.max(jnp.abs(w), axis=0)
            s = jnp.sqrt(jnp.maximum(amax_x, EPS) / jnp.maximum(amax_w, EPS))
            s = jnp.maximum(s, EPS)
            xs = x / s
            ws = w * s
            x_scale = jnp.maximum(jnp.max(jnp.abs(xs), axis=-1, keepdims=True), EPS) / QMAX
            w_scale = jnp.maximum(jnp.max(jnp.abs(ws), axis=-1, keepdims=True), EPS) / QMAX
            x_q = jnp.clip(jnp.round(xs / x_scale), -QMAX, QMAX)
            w_q = jnp.clip(jnp.round(ws / w_scale), -QMAX, QMAX)
            return x_q @ w_q.T * x_scale * w_scale.T

        def _expert_forward(xe, guw, dw):
            h = _smooth_quant_linear(xe, guw)
            gate, up = jnp.split(h, 2, axis=-1)
            a = jax.nn.silu(gate) * up
            return _smooth_quant_linear(a, dw)
        return jax.vmap(_expert_forward)(x, gate_up_weight, down_weight)

    def _L0_ffn_ref(x, gate_w, W, atoms, expert_atom_weights, importance, mask_idx):
        import jax, jax.numpy as jnp
        import numpy as np
        TOP_K = 2
        B, S, H = x.shape
        xt = x.reshape(-1, H)
        logits = jnp.clip(xt @ gate_w.T, -50.0, 50.0)
        top_w, top_idx = jax.lax.top_k(logits, TOP_K)
        rw = jax.nn.softmax(top_w, axis=-1)
        deltas = jax.nn.softmax(expert_atom_weights, axis=-1) @ atoms
        weighted = deltas * jax.nn.sigmoid(importance)
        rows = mask_idx // H
        cols = mask_idx % H
        vals = jnp.einsum('tk,tks->ts', rw, weighted[top_idx])
        xg = xt[:, cols]
        contrib = jax.ops.segment_sum((xg * vals).T, rows, num_segments=H)
        out = xt @ W.T + contrib.T
        return out.reshape(B, S, H)
    x = _layernorm(x + _L0_attn_ref(x, L0_attn_wq_codes, L0_attn_wq_scales, L0_attn_bq, L0_attn_wk_codes, L0_attn_wk_scales, L0_attn_bk, L0_attn_wv_codes, L0_attn_wv_scales, L0_attn_bv, L0_attn_wo_codes, L0_attn_wo_scales, L0_attn_bo), axis=-1)
    x = _layernorm(x + _L0_xattn_ref(x, fside_BxS2xS2_0, ctx_1024), axis=-1)
    x = _layernorm(x + _L0_ffn_ref(x, L0_ffn_gate_w, L0_ffn_W, L0_ffn_atoms, L0_ffn_expert_atom_weights, L0_ffn_importance, L0_ffn_mask_idx), axis=-1)
    return x

_drawn_inputs = setup_inputs


def setup_inputs(seed=0):
    import zlib

    import numpy as np

    out = dict(_drawn_inputs(seed))
    spreads = {'L0_attn_bq': (0.0, 0.8),
     'L0_attn_bk': (0.0, 2.0),
     'L0_attn_bv': (0.0, 0.1),
     'L0_attn_bo': (0.0, 0.1)}
    factors = {'fside_BxS2xS2_0': 5.531,
     'ctx_1024': 5.352,
     'L0_attn_wq_scales': 3.311,
     'L0_attn_wk_scales': 3.317,
     'L0_attn_wv_scales': 2.973,
     'L0_ffn_gate_w': 22.375,
     'L0_ffn_atoms': 8.0,
     'L0_ffn_expert_atom_weights': 8.0,
     'L0_ffn_importance': 44.034}
    for name, (base, spread) in spreads.items():
        noise = np.random.default_rng([zlib.crc32(name.encode()), seed]).standard_normal(out[name].shape)
        drawn = base * np.exp(spread * noise) if base else spread * noise
        out[name] = jnp.asarray(drawn.astype(out[name].dtype))
    for name, factor in factors.items():
        out[name] = (out[name] * factor).astype(out[name].dtype)
    return out
```

```python
from contextlib import ExitStack

import concourse.bass as bass
from concourse import mybir

F32 = mybir.dt.float32
F32R = mybir.dt.float32r
ALU = mybir.AluOpType
ACT = mybir.ActivationFunctionType
AX = mybir.AxisListType
P = 128

B, S, D = 4, 256, 256
HEADS, HD, BLK = 16, 128, 32
T = B * S
TILES = T // P
KT = D // P
PAIRS = HEADS // 2
STEPS = 2 * B
SCALE = float(HD) ** -0.5
I32, U32, BF16 = mybir.dt.int32, mybir.dt.uint32, mybir.dt.bfloat16
EXPERTS, ATOMS, NS = 8, 64, 2048
NS_TILES = NS // P
TABLE_ROWS = D * D + P
SETUP_DONE = 3

QK_SLOT = [0, 2, 3, 4, 5, 6, 8, 10]
V_SLOT = {0: 1, 5: 7, 6: 9, 7: 11}
UNITS = 12


def qk_seq(i, c):
    return (i + (c - 5) // 8) * UNITS + 8 + QK_SLOT[(c - 5) % 8]


def v_seq(i, b):
    return i * UNITS + 8 + V_SLOT[0] if b == 3 else (i - 1) * UNITS + 8 + V_SLOT[5 + b]


def positive(eng, sem, value):
    if not isinstance(value, int) or value > 0:
        eng.wait_ge(sem, value)


def hold(eng, sem, value, passed):
    eng.wait_ge(sem, value)
    if not isinstance(value, int):
        eng.sem_inc(passed, 1)


def attention(nc, x, w, bias_rows, moe, kept):
    with ExitStack() as ctx:
        def sb(name, shape, dt=F32):
            return ctx.enter_context(nc.sbuf_tensor(name, shape, dt))

        def ps(name, shape, dt=F32):
            return ctx.enter_context(nc.psum_tensor(name, shape, dt))

        def sem(name):
            return ctx.enter_context(nc.semaphore(name))

        ident, ot, wo_hi, wo_lo = kept
        xt_hi = sb("xt_hi", [P, KT, T], F32R)
        xt_lo = sb("xt_lo", [P, KT, T], F32R)
        bias = sb("bias", [P, 3 * HEADS])
        code = [sb(f"code{g}", [P, 512]) for g in range(4)]
        scal = [sb(f"scal{g}", [P, 512]) for g in range(4)]
        wqk_hi = [sb(f"wqk_hi{p}", [P, 2, KT, P], F32R) for p in range(2)]
        wqk_lo = [sb(f"wqk_lo{p}", [P, 2, KT, P], F32R) for p in range(2)]
        wv_hi = sb("wv_hi", [P, KT, 256], F32R)
        wv_lo = sb("wv_lo", [P, KT, 256], F32R)
        qk_hi = [sb(f"qk_hi{p}", [P, 2, T], F32R) for p in range(2)]
        qk_lo = [sb(f"qk_lo{p}", [P, 2, T], F32R) for p in range(2)]
        v_hi = sb("v_hi", [P, TILES, 256], F32R)
        v_lo = sb("v_lo", [P, TILES, 256], F32R)
        prob = [sb(f"prob{p}", [P, 2, S]) for p in range(2)]
        pt_hi = [sb(f"pt_hi{p}", [P, 2, S], F32R) for p in range(2)]
        pt_lo = [sb(f"pt_lo{p}", [P, 2, S], F32R) for p in range(2)]
        xrow = ot[:, 0:TILES * D].rearrange("p (t d) -> p t d", t=TILES)
        brow = ot[0:3 * HEADS, TILES * D:TILES * D + P]
        idx, importance, atoms, expert_atoms, table = moe
        at = TILES * D + P
        def region(cols, dt=F32):
            nonlocal at
            at += cols
            return ot[:, at - cols:at] if dt is F32 else ot[:, at - cols:at].bitcast(dt)
        zeros = region(TABLE_ROWS * EXPERTS // P)
        idx_row = region(NS, I32)
        same = region(NS).rearrange("p (t s) -> p t s", t=NS_TILES)
        earlier = region(NS).rearrange("p (t s) -> p t s", t=NS_TILES)
        atoms_imp = region(NS)
        atoms_sb, imp_sb = atoms_imp[0:ATOMS, :], atoms_imp[96:96 + EXPERTS, :]
        before = region(P)
        idx_16 = region(P, I32)[0:NS_TILES, :]
        idx_16f = region(P)[0:NS_TILES, :]
        mix = region(ATOMS)[0:EXPERTS, :]
        mix_t = region(EXPERTS)[0:ATOMS, :]
        mix_s = region(4)[0:EXPERTS, :]
        idx_f = region(NS_TILES)
        idx_i = region(NS_TILES, I32)
        col_i = region(NS_TILES, I32)
        row_i = region(NS_TILES, I32)
        dup = region(NS_TILES)
        place_f = region(NS_TILES)
        spare_i = region(1, I32)
        gates = region(NS_TILES * EXPERTS)
        scaled = region(NS_TILES * EXPERTS)
        assert at <= HEADS * T
        summed = sb("summed", [P, NS_TILES * EXPERTS])
        place = sb("place", [P, NS_TILES], U32)
        tile_rows = sb("tile_rows", [P, EXPERTS])
        tile_place = sb("tile_place", [P, 1], U32)
        negmax = [sb(f"negmax{p}", [P, 2]) for p in range(2)]
        rowsum = [sb(f"rowsum{p}", [P, 2]) for p in range(2)]
        rowmax = [sb(f"rowmax{p}", [P, 2]) for p in range(2)]
        rinv = [sb(f"rinv{p}", [P, 2]) for p in range(2)]

        proj = [ps(f"proj{p}", [P, 512]) for p in range(2)]
        score = [ps(f"score{p}", [P, 2, S]) for p in range(2)]
        ptp = [ps(f"ptp{p}", [P, 2, S]) for p in range(2)]
        op = [ps(f"op{p}", [P, 512]) for p in range(2)]

        x_loaded, b_loaded = sem("x_loaded"), sem("b_loaded")
        ident_ready = sem("ident_ready")
        xt_ready, xt_copied, xt_split = sem("xt_ready"), sem("xt_copied"), sem("xt_split")
        bias_turned, bias_ready = sem("bias_turned"), sem("bias_ready")
        w_loaded = [sem(f"w_loaded{g}") for g in range(4)]
        w_made = [sem(f"w_made{g}") for g in range(4)]
        w_split = [sem(f"w_split{g}") for g in range(4)]
        proj_ready, proj_hi, proj_lo = sem("proj_ready"), sem("proj_hi"), sem("proj_lo")
        score_ready, negmax_ready, exp_done = sem("score_ready"), sem("negmax_ready"), sem("exp_done")
        rinv_ready, prob_ready = sem("rinv_ready"), sem("prob_ready")
        pt_ready, pt_hi_ready, pt_lo_ready = sem("pt_ready"), sem("pt_hi_ready"), sem("pt_lo_ready")
        o_ready, o_stored = sem("o_ready"), sem("o_stored")
        setup_loaded, zeros_ready, table_zeroed = sem("setup_loaded"), sem("zeros_ready"), sem("table_zeroed")
        masks_ready, idx_float, mix_ready = sem("masks_ready"), sem("idx_float"), sem("mix_ready")
        setup_pe, setup_dve, setup_act = sem("setup_pe"), sem("setup_dve"), sem("setup_act")
        pool_passed, act_passed = sem("pool_passed"), sem("act_passed")
        tile_staged, scattered = sem("tile_staged"), sem("scattered")

        def passes(eng, body, first_t=3):
            for t in range(first_t, STEPS):
                body(-1, t)
            for t in range(STEPS):
                body(0, t)
            with eng.Fori(1, PAIRS - 1) as i:
                for t in range(STEPS):
                    body(i, t)
            for t in range(STEPS):
                body(PAIRS - 1, t)

        def within(i, t, ahead, count=STEPS * PAIRS):
            return not isinstance(i, int) or 0 <= STEPS * i + t + ahead < count

        block = ctx.enter_context(nc.Block())

        @block.sync
        def _(sp):
            sp.dma_start(xrow, x.rearrange("b (s p) d -> p (b s) d", p=P)).then_inc(x_loaded, 16)
            for k in range(3):
                sp.dma_start(brow[k * HEADS:(k + 1) * HEADS, :],
                             bias_rows[k].rearrange("(h f) -> h f", f=HD)).then_inc(b_loaded, 16)

            def load(p):
                for g in range(4):
                    if not isinstance(p, int) or p > 0:
                        sp.wait_ge(w_split[g], 2 * p)
                    if g == 3:
                        codes, scales = w[6], w[7]
                        src = codes[bass.ds(p * 256, 256), :].rearrange("(k p) f -> p k f", p=P)
                        sp.dma_start(code[g][:, :].rearrange("p (k f) -> p k f", k=2), src).then_inc(w_loaded[g], 16)
                        rows = scales[bass.ds(p * 8, 8), :].rearrange("(k b) f -> b k f", k=2)
                        for b in range(4):
                            sp.dma_start(scal[g][b * BLK:(b + 1) * BLK, :].rearrange("p (k f) -> p k f", k=2),
                                         rows[b:b + 1].broadcast_to([BLK, 2, 256])).then_inc(w_loaded[g], 16)
                        continue
                    width = 256 if g == 1 else P
                    col = p * 256 + (P if g == 2 else 0)
                    for m in range(1 if g == 1 else 2):
                        codes, scales = (w[4], w[5]) if g == 1 else (w[2 * m], w[2 * m + 1])
                        span = slice(m * 256, m * 256 + KT * width)
                        src = codes.rearrange("(k p) f -> p k f", p=P)[:, :, bass.ds(col, width)]
                        sp.dma_start(code[g][:, span].rearrange("p (k f) -> p k f", k=KT), src)\
                          .then_inc(w_loaded[g], 16)
                        rows = scales.rearrange("(k b) f -> b k f", k=KT)[:, :, bass.ds(col, width)]
                        for b in range(4):
                            sp.dma_start(scal[g][b * BLK:(b + 1) * BLK, span].rearrange("p (k f) -> p k f", k=KT),
                                         rows[b:b + 1].broadcast_to([BLK, KT, width])).then_inc(w_loaded[g], 16)

            load(0)
            for dst, src in ((idx_row, idx.rearrange("(a n) -> a n", a=1).broadcast_to([P, NS])),
                             (idx_16, idx.rearrange("(t s) -> t s", s=P)),
                             (atoms_sb, atoms), (imp_sb, importance), (mix, expert_atoms)):
                sp.dma_start(dst, src).then_inc(setup_loaded, 16)
            sp.wait_ge(zeros_ready, 1)
            sp.dma_start(table.rearrange("(p a) e -> p (a e)", p=P), zeros).then_inc(table_zeroed, 16)
            with sp.Fori(1, PAIRS) as p:
                load(p)
            sp.wait_ge(o_stored, PAIRS * STEPS)

        @block.gpsimd
        def _(pool):
            pool.memset(ident[:, :], 0.0).then_inc(ident_ready, 1)
            pool.wait_ge(ident_ready, 1)
            pool.affine_select(out=ident[:, :], in_=ident[:, :], compare_op=ALU.not_equal, fill=1.0,
                               base=0, pattern=[[-1, P]], channel_multiplier=1).then_inc(ident_ready, 1)

            pool.memset(before, 1.0).then_inc(masks_ready, 1)
            pool.iota(spare_i, pattern=[[0, 1]], base=D * D, channel_multiplier=1).then_inc(masks_ready, 1)
            pool.wait_ge(masks_ready, 2)
            pool.affine_select(out=before, in_=before, compare_op=ALU.is_gt, fill=0.0, base=0,
                               pattern=[[-1, P]], channel_multiplier=1).then_inc(masks_ready, 1)

            def scatter(i, half):
                n = 2 * i + half
                if isinstance(i, int) and n == 0:
                    pool.wait_ge(table_zeroed, 16)
                    pool.wait_ge(setup_dve, SETUP_DONE)
                else:
                    hold(pool, scattered, 16 * n, pool_passed)
                pool.tensor_copy(tile_rows[:, :], summed[:, bass.ds(n * EXPERTS, EXPERTS)]).then_inc(tile_staged, 1)
                pool.tensor_copy(tile_place[:, :], place[:, bass.ds(n, 1)]).then_inc(tile_staged, 1)
                hold(pool, tile_staged, 2 * (n + 1), pool_passed)
                pool.indirect_dma_start(
                    out=table, out_offset=bass.IndirectOffsetOnAxis(ap=tile_place[:, 0:1], axis=0),
                    in_=tile_rows[:, :], in_offset=None, compute_op=ALU.add).then_inc(scattered, 16)

            def make(g, i):
                hi, lo = [(wqk_hi[0], wqk_lo[0]), (wv_hi, wv_lo), (wqk_hi[1], wqk_lo[1]), (None, None)][g]
                if g == 3:
                    hi = wo_hi[:, bass.ds(2 * (i + 1), 2), :].rearrange("p a b -> p (a b)")
                    lo = wo_lo[:, bass.ds(2 * (i + 1), 2), :].rearrange("p a b -> p (a b)")
                elif g == 1:
                    hi, lo = (z[:, :, :].rearrange("p a b -> p (a b)") for z in (hi, lo))
                else:
                    hi, lo = (z[:, :, :, :].rearrange("p a b c -> p (a b c)") for z in (hi, lo))
                loads = [10, 5, 10, 5][g]
                pool.wait_ge(w_loaded[g], 16 * loads * (i + 2))
                pool.tensor_tensor(code[g][:, :], code[g][:, :], scal[g][:, :], ALU.mult).then_inc(w_made[g], 1)
                if g == 0:
                    positive(pool, proj_ready, qk_seq(i, 3) + 1)
                if g == 1:
                    positive(pool, proj_ready, v_seq(i, 3) + 1)
                if g == 2:
                    positive(pool, proj_ready, qk_seq(i, 7) + 1)
                hold(pool, w_made[g], i + 2, pool_passed)
                pool.tensor_copy(hi, code[g][:, :]).then_inc(w_split[g], 1)
                pool.wait_ge(w_split[g], 2 * (i + 1) + 1)
                pool.tensor_tensor(lo, code[g][:, :], hi.bitcast(F32), ALU.subtract).then_inc(w_split[g], 1)

            def step(i, t):
                n = STEPS * i + t
                last = isinstance(i, int) and i == PAIRS - 1
                if i == -1 if isinstance(i, int) else False:
                    if t == 3:
                        for g in range(4):
                            make(g, i)
                elif not last and t % 2 == 0:
                    make(t // 2, i)
                if t in (3, 7) and not (isinstance(i, int) and i < 0):
                    scatter(i, t // 4)
                if within(i, t, 1):
                    hold(pool, rinv_ready, n + 2, pool_passed)
                    k = (t + 1) % 2
                    for q in range(2):
                        pool.tensor_scalar(prob[k][:, q, :], prob[k][:, q, :], rinv[k][:, q:q + 1], 1.0,
                                           ALU.mult, ALU.mult).then_inc(prob_ready, 1)

            passes(pool, step)
            pool.wait_ge(scattered, 16 * NS_TILES)

        @block.tensor
        def _(pe):
            pe.wait_ge(ident_ready, 2)
            pe.wait_ge(x_loaded, 16)
            for u in range(4):
                k, half = u % 2, u // 2
                if u >= 2:
                    pe.wait_ge(xt_split, u - 1)
                for j in range(4):
                    last = pe.transpose(proj[u % 2][:, j * P:(j + 1) * P],
                                        xrow[:, half * 4 + j, k * P:(k + 1) * P], ident[:, :])
                last.then_inc(xt_ready, 1)
            pe.wait_ge(b_loaded, 48)
            pe.transpose(op[0][:, 0:3 * HEADS], brow, ident[0:3 * HEADS, 0:3 * HEADS]).then_inc(bias_turned, 1)
            pe.wait_ge(xt_split, 4)
            pe.wait_ge(bias_ready, 1)

            pe.wait_ge(idx_float, 1)
            pe.transpose(op[1][:, 0:NS_TILES], idx_16f, ident[0:NS_TILES, 0:NS_TILES]).then_inc(setup_pe, 1)
            pe.wait_ge(setup_loaded, 80)
            for t in range(NS_TILES):
                last = pe.transpose(score[0][:, t // 8, (t % 8) * EXPERTS:(t % 8 + 1) * EXPERTS],
                                    imp_sb[:, t * P:(t + 1) * P], ident[96:96 + EXPERTS, 96:96 + EXPERTS])
            last.then_inc(setup_pe, 1)
            pe.wait_ge(mix_ready, 1)
            pe.transpose(score[1][0:ATOMS, 0, 0:EXPERTS], mix, ident[0:EXPERTS, 0:EXPERTS]).then_inc(setup_pe, 1)
            pe.wait_ge(setup_dve, 1)
            for t in range(NS_TILES):
                last = pe.matmul(ptp[0][:, t // 8, (t % 8) * EXPERTS:(t % 8 + 1) * EXPERTS],
                                 atoms_sb[:, t * P:(t + 1) * P], mix_t, start=True, stop=True)
            last.then_inc(setup_pe, 1)
            pe.wait_ge(setup_dve, 2)
            for t in range(NS_TILES):
                last = pe.matmul(ptp[1][:, t // 8, (t % 8) * EXPERTS:(t % 8 + 1) * EXPERTS],
                                 same[:, t, :], scaled[:, t * EXPERTS:(t + 1) * EXPERTS], start=True, stop=True)
            last.then_inc(setup_pe, 1)
            pe.wait_ge(setup_dve, SETUP_DONE)

            def three(out, lh, ll, rh, rl, k, n):
                pe.matmul(out, lh, rh, start=(k == 0), stop=False)
                pe.matmul(out, lh, rl, start=False, stop=False)
                return pe.matmul(out, ll, rh, start=False, stop=(k == n - 1))

            def step(i, t):
                n = STEPS * i + t
                if within(i, t, 2):
                    m = n + 2
                    c = t + 2
                    par, b = (c // 4) % 2, c % 4
                    pe.wait_ge(proj_lo, qk_seq(i, 4 * (c // 4) + 2 * (b // 2) + 1) + 1)
                    positive(pe, exp_done, m - 1)
                    lo, hi = qk_lo[par], qk_hi[par]
                    keys = slice(b * S, (b + 1) * S)
                    for q in range(2):
                        rows = slice(b * S + q * P, b * S + (q + 1) * P)
                        last = three(score[c % 2][:, q, :], hi[:, 0, rows], lo[:, 0, rows],
                                     hi[:, 1, keys], lo[:, 1, keys], 0, 1)
                    last.then_inc(score_ready, 1)
                if within(i, t, 5):
                    c = t + 5
                    par, part = (c // 4) % 2, c % 4
                    pair = i + c // 8
                    seq = qk_seq(i, c)
                    bank = proj[QK_SLOT[t] % 2]
                    pe.wait_ge(w_split[2 * par], 2 * (pair + 1))
                    positive(pe, proj_lo, seq - 1)
                    m, half = part % 2, part // 2
                    cols = slice(half * 512, (half + 1) * 512)
                    for k in range(KT):
                        last = three(bank[:, :], wqk_hi[par][:, m, k, :], wqk_lo[par][:, m, k, :],
                                     xt_hi[:, k, cols], xt_lo[:, k, cols], k, KT)
                    last.then_inc(proj_ready, 1)
                if within(i, t, 0):
                    pe.wait_ge(prob_ready, 2 * (n + 1))
                    positive(pe, pt_lo_ready, n - 1)
                    for k in range(2):
                        for q in range(2):
                            last = pe.transpose(ptp[t % 2][:, k, q * P:(q + 1) * P],
                                                prob[t % 2][:, q, k * P:(k + 1) * P], ident[:, :])
                    last.then_inc(pt_ready, 1)
                if within(i, t, -1):
                    m, c = n - 1, (t - 1) % 8
                    weigh(i, t, m, c)
                if t in V_SLOT and not (isinstance(i, int) and (i == PAIRS - 1 and t > 0 or i == -1 and t == 0)):
                    b = 3 if t == 0 else t - 5
                    pair = i if t == 0 else i + 1
                    seq = v_seq(pair, b)
                    bank = proj[V_SLOT[t] % 2]
                    pe.wait_ge(w_split[1], 2 * (pair + 1))
                    positive(pe, proj_lo, seq - 1)
                    for j in range(2):
                        rows = slice(b * S + j * P, b * S + (j + 1) * P)
                        for k in range(KT):
                            last = three(bank[:, j * 256:(j + 1) * 256], xt_hi[:, k, rows], xt_lo[:, k, rows],
                                         wv_hi[:, k, :], wv_lo[:, k, :], k, KT)
                    last.then_inc(proj_ready, 1)

            def weigh(i, t, m, c):
                par, b = c // 4, c % 4
                pair = i - 1 if t == 0 else i
                pe.wait_ge(pt_lo_ready, m + 1)
                pe.wait_ge(proj_lo, v_seq(pair, b) + 1)
                positive(pe, o_stored, m - 1)
                for k in range(2):
                    cols = slice(par * P, (par + 1) * P)
                    last = three(op[c % 2][:, 0:S], v_hi[:, 2 * b + k, cols], v_lo[:, 2 * b + k, cols],
                                 pt_hi[c % 2][:, k, :], pt_lo[c % 2][:, k, :], k, 2)
                last.then_inc(o_ready, 1)

            passes(pe, step)
            weigh(PAIRS, 0, STEPS * PAIRS - 1, 7)

        @block.scalar
        def _(act):
            for u in range(4):
                k, half = u % 2, u // 2
                act.wait_ge(xt_ready, u + 1)
                act.copy(xt_hi[:, k, half * 512:(half + 1) * 512], proj[u % 2][:, :]).then_inc(xt_copied, 1)
            act.wait_ge(bias_turned, 1)
            act.copy(bias[:, :], op[0][:, 0:3 * HEADS]).then_inc(bias_ready, 1)
            act.wait_ge(bias_ready, 1)
            act.wait_ge(setup_act, 1)
            act.activation(mix, mix, ACT.Exp, bias=mix_s[:, 0:1], accum_out=mix_s[:, 1:2]).then_inc(setup_act, 1)
            act.wait_ge(setup_pe, 2)
            act.activation(gates.rearrange("p (a b) -> p a b", a=2), score[0][:, :, 0:8 * EXPERTS], ACT.Exp,
                           scale=-1.0).then_inc(setup_act, 1)

            def step(i, t):
                n = STEPS * i + t
                if within(i, t, 5):
                    c = t + 5
                    par, part = (c // 4) % 2, c % 4
                    m, half = part % 2, part // 2
                    head = 2 * (i + c // 8) + par
                    seq = qk_seq(i, c)
                    hold(act, proj_ready, seq + 1, act_passed)
                    act.activation(qk_hi[par][:, m, half * 512:(half + 1) * 512], proj[QK_SLOT[t] % 2][:, :],
                                   ACT.Identity, bias=bias[:, bass.ds(m * HEADS + head, 1)]).then_inc(proj_hi, 1)
                if within(i, t, 0):
                    act.wait_ge(pt_ready, n + 1)
                    positive(act, o_ready, n - 1)
                    act.copy(pt_hi[t % 2][:, :, :], ptp[t % 2][:, :, :]).then_inc(pt_hi_ready, 1)
                if t in V_SLOT and not (isinstance(i, int) and (i == PAIRS - 1 and t > 0 or i == -1 and t == 0)):
                    b = 3 if t == 0 else t - 5
                    pair = i if t == 0 else i + 1
                    act.wait_ge(proj_ready, v_seq(pair, b) + 1)
                    act.copy(v_hi[:, 2 * b:2 * b + 2, :],
                             proj[V_SLOT[t] % 2][:, :].rearrange("p (j f) -> p j f", j=2)).then_inc(proj_hi, 1)
                if within(i, t, 2):
                    k = t % 2
                    act.wait_ge(negmax_ready, n + 3)
                    positive(act, pt_ready, n + 1)
                    for q in range(2):
                        last = act.activation(prob[k][:, q, :], score[k][:, q, :], ACT.Exp,
                                              bias=negmax[k][:, q:q + 1], scale=SCALE,
                                              accum_out=rowsum[k][:, q:q + 1])
                    last.then_inc(exp_done, 1)

            passes(act, step)

        @block.vector
        def _(dve):
            for u in range(4):
                k, half = u % 2, u // 2
                dve.wait_ge(xt_copied, u + 1)
                cols = slice(half * 512, (half + 1) * 512)
                dve.tensor_tensor(xt_lo[:, k, cols], proj[u % 2][:, :], xt_hi[:, k, cols].bitcast(F32),
                                  ALU.subtract).then_inc(xt_split, 1)
            dve.wait_ge(bias_ready, 1)
            small = sem("small")
            setup_small = sem("setup_small")
            count = [0]

            def then(ins):
                count[0] += 1
                ins.then_inc(setup_small, 1)
                dve.wait_ge(setup_small, count[0])

            dve.wait_ge(setup_loaded, 80)
            dve.tensor_copy(idx_16f, idx_16).then_inc(idx_float, 1)
            dve.memset(zeros, 0.0).then_inc(zeros_ready, 1)
            dve.tensor_reduce(mix_s[:, 0:1], mix, AX.X, ALU.max, negate=True).then_inc(setup_act, 1)
            dve.wait_ge(setup_pe, 1)
            then(dve.tensor_copy(idx_f, op[1][:, 0:NS_TILES]))
            then(dve.tensor_copy(idx_i, idx_f))
            dve.tensor_scalar(row_i, idx_i, 8, None, ALU.logical_shift_right)
            then(dve.tensor_scalar(col_i, idx_i, D - 1, 8, ALU.bitwise_and, ALU.logical_shift_left))
            then(dve.tensor_tensor(place_f, col_i, row_i, ALU.add))
            then(dve.tensor_tensor(same, idx_row.rearrange("p (t s) -> p t s", t=NS_TILES),
                                   idx_f.unsqueeze(2).broadcast_to([P, NS_TILES, P]), ALU.is_equal))
            dve.wait_ge(masks_ready, 3)
            then(dve.tensor_tensor(earlier, same, before.unsqueeze(1).broadcast_to([P, NS_TILES, P]), ALU.mult))
            then(dve.tensor_reduce(dup, earlier, AX.X, ALU.max))
            then(dve.tensor_copy(idx_f, spare_i.broadcast_to([P, NS_TILES])))
            then(dve.tensor_tensor(idx_f, idx_f, place_f, ALU.subtract))
            then(dve.tensor_tensor(idx_f, idx_f, dup, ALU.mult))
            then(dve.tensor_tensor(place[:, :], place_f, idx_f, ALU.add))
            dve.wait_ge(setup_act, 2)
            then(dve.reciprocal(mix_s[:, 2:3], mix_s[:, 1:2]))
            dve.tensor_scalar(mix, mix, mix_s[:, 2:3], None, ALU.mult).then_inc(mix_ready, 1)
            dve.wait_ge(setup_pe, 3)
            dve.tensor_copy(mix_t, score[1][0:ATOMS, 0, 0:EXPERTS]).then_inc(setup_dve, 1)
            dve.wait_ge(setup_act, 3)
            then(dve.tensor_scalar(gates, gates, 1.0, None, ALU.add))
            then(dve.reciprocal(gates, gates))
            dve.wait_ge(setup_pe, 4)
            dve.tensor_tensor(scaled.rearrange("p (a b) -> p a b", a=2), ptp[0][:, :, 0:8 * EXPERTS],
                              gates.rearrange("p (a b) -> p a b", a=2), ALU.mult).then_inc(setup_dve, 1)
            dve.wait_ge(setup_pe, 5)
            dve.tensor_copy(summed[:, :].rearrange("p (a b) -> p a b", a=2),
                            ptp[1][:, :, 0:8 * EXPERTS]).then_inc(setup_dve, 1)
            dve.wait_ge(table_zeroed, 16)

            def store_o(i, t, m, c):
                par, b = c // 4, c % 4
                head = 2 * (i - 1 if t == 0 else i) + par
                dve.wait_ge(o_ready, m + 1)
                dve.tensor_scalar(ot[:, bass.ds(head * T + b * S, S)], op[c % 2][:, 0:S],
                                  bias[:, bass.ds(2 * HEADS + head, 1)], None, ALU.add).then_inc(o_stored, 1)

            def step(i, t):
                n = STEPS * i + t
                if within(i, t, 2):
                    k = t % 2
                    dve.wait_ge(score_ready, n + 3)
                    dve.tensor_reduce(rowmax[k][:, :], score[k][:, :, :], AX.X, ALU.max).then_inc(small, 1)
                    dve.wait_ge(small, n + 3)
                    dve.tensor_scalar(negmax[k][:, :], rowmax[k][:, :], -SCALE, None, ALU.mult)\
                       .then_inc(negmax_ready, 1)
                if within(i, t, 5):
                    c = t + 5
                    par, part = (c // 4) % 2, c % 4
                    m, half = part % 2, part // 2
                    head = 2 * (i + c // 8) + par
                    cols = slice(half * 512, (half + 1) * 512)
                    dve.wait_ge(proj_hi, qk_seq(i, c) + 1)
                    dve.scalar_tensor_tensor(qk_lo[par][:, m, cols], proj[QK_SLOT[t] % 2][:, :],
                                             bias[:, bass.ds(m * HEADS + head, 1)],
                                             qk_hi[par][:, m, cols].bitcast(F32),
                                             ALU.add, ALU.subtract).then_inc(proj_lo, 1)
                if within(i, t, 1):
                    k = (t + 1) % 2
                    dve.wait_ge(exp_done, n + 2)
                    dve.reciprocal(rinv[k][:, :], rowsum[k][:, :]).then_inc(rinv_ready, 1)
                if within(i, t, 0):
                    dve.wait_ge(pt_hi_ready, n + 1)
                    dve.tensor_tensor(pt_lo[t % 2][:, :, :], ptp[t % 2][:, :, :],
                                      pt_hi[t % 2][:, :, :].bitcast(F32), ALU.subtract).then_inc(pt_lo_ready, 1)
                if within(i, t, -1):
                    store_o(i, t, n - 1, (t - 1) % 8)
                if t in V_SLOT and not (isinstance(i, int) and (i == PAIRS - 1 and t > 0 or i == -1 and t == 0)):
                    b = 3 if t == 0 else t - 5
                    pair = i if t == 0 else i + 1
                    dve.wait_ge(proj_hi, v_seq(pair, b) + 1)
                    dve.tensor_tensor(v_lo[:, 2 * b:2 * b + 2, :],
                                      proj[V_SLOT[t] % 2][:, :].rearrange("p (j f) -> p j f", j=2),
                                      v_hi[:, 2 * b:2 * b + 2, :].bitcast(F32), ALU.subtract)\
                       .then_inc(proj_lo, 1)

            passes(dve, step)
            store_o(PAIRS, 0, STEPS * PAIRS - 1, 7)


EPS_LN, EPS_Q, QMAX = 1e-5, 1e-6, 127.0
ROUND = 1.5 * 2.0 ** 23
INNER = 128
TB = S // P
HG, RING = 4, 4
UPB = TB * HEADS // HG
WIDE = EXPERTS * D
CLIP = 50.0


def layers(nc, x, bo, guw, dw, gate_w, w_ffn, table, out, kept):
    ident, ot, wo_hi, wo_lo = kept
    with ExitStack() as ctx:
        def sb(name, shape, dt=F32):
            return ctx.enter_context(nc.sbuf_tensor(name, shape, dt))

        def ps(name, shape, dt=F32):
            return ctx.enter_context(nc.psum_tensor(name, shape, dt))

        def sem(name):
            return ctx.enter_context(nc.semaphore(name))

        o_hi = [sb(f"o_hi{k}", [P, HG, P], F32R) for k in range(RING)]
        o_lo = [sb(f"o_lo{k}", [P, HG, P], F32R) for k in range(RING)]
        xb = [sb(f"xb{k}", [P, TB, D]) for k in range(2)]
        bo_row = sb("bo_row", [P, D])
        ones = sb("ones", [P, P])
        half = sb("half", [P, 4])
        iota8 = sb("iota8", [P, EXPERTS])
        gu_sb = [sb(f"gu_sb{k}", [P, TB, D]) for k in range(2)]
        dw_sb = [sb(f"dw_sb{k}", [P, TB, INNER]) for k in range(2)]
        wall_hi = sb("wall_hi", [P, KT, WIDE + D + EXPERTS], F32R)
        wall_lo = sb("wall_lo", [P, KT, WIDE + D + EXPERTS], F32R)
        amax_w = sb("amax_w", [P, KT + 1])
        y1 = sb("y1", [P, TB, D])
        x1 = sb("x1", [P, TB, D])
        x2 = [sb(f"x2_{k}", [P, TB, D]) for k in range(B)]
        raw = sb("raw", [P, WIDE])
        scaled, mixed, *result = (raw[:, k * TB * D:(k + 1) * TB * D].rearrange("p (j d) -> p j d", j=TB)
                                  for k in range(4))
        diag = sb("diag", [P, 4, P])
        xq_t = sb("xq_t", [P, KT, S], BF16)
        wq_t = sb("wq_t", [P, KT, S], BF16)
        row = sb("row", [P, D])
        hidden = sb("hidden", [P, TB, 2 * INNER])
        gate = sb("gate", [P, TB, INNER])
        act_sb = sb("act_sb", [P, TB, INNER])
        st = sb("st", [P, TB, 6])
        mv = sb("mv", [P, TB, 2])
        v1 = sb("v1", [P, 16])
        x2t_hi = sb("x2t_hi", [P, KT, S], F32R)
        x2t_lo = sb("x2t_lo", [P, KT, S], F32R)
        logit = sb("logit", [P, EXPERTS])
        top = sb("top", [P, EXPERTS])
        top_at = sb("top_at", [P, EXPERTS], U32)
        top_f = sb("top_f", [P, 2])
        share = sb("share", [P, 4])
        weight = sb("weight", [P, EXPERTS])
        second = sb("second", [P, EXPERTS])
        x_scale, w_scale = sb("x_scale", [P, TB]), sb("w_scale", [P, TB])
        inv = sb("inv", [P, TB])
        smooth = sb("smooth", [P, 4])
        w_rows, g_rows = hidden, row[0:EXPERTS, :]

        y_ps = [ps(f"y_ps{k}", [P, TB, D]) for k in range(2)]
        link_ps = [ps(f"link_ps{k}", [P, 512]) for k in range(2)]
        f_ps = [ps(f"f_ps{k}", [P, 512]) for k in range(4)]

        w_in, raw_in, bo_in = sem("w_in"), sem("raw_in"), sem("bo_in")
        x_in, q_in = [sem(f"x_in{k}") for k in range(2)], [sem(f"q_in{k}") for k in range(2)]
        consts = sem("consts")
        raw_used = sem("raw_used")
        q_used = sem("q_used")
        o_hi_ready, o_lo_ready = sem("o_hi_ready"), sem("o_lo_ready")
        xb_ready = sem("xb_ready")
        o_used = sem("o_used")
        y_used = sem("y_used")
        link_ready, link_used, link_in = sem("link_ready"), sem("link_used"), sem("link_in")
        row_ready = sem("row_ready")
        exp_in, exp_out = sem("exp_in"), sem("exp_out")
        pow_in, pow_out = sem("pow_in"), sem("pow_out")
        wall_hi_ready = sem("wall_hi_ready")
        x2t_hi_ready = sem("x2t_hi_ready")
        f_ready, f_used = sem("f_ready"), sem("f_used")
        result_ready, stored = sem("result_ready"), [sem(f"stored{k}") for k in range(2)]
        chain = sem("chain")

        LINKS = ["x1", "scale", "xq", "wq", "mm1", "row1", "act", "scale2", "q2", "mm2", "row2"]

        def links(b):
            return [f"{name}.{b}" for name in ["prep", "prepd"] + LINKS]

        order = ["wt0", "wt1"] + links(0) + links(1) + links(2) + ["x2.0"] + links(3) + ["x2.1", "x2.2", "x2.3"]
        nth = {name: k for k, name in enumerate(order)}
        fed = {f"{name}.{b}": b * (len(LINKS) + 1) + k + 1
               for b in range(B) for k, name in enumerate(LINKS + ["x2"])}
        heads_in = lambda heads: range(heads.start, heads.stop)

        def unit_of(u):
            b, j, q = u // UPB, u % UPB * TB // UPB, u % (UPB // TB)
            return slice(HG * q, HG * (q + 1)), slice(b * S + j * P, b * S + (j + 1) * P)

        FFN = [(b, j, c) for b in range(B) for j in range(TB) for c in range(5)]
        fth = {key: k for k, key in enumerate(FFN)}

        block = ctx.enter_context(nc.Block())

        @block.sync
        def _(sp):
            sp.dma_start(w_rows[:, :, :], w_ffn.rearrange("(j p) d -> p j d", p=P)).then_inc(w_in, 16)
            sp.dma_start(g_rows[:, :], gate_w).then_inc(w_in, 16)
            sp.dma_start(bo_row[:, :], bo.rearrange("(a n) -> a n", a=1).broadcast_to([P, D])).then_inc(bo_in, 16)
            rows = table[0:D * D, :].rearrange("(k p r) e -> k p (r e)", k=KT, p=P)

            def load_x(b):
                sp.dma_start(xb[b % 2][:, :, :], x[b].rearrange("(j p) d -> p j d", p=P)).then_inc(x_in[b % 2], 16)

            def load_q(b):
                sp.dma_start(gu_sb[b % 2][:, :, :], guw[b].rearrange("(j p) d -> p j d", p=P))\
                  .then_inc(q_in[b % 2], 16)
                sp.dma_start(dw_sb[b % 2][:, :, :], dw[b].rearrange("(j p) d -> p j d", p=P))\
                  .then_inc(q_in[b % 2], 16)

            load_x(0)
            load_q(0)
            sp.dma_start(raw[:, :], rows[0]).then_inc(raw_in, 16)
            load_x(1)
            load_q(1)
            sp.wait_ge(raw_used, 1)
            sp.dma_start(raw[:, :], rows[1]).then_inc(raw_in, 16)
            for b in range(2, B):
                sp.wait_ge(y_used, b - 1)
                load_x(b)
                sp.wait_ge(q_used, b - 1)
                load_q(b)
            for b in range(B):
                for j in range(TB):
                    sp.wait_ge(result_ready, TB * b + j + 1)
                    sp.dma_start(out[b, j * P:(j + 1) * P, :], result[b % 2][:, j, :]).then_inc(stored[b % 2], 16)
            for k in range(2):
                sp.wait_ge(stored[k], 16 * TB * B // 2)

        @block.gpsimd
        def _(pool):
            pool.memset(ones[:, :], 1.0).then_inc(consts, 1)
            pool.memset(half[:, 0:2], -0.5).then_inc(consts, 1)
            pool.memset(half[:, 2:4], 0.5).then_inc(consts, 1)
            pool.iota(iota8[:, :], pattern=[[1, EXPERTS]], base=0, channel_multiplier=0,
                      allow_small_or_imprecise_dtypes=True).then_inc(consts, 1)
            pool.wait_ge(consts, 4)

            ot_view = ot[:, :].rearrange("p (h t) -> p h t", h=HEADS)

            def low_parts(b):
                for u in range(UPB * b, UPB * (b + 1)):
                    heads, rows = unit_of(u)
                    pool.wait_ge(o_hi_ready, u + 1)
                    pool.tensor_tensor(o_lo[u % RING][:, :, :], ot_view[:, heads, rows],
                                       o_hi[u % RING][:, :, :].bitcast(F32), ALU.subtract).then_inc(o_lo_ready, 1)

            def add_bias(b):
                pool.wait_ge(x_in[b % 2], 16 * (b // 2 + 1))
                pool.tensor_tensor(xb[b % 2][:, :, :], xb[b % 2][:, :, :],
                                   bo_row[:, :].unsqueeze(1).broadcast_to([P, TB, D]), ALU.add).then_inc(xb_ready, 1)

            powers = [0]

            def power(width, positive_half=False):
                powers[0] += 1
                pool.wait_ge(pow_in, powers[0])
                e = half[:, 2:2 + width] if positive_half else half[:, 0:width]
                pool.tensor_tensor(v1[:, 8:8 + width], v1[:, 0:width], e, ALU.pow).then_inc(pow_out, 1)

            def chain_powers():
                power(2)
                power(2, True)
                power(1, True)
                power(2)

            pool.wait_ge(bo_in, 16)
            low_parts(0)
            add_bias(0)
            for b in range(1, B):
                low_parts(b)
                add_bias(b)
                chain_powers()
            for j in range(TB):
                power(1)
            chain_powers()
            for b in range(1, B):
                for j in range(TB):
                    power(1)

        @block.tensor
        def _(pe):
            def three(out, lh, ll, rh, rl, k, n):
                pe.matmul(out, lh, rh, start=(k == 0), stop=False)
                pe.matmul(out, lh, rl, start=False, stop=False)
                return pe.matmul(out, ll, rh, start=False, stop=(k == n - 1))

            def link(name):
                if name in fed:
                    pe.wait_ge(link_in, fed[name])
                k = nth[name]
                if k >= 2:
                    pe.wait_ge(link_used, k - 1)
                return link_ps[k % 2]

            def turn_rows(bank, src, width=D):
                for k in range(width // P):
                    for j in range(TB):
                        last = pe.transpose(bank[:, k * S + j * P:k * S + (j + 1) * P],
                                            src[:, j, k * P:(k + 1) * P], ident[:, :])
                return last

            def project(b, j):
                if j == 0 and b >= 2:
                    pe.wait_ge(y_used, b - 1)
                for u in range(UPB * b + j * UPB // TB, UPB * b + (j + 1) * UPB // TB):
                    heads, _ = unit_of(u)
                    pe.wait_ge(o_lo_ready, u + 1)
                    for k, h in enumerate(heads_in(heads)):
                        last = three(y_ps[b % 2][:, j, :], o_hi[u % RING][:, k, :], o_lo[u % RING][:, k, :],
                                     wo_hi[:, h, :], wo_lo[:, h, :], h, HEADS)
                    last.then_inc(o_used, 1)

            def prepare(b):
                pe.wait_ge(q_in[b % 2], 32 * (b // 2 + 1))
                turn_rows(link(f"prep.{b}"), gu_sb[b % 2]).then_inc(link_ready, 1)
                turn_rows(link(f"prepd.{b}"), dw_sb[b % 2], INNER).then_inc(link_ready, 1)

            def chain_of(b):
                turn_rows(link(f"x1.{b}"), x1).then_inc(link_ready, 1)
                bank = link(f"scale.{b}")
                for k in range(4):
                    last = pe.matmul(bank[:, k * P:(k + 1) * P], ones[:, :], diag[:, k, :], start=True, stop=True)
                last.then_inc(link_ready, 1)
                turn_rows(link(f"xq.{b}"), scaled).then_inc(link_ready, 1)
                turn_rows(link(f"wq.{b}"), hidden).then_inc(link_ready, 1)
                bank = link(f"mm1.{b}")
                for j in range(TB):
                    for k in range(KT):
                        last = pe.matmul(bank[:, j * S:(j + 1) * S], xq_t[:, k, j * P:(j + 1) * P], wq_t[:, k, :],
                                         start=(k == 0), stop=(k == KT - 1))
                last.then_inc(link_ready, 1)
                bank = link(f"row1.{b}")
                for k in range(2):
                    last = pe.matmul(bank[:, k * P:(k + 1) * P], ones[:, :], diag[:, k, :], start=True, stop=True)
                last.then_inc(link_ready, 1)
                turn_rows(link(f"act.{b}"), act_sb, INNER).then_inc(link_ready, 1)
                bank = link(f"scale2.{b}")
                for k in range(2):
                    last = pe.matmul(bank[:, k * P:(k + 1) * P], ones[:, :], diag[:, 2 + k, :], start=True, stop=True)
                last.then_inc(link_ready, 1)
                bank = link(f"q2.{b}")
                for j in range(TB):
                    pe.transpose(bank[:, j * P:(j + 1) * P], act_sb[:, j, :], ident[:, :])
                for j in range(TB):
                    last = pe.transpose(bank[:, S + j * P:S + (j + 1) * P], gate[:, j, :], ident[:, :])
                last.then_inc(link_ready, 1)
                bank = link(f"mm2.{b}")
                for j in range(TB):
                    last = pe.matmul(bank[:, j * D:(j + 1) * D], xq_t[:, 0, j * P:(j + 1) * P], wq_t[:, 0, :],
                                     start=True, stop=True)
                last.then_inc(link_ready, 1)
                bank = link(f"row2.{b}")
                for k in range(2):
                    last = pe.matmul(bank[:, k * P:(k + 1) * P], ones[:, :], diag[:, k, :], start=True, stop=True)
                last.then_inc(link_ready, 1)

            def experts(b):
                turn_rows(link(f"x2.{b}"), x2[b]).then_inc(link_ready, 1)
                pe.wait_ge(link_used, nth[f"x2.{b}"] + 1)
                for j in range(TB):
                    rows = slice(j * P, (j + 1) * P)
                    for c in range(5):
                        f = fth[b, j, c]
                        pe.wait_ge(raw_used, KT)
                        if f >= 4:
                            pe.wait_ge(f_used, f - 3)
                        cols = slice(WIDE, WIDE + D + EXPERTS) if c == 0 else slice((c - 1) * 512, c * 512)
                        width = cols.stop - cols.start
                        for k in range(KT):
                            last = three(f_ps[f % 4][:, 0:width], x2t_hi[:, k, rows], x2t_lo[:, k, rows],
                                         wall_hi[:, k, cols], wall_lo[:, k, cols], k, KT)
                        last.then_inc(f_ready, 1)

            pe.wait_ge(w_in, 32)
            for k in range(KT):
                bank = link(f"wt{k}")
                for j in range(TB):
                    pe.transpose(bank[:, j * P:(j + 1) * P], w_rows[:, j, k * P:(k + 1) * P], ident[:, :])
                pe.transpose(bank[:, D:D + EXPERTS], g_rows[:, k * P:(k + 1) * P],
                             ident[0:EXPERTS, 0:EXPERTS]).then_inc(link_ready, 1)
            pe.wait_ge(consts, 4)
            project(0, 0)
            project(0, 1)
            prepare(0)
            for b in range(1, B):
                project(b, 0)
                project(b, 1)
                chain_of(b - 1)
                if b < B - 1:
                    prepare(b)
            experts(0)
            prepare(3)
            chain_of(3)
            for b in range(1, B):
                experts(b)

        @block.scalar
        def _(act):
            ot_view = ot[:, :].rearrange("p (h t) -> p h t", h=HEADS)

            def high_parts(b):
                for u in range(UPB * b, UPB * (b + 1)):
                    heads, rows = unit_of(u)
                    if u >= RING:
                        act.wait_ge(o_used, u - RING + 1)
                    act.copy(o_hi[u % RING][:, :, :], ot_view[:, heads, rows]).then_inc(o_hi_ready, 1)

            def row_of(name):
                act.wait_ge(link_ready, nth[name] + 1)
                act.copy(row[:, :], link_ps[nth[name] % 2][:, 0:D]).then_inc(row_ready, 1)

            exps = [0]

            def exponential(dst, src, scale=1.0, bias=None):
                exps[0] += 1
                act.wait_ge(exp_in, exps[0])
                if bias is None:
                    act.activation(dst, src, ACT.Exp, scale=scale).then_inc(exp_out, 1)
                else:
                    act.activation(dst, src, ACT.Exp, scale=scale, bias=bias).then_inc(exp_out, 1)

            def chain_of(b):
                row_of(f"row1.{b}")
                exponential(gate[:, :, :], hidden[:, :, 0:INNER], -1.0)
                row_of(f"row2.{b}")

            def experts(b):
                name = f"x2.{b}"
                act.wait_ge(link_ready, nth[name] + 1)
                act.copy(x2t_hi[:, :, :].rearrange("p k t -> p (k t)"),
                         link_ps[nth[name] % 2][:, :]).then_inc(x2t_hi_ready, 1)
                for j in range(TB):
                    exponential(share[:, 1:2], top[:, 1:2], 1.0, share[:, 0:1])

            for k in range(KT):
                act.wait_ge(link_ready, k + 1)
                act.copy(wall_hi[:, k, WIDE:], link_ps[k][:, 0:D + EXPERTS]).then_inc(wall_hi_ready, 1)
            high_parts(0)
            for k in range(KT):
                act.wait_ge(raw_in, 16 * (k + 1))
                act.copy(wall_hi[:, k, 0:WIDE].rearrange("p (e r) -> p e r", e=EXPERTS),
                         raw[:, :].rearrange("p (r e) -> p e r", e=EXPERTS)).then_inc(wall_hi_ready, 1)
            high_parts(1)
            chain_of(0)
            high_parts(2)
            chain_of(1)
            high_parts(3)
            chain_of(2)
            experts(0)
            chain_of(3)
            for b in range(1, B):
                experts(b)

        @block.vector
        def _(dve):
            count = [0]

            def then(ins):
                count[0] += 1
                ins.then_inc(chain, 1)
                dve.wait_ge(chain, count[0])

            def arrived(name):
                dve.wait_ge(link_ready, nth[name] + 1)
                return link_ps[nth[name] % 2]

            exps, powers = [0], [0]

            def exp_made():
                exps[0] += 1
                dve.wait_ge(exp_out, exps[0])

            def power_made():
                powers[0] += 1
                dve.wait_ge(pow_out, powers[0])

            def normalise(src, dst, tiles, done):
                n = len(tiles)
                for j in tiles:
                    ins = dve.bn_stats(st[:, j, :], src[:, j, :])
                then(ins)
                for j in tiles:
                    ins = dve.bn_aggr(mv[:, j, :], st[:, j, :])
                then(ins)
                dve.tensor_scalar(v1[:, 0:n], mv[:, tiles[0]:tiles[0] + n, 1], EPS_LN, None, ALU.add)\
                   .then_inc(pow_in, 1)
                power_made()
                for k, j in enumerate(tiles):
                    ins = dve.tensor_scalar(dst[:, j, :], src[:, j, :], mv[:, j, 0:1], v1[:, 8 + k:9 + k],
                                            ALU.subtract, ALU.mult)
                    done(ins, j)

            def quantise(src, scales, inverse, width):
                then(dve.tensor_reduce(scales, src, AX.X, ALU.max, apply_absolute_value=True))
                then(dve.tensor_scalar(scales, scales, EPS_Q, 1.0 / QMAX, ALU.max, ALU.mult))
                then(dve.reciprocal(inverse, scales))
                for j in range(TB):
                    ins = dve.tensor_scalar(src[:, j, :], src[:, j, :], inverse[:, j:j + 1], ROUND,
                                            ALU.mult, ALU.add)
                then(ins)
                return dve.tensor_scalar(src, src, ROUND + QMAX, ROUND - QMAX, ALU.min, ALU.max)

            def balance(amax_x, amax_weight, n):
                then(dve.tensor_scalar(v1[:, 0:n], amax_weight, EPS_Q, None, ALU.max))
                then(dve.reciprocal(v1[:, 4:4 + n], v1[:, 0:n]))
                dve.scalar_tensor_tensor(v1[:, 0:n], amax_x, EPS_Q, v1[:, 4:4 + n], ALU.max, ALU.mult)\
                   .then_inc(pow_in, 1)
                power_made()
                then(dve.tensor_scalar(smooth[:, 0:n], v1[:, 8:8 + n], EPS_Q, None, ALU.max))
                then(dve.reciprocal(smooth[:, 2:2 + n], smooth[:, 0:n]))

            for k in range(KT):
                dve.wait_ge(wall_hi_ready, k + 1)
                dve.tensor_tensor(wall_lo[:, k, WIDE:], link_ps[k][:, 0:D + EXPERTS],
                                  wall_hi[:, k, WIDE:].bitcast(F32), ALU.subtract).then_inc(link_used, 1)

            def chain_of(b):
                bank = arrived(f"prep.{b}")
                dve.tensor_reduce(amax_w[:, 0:KT], bank[:, :].rearrange("p (k o) -> p k o", k=KT), AX.X,
                                  ALU.max, apply_absolute_value=True).then_inc(link_used, 1)
                bank = arrived(f"prepd.{b}")
                dve.tensor_reduce(amax_w[:, KT:KT + 1], bank[:, 0:S], AX.X, ALU.max,
                                  apply_absolute_value=True).then_inc(link_used, 1)
                dve.wait_ge(link_used, nth[f"prepd.{b}"] + 1)
                dve.wait_ge(xb_ready, b + 1)
                dve.wait_ge(o_used, UPB * (b + 1))
                dve.tensor_tensor(y1[:, :, :], y_ps[b % 2][:, :, :], xb[b % 2][:, :, :], ALU.add).then_inc(y_used, 1)
                dve.wait_ge(y_used, b + 1)
                normalise(y1, x1, [0, 1], lambda ins, j: ins.then_inc(link_in, 1) if j else None)
                dve.wait_ge(link_in, fed[f"x1.{b}"])
                bank = arrived(f"x1.{b}")
                dve.tensor_reduce(smooth[:, 0:2], bank[:, :].rearrange("p (k t) -> p k t", k=KT), AX.X,
                                  ALU.max, apply_absolute_value=True).then_inc(link_used, 1)
                dve.wait_ge(link_used, nth[f"x1.{b}"] + 1)
                balance(smooth[:, 0:2], amax_w[:, 0:KT], 2)
                for k in range(4):
                    ins = dve.tensor_scalar(diag[:, k, :], ident[:, :], smooth[:, (k + 2) % 4:(k + 2) % 4 + 1],
                                            None, ALU.mult)
                ins.then_inc(link_in, 1)
                bank = arrived(f"scale.{b}")
                wide = lambda a, n: a.unsqueeze(1).broadcast_to([P, TB, n])
                dve.wait_ge(q_in[b % 2], 32 * (b // 2 + 1))
                then(dve.tensor_tensor(scaled[:, :, :], x1[:, :, :], wide(bank[:, 0:D], D), ALU.mult))
                dve.tensor_tensor(hidden[:, :, :], gu_sb[b % 2][:, :, :], wide(bank[:, D:2 * D], D), ALU.mult)\
                   .then_inc(link_used, 1)
                dve.wait_ge(link_used, nth[f"scale.{b}"] + 1)
                quantise(scaled[:, :, :], x_scale[:, :], inv[:, :], D).then_inc(link_in, 1)
                quantise(hidden[:, :, :], w_scale[:, :], inv[:, :], D).then_inc(link_in, 1)
                bank = arrived(f"xq.{b}")
                dve.tensor_scalar(xq_t[:, :, :].rearrange("p k t -> p (k t)"), bank[:, :], -ROUND, None,
                                  ALU.add).then_inc(link_used, 1)
                for k in range(2):
                    ins = dve.tensor_scalar(diag[:, k, :], ident[:, :], w_scale[:, k:k + 1], None, ALU.mult)
                bank = arrived(f"wq.{b}")
                dve.tensor_scalar(wq_t[:, :, :].rearrange("p k t -> p (k t)"), bank[:, :], -ROUND, None,
                                  ALU.add).then_inc(link_used, 1)
                dve.wait_ge(link_used, nth[f"wq.{b}"] + 1)
                dve.sem_inc(link_in, 2)
                bank = arrived(f"mm1.{b}")
                dve.wait_ge(row_ready, 2 * b + 1)
                for j in range(TB):
                    ins = dve.scalar_tensor_tensor(hidden[:, j, :], bank[:, j * S:(j + 1) * S],
                                                   x_scale[:, j:j + 1], row[:, :], ALU.mult, ALU.mult)
                ins.then_inc(link_used, 1)
                dve.wait_ge(link_used, nth[f"mm1.{b}"] + 1)
                dve.sem_inc(link_used, 1)
                dve.sem_inc(exp_in, 1)
                then(dve.tensor_tensor(act_sb[:, :, :], hidden[:, :, 0:INNER], hidden[:, :, INNER:], ALU.mult))
                exp_made()
                then(dve.tensor_scalar(gate[:, :, :], gate[:, :, :], 1.0, None, ALU.add))
                then(dve.reciprocal(gate[:, :, :], gate[:, :, :]))
                then(dve.tensor_tensor(act_sb[:, :, :], act_sb[:, :, :], gate[:, :, :], ALU.mult))
                dve.sem_inc(link_in, 1)
                bank = arrived(f"act.{b}")
                dve.tensor_reduce(smooth[:, 0:1], bank[:, 0:S], AX.X, ALU.max,
                                  apply_absolute_value=True).then_inc(link_used, 1)
                dve.wait_ge(link_used, nth[f"act.{b}"] + 1)
                balance(smooth[:, 0:1], amax_w[:, KT:KT + 1], 1)
                for k in range(2):
                    ins = dve.tensor_scalar(diag[:, 2 + k, :], ident[:, :],
                                            smooth[:, 2 - 2 * k:3 - 2 * k], None, ALU.mult)
                ins.then_inc(link_in, 1)
                bank = arrived(f"scale2.{b}")
                then(dve.tensor_tensor(act_sb[:, :, :], act_sb[:, :, :], wide(bank[:, 0:P], P), ALU.mult))
                dve.tensor_tensor(gate[:, :, :], dw_sb[b % 2][:, :, :], wide(bank[:, P:2 * P], P), ALU.mult)\
                   .then_inc(link_used, 1)
                dve.wait_ge(link_used, nth[f"scale2.{b}"] + 1)
                dve.sem_inc(q_used, 1)
                then(quantise(act_sb[:, :, :], x_scale[:, :], inv[:, :], INNER))
                then(quantise(gate[:, :, :], w_scale[:, :], inv[:, :], INNER))
                dve.sem_inc(link_in, 1)
                for k in range(2):
                    ins = dve.tensor_scalar(diag[:, k, :], ident[:, :], w_scale[:, k:k + 1], None, ALU.mult)
                bank = arrived(f"q2.{b}")
                dve.tensor_scalar(xq_t[:, 0, :], bank[:, 0:S], -ROUND, None, ALU.add)
                dve.tensor_scalar(wq_t[:, 0, :], bank[:, S:2 * S], -ROUND, None, ALU.add).then_inc(link_used, 1)
                dve.wait_ge(link_used, nth[f"q2.{b}"] + 1)
                dve.sem_inc(link_in, 2)
                bank = arrived(f"mm2.{b}")
                dve.wait_ge(row_ready, 2 * b + 2)
                for j in range(TB):
                    ins = dve.scalar_tensor_tensor(y1[:, j, :], bank[:, j * D:(j + 1) * D],
                                                   x_scale[:, j:j + 1], row[:, :], ALU.mult, ALU.mult)
                ins.then_inc(link_used, 1)
                dve.wait_ge(link_used, nth[f"mm2.{b}"] + 1)
                dve.sem_inc(link_used, 1)
                then(dve.tensor_tensor(y1[:, :, :], y1[:, :, :], x1[:, :, :], ALU.add))
                normalise(y1, x2[b], [0, 1], lambda ins, j: ins.then_inc(link_in, 1) if j else None)

            def experts(b):
                name = f"x2.{b}"
                bank = arrived(name)
                dve.wait_ge(x2t_hi_ready, b + 1)
                dve.tensor_tensor(x2t_lo[:, :, :].rearrange("p k t -> p (k t)"), bank[:, :],
                                  x2t_hi[:, :, :].rearrange("p k t -> p (k t)").bitcast(F32),
                                  ALU.subtract).then_inc(link_used, 1)
                if b >= 2:
                    dve.wait_ge(stored[b % 2], 16 * TB * (b // 2))
                for j in range(TB):
                    f = fth[b, j, 0]
                    bank = f_ps[f % 4]
                    dve.wait_ge(f_ready, f + 1)
                    then(dve.tensor_scalar(logit[:, :], bank[:, D:D + EXPERTS], CLIP, -CLIP, ALU.min, ALU.max))
                    dve.tensor_tensor(mixed[:, j, :], bank[:, 0:D], x2[b][:, j, :], ALU.add).then_inc(f_used, 1)
                    dve.wait_ge(f_used, f + 1)
                    then(dve.max(top[:, :], logit[:, :]))
                    then(dve.max_index(top_at[:, :], top[:, :], logit[:, :]))
                    dve.tensor_copy(top_f[:, :], top_at[:, 0:2])
                    dve.tensor_scalar(share[:, 0:1], top[:, 0:1], -1.0, None, ALU.mult).then_inc(exp_in, 1)
                    exp_made()
                    then(dve.tensor_scalar(share[:, 2:3], share[:, 1:2], 1.0, None, ALU.add))
                    then(dve.reciprocal(share[:, 2:3], share[:, 2:3]))
                    then(dve.tensor_tensor(share[:, 3:4], share[:, 1:2], share[:, 2:3], ALU.mult))
                    then(dve.tensor_scalar(weight[:, :], iota8[:, :], top_f[:, 0:1], share[:, 2:3],
                                           ALU.is_equal, ALU.mult))
                    then(dve.tensor_scalar(second[:, :], iota8[:, :], top_f[:, 1:2], share[:, 3:4],
                                           ALU.is_equal, ALU.mult))
                    then(dve.tensor_tensor(weight[:, :], weight[:, :], second[:, :], ALU.add))
                    for c in range(1, 5):
                        f = fth[b, j, c]
                        dve.wait_ge(f_ready, f + 1)
                        for h in range(2):
                            e = 2 * (c - 1) + h
                            ins = dve.scalar_tensor_tensor(mixed[:, j, :], f_ps[f % 4][:, h * D:(h + 1) * D],
                                                           weight[:, e:e + 1], mixed[:, j, :],
                                                           ALU.mult, ALU.add)
                            if h == 0:
                                then(ins)
                        ins.then_inc(f_used, 1)
                        dve.wait_ge(f_used, f + 1)
                    normalise(mixed, result[b % 2], [j], lambda ins, j: ins.then_inc(result_ready, 1))

            def low_table():
                for k in range(KT):
                    dve.wait_ge(wall_hi_ready, KT + k + 1)
                    dve.tensor_tensor(wall_lo[:, k, 0:WIDE].rearrange("p (e r) -> p e r", e=EXPERTS),
                                      raw[:, :].rearrange("p (r e) -> p e r", e=EXPERTS),
                                      wall_hi[:, k, 0:WIDE].bitcast(F32).rearrange("p (e r) -> p e r", e=EXPERTS),
                                      ALU.subtract).then_inc(raw_used, 1)

            low_table()
            chain_of(0)
            chain_of(1)
            chain_of(2)
            experts(0)
            chain_of(3)
            for b in range(1, B):
                experts(b)


def program(nc, inputs, out):
    a = inputs
    table = nc.dram_tensor("table", (TABLE_ROWS, EXPERTS), F32, kind="Internal").ap()
    with ExitStack() as ctx:
        def sb(name, shape, dt=F32):
            return ctx.enter_context(nc.sbuf_tensor(name, shape, dt))

        kept = (sb("ident", [P, P]), sb("ot", [P, HEADS * T]), sb("wo_hi", [P, HEADS, D], F32R),
                sb("wo_lo", [P, HEADS, D], F32R))
        w = [a[f"L0_attn_w{m}_{part}"] for m in "qkvo" for part in ("codes", "scales")]
        attention(nc, a["x"], w, [a[f"L0_attn_b{m}"] for m in "qkv"],
                  [a["L0_ffn_mask_idx"], a["L0_ffn_importance"], a["L0_ffn_atoms"],
                   a["L0_ffn_expert_atom_weights"], table], kept)
        layers(nc, a["x"], a["L0_attn_bo"], a["fside_BxS2xS2_0"], a["ctx_1024"], a["L0_ffn_gate_w"],
               a["L0_ffn_W"], table, out, kept)


_INS = ["x", "fside_BxS2xS2_0", "ctx_1024",
        "L0_attn_wq_codes", "L0_attn_wq_scales", "L0_attn_bq", "L0_attn_wk_codes", "L0_attn_wk_scales",
        "L0_attn_bk", "L0_attn_wv_codes", "L0_attn_wv_scales", "L0_attn_bv", "L0_attn_wo_codes",
        "L0_attn_wo_scales", "L0_attn_bo", "L0_ffn_gate_w", "L0_ffn_W", "L0_ffn_atoms",
        "L0_ffn_expert_atom_weights", "L0_ffn_importance", "L0_ffn_mask_idx"]


def kernel(**inputs):
    import numpy as np
    import concourse.bacc as bacc
    from concourse.bass_utils import run_bass_kernel_spmd

    nc = bacc.Bacc("TRN2", target_bir_lowering=False, num_devices=1)
    arrays, args = {}, {}
    for name in _INS:
        a = np.ascontiguousarray(inputs[name])
        arrays["in_" + name] = a
        args[name] = nc.dram_tensor("in_" + name, a.shape, mybir.dt.from_np(a.dtype), kind="ExternalInput").ap()
    out = nc.dram_tensor("out_0", (B, S, D), F32, kind="ExternalOutput").ap()
    program(nc, args, out)
    r = run_bass_kernel_spmd(nc, [arrays], core_ids=[0])
    return r.results[0]["out_0"]
```

```python
from contextlib import ExitStack

import concourse.bass as bass
from concourse import mybir

F32 = mybir.dt.float32
F32R = mybir.dt.float32r
ALU = mybir.AluOpType
ACT = mybir.ActivationFunctionType
AX = mybir.AxisListType
P = 128

B, S, D = 4, 256, 256
HEADS, HD, BLK = 16, 128, 32
T = B * S
TILES = T // P
KT = D // P
PAIRS = HEADS // 2
STEPS = 2 * B
SCALE = float(HD) ** -0.5
I32, U32, BF16 = mybir.dt.int32, mybir.dt.uint32, mybir.dt.bfloat16
EXPERTS, ATOMS, NS = 8, 64, 2048
NS_TILES = NS // P
TABLE_ROWS = D * D + P
SETUP_DONE = 3

QK_SLOT = [0, 2, 3, 4, 5, 6, 8, 10]
V_SLOT = {0: 1, 5: 7, 6: 9, 7: 11}
UNITS = 12


def qk_seq(i, c):
    return (i + (c - 5) // 8) * UNITS + 8 + QK_SLOT[(c - 5) % 8]


def v_seq(i, b):
    return i * UNITS + 8 + V_SLOT[0] if b == 3 else (i - 1) * UNITS + 8 + V_SLOT[5 + b]


def positive(eng, sem, value):
    if not isinstance(value, int) or value > 0:
        eng.wait_ge(sem, value)


def hold(eng, sem, value, passed):
    eng.wait_ge(sem, value)
    if not isinstance(value, int):
        eng.sem_inc(passed, 1)


def attention(nc, x, w, bias_rows, moe, kept):
    with ExitStack() as ctx:
        def sb(name, shape, dt=F32):
            return ctx.enter_context(nc.sbuf_tensor(name, shape, dt))

        def ps(name, shape, dt=F32):
            return ctx.enter_context(nc.psum_tensor(name, shape, dt))

        def sem(name):
            return ctx.enter_context(nc.semaphore(name))

        ident, ot, wo_hi, wo_lo = kept
        xt_hi = sb("xt_hi", [P, KT, T], F32R)
        xt_lo = sb("xt_lo", [P, KT, T], F32R)
        bias = sb("bias", [P, 3 * HEADS])
        code = [sb(f"code{g}", [P, 512]) for g in range(4)]
        scal = [sb(f"scal{g}", [P, 512]) for g in range(4)]
        wqk_hi = [sb(f"wqk_hi{p}", [P, 2, KT, P], F32R) for p in range(2)]
        wqk_lo = [sb(f"wqk_lo{p}", [P, 2, KT, P], F32R) for p in range(2)]
        wv_hi = sb("wv_hi", [P, KT, 256], F32R)
        wv_lo = sb("wv_lo", [P, KT, 256], F32R)
        qk_hi = [sb(f"qk_hi{p}", [P, 2, T], F32R) for p in range(2)]
        qk_lo = [sb(f"qk_lo{p}", [P, 2, T], F32R) for p in range(2)]
        v_hi = sb("v_hi", [P, TILES, 256], F32R)
        v_lo = sb("v_lo", [P, TILES, 256], F32R)
        prob = [sb(f"prob{p}", [P, 2, S]) for p in range(2)]
        pt_hi = [sb(f"pt_hi{p}", [P, 2, S], F32R) for p in range(2)]
        pt_lo = [sb(f"pt_lo{p}", [P, 2, S], F32R) for p in range(2)]
        xrow = ot[:, 0:TILES * D].rearrange("p (t d) -> p t d", t=TILES)
        brow = ot[0:3 * HEADS, TILES * D:TILES * D + P]
        idx, importance, atoms, expert_atoms, table = moe
        at = TILES * D + P
        def region(cols, dt=F32):
            nonlocal at
            at += cols
            return ot[:, at - cols:at] if dt is F32 else ot[:, at - cols:at].bitcast(dt)
        zeros = region(TABLE_ROWS * EXPERTS // P)
        idx_row = region(NS, I32)
        same = region(NS).rearrange("p (t s) -> p t s", t=NS_TILES)
        earlier = region(NS).rearrange("p (t s) -> p t s", t=NS_TILES)
        atoms_imp = region(NS)
        atoms_sb, imp_sb = atoms_imp[0:ATOMS, :], atoms_imp[96:96 + EXPERTS, :]
        before = region(P)
        idx_16 = region(P, I32)[0:NS_TILES, :]
        idx_16f = region(P)[0:NS_TILES, :]
        mix = region(ATOMS)[0:EXPERTS, :]
        mix_t = region(EXPERTS)[0:ATOMS, :]
        mix_s = region(4)[0:EXPERTS, :]
        idx_f = region(NS_TILES)
        idx_i = region(NS_TILES, I32)
        col_i = region(NS_TILES, I32)
        row_i = region(NS_TILES, I32)
        dup = region(NS_TILES)
        place_f = region(NS_TILES)
        spare_i = region(1, I32)
        gates = region(NS_TILES * EXPERTS)
        scaled = region(NS_TILES * EXPERTS)
        assert at <= HEADS * T
        summed = sb("summed", [P, NS_TILES * EXPERTS])
        place = sb("place", [P, NS_TILES], U32)
        tile_rows = sb("tile_rows", [P, EXPERTS])
        tile_place = sb("tile_place", [P, 1], U32)
        negmax = [sb(f"negmax{p}", [P, 2]) for p in range(2)]
        rowsum = [sb(f"rowsum{p}", [P, 2]) for p in range(2)]
        rowmax = [sb(f"rowmax{p}", [P, 2]) for p in range(2)]
        rinv = [sb(f"rinv{p}", [P, 2]) for p in range(2)]

        proj = [ps(f"proj{p}", [P, 512]) for p in range(2)]
        score = [ps(f"score{p}", [P, 2, S]) for p in range(2)]
        ptp = [ps(f"ptp{p}", [P, 2, S]) for p in range(2)]
        op = [ps(f"op{p}", [P, 512]) for p in range(2)]

        x_loaded, b_loaded = sem("x_loaded"), sem("b_loaded")
        ident_ready = sem("ident_ready")
        xt_ready, xt_copied, xt_split = sem("xt_ready"), sem("xt_copied"), sem("xt_split")
        bias_turned, bias_ready = sem("bias_turned"), sem("bias_ready")
        w_loaded = [sem(f"w_loaded{g}") for g in range(4)]
        w_made = [sem(f"w_made{g}") for g in range(4)]
        w_hi = [sem(f"w_hi{g}") for g in range(4)]
        w_lo = [sem(f"w_lo{g}") for g in range(4)]
        proj_ready, proj_hi, proj_lo = sem("proj_ready"), sem("proj_hi"), sem("proj_lo")
        score_ready, negmax_ready, exp_done = sem("score_ready"), sem("negmax_ready"), sem("exp_done")
        rinv_ready, prob_ready = sem("rinv_ready"), sem("prob_ready")
        pt_ready, pt_hi_ready, pt_lo_ready = sem("pt_ready"), sem("pt_hi_ready"), sem("pt_lo_ready")
        o_ready, o_stored = sem("o_ready"), sem("o_stored")
        setup_loaded, zeros_ready, table_zeroed = sem("setup_loaded"), sem("zeros_ready"), sem("table_zeroed")
        masks_ready, idx_float, mix_ready = sem("masks_ready"), sem("idx_float"), sem("mix_ready")
        setup_pe, setup_dve, setup_act = sem("setup_pe"), sem("setup_dve"), sem("setup_act")
        pool_passed, act_passed = sem("pool_passed"), sem("act_passed")
        tile_staged, scattered = sem("tile_staged"), sem("scattered")

        def passes(eng, body, setup):
            for t in range(3, STEPS):
                body(-1, t)
                setup(t)
            for t in range(STEPS):
                body(0, t)
            with eng.Fori(1, PAIRS - 1) as i:
                for t in range(STEPS):
                    body(i, t)
            for t in range(STEPS):
                body(PAIRS - 1, t)

        LOADS = [10, 5, 10, 5]

        def weight_parts(g, i):
            if g == 3:
                return (z[:, bass.ds(2 * (i + 1), 2), :].rearrange("p a b -> p (a b)") for z in (wo_hi, wo_lo))
            if g == 1:
                return (z[:, :, :].rearrange("p a b -> p (a b)") for z in (wv_hi, wv_lo))
            return (z[g // 2][:, :, :, :].rearrange("p a b c -> p (a b c)") for z in (wqk_hi, wqk_lo))

        def within(i, t, ahead, count=STEPS * PAIRS):
            return not isinstance(i, int) or 0 <= STEPS * i + t + ahead < count

        block = ctx.enter_context(nc.Block())

        @block.sync
        def _(sp):
            sp.dma_start(xrow, x.rearrange("b (s p) d -> p (b s) d", p=P)).then_inc(x_loaded, 16)

            def load(p, blocks=range(4)):
                for g in blocks:
                    if not isinstance(p, int) or p > 0:
                        sp.wait_ge(w_lo[g], p)
                    if g == 3:
                        codes, scales = w[6], w[7]
                        src = codes[bass.ds(p * 256, 256), :].rearrange("(k p) f -> p k f", p=P)
                        sp.dma_start(code[g][:, :].rearrange("p (k f) -> p k f", k=2), src).then_inc(w_loaded[g], 16)
                        rows = scales[bass.ds(p * 8, 8), :].rearrange("(k b) f -> b k f", k=2)
                        for b in range(4):
                            sp.dma_start(scal[g][b * BLK:(b + 1) * BLK, :].rearrange("p (k f) -> p k f", k=2),
                                         rows[b:b + 1].broadcast_to([BLK, 2, 256])).then_inc(w_loaded[g], 16)
                        continue
                    width = 256 if g == 1 else P
                    col = p * 256 + (P if g == 2 else 0)
                    for m in range(1 if g == 1 else 2):
                        codes, scales = (w[4], w[5]) if g == 1 else (w[2 * m], w[2 * m + 1])
                        span = slice(m * 256, m * 256 + KT * width)
                        src = codes.rearrange("(k p) f -> p k f", p=P)[:, :, bass.ds(col, width)]
                        sp.dma_start(code[g][:, span].rearrange("p (k f) -> p k f", k=KT), src)\
                          .then_inc(w_loaded[g], 16)
                        rows = scales.rearrange("(k b) f -> b k f", k=KT)[:, :, bass.ds(col, width)]
                        for b in range(4):
                            sp.dma_start(scal[g][b * BLK:(b + 1) * BLK, span].rearrange("p (k f) -> p k f", k=KT),
                                         rows[b:b + 1].broadcast_to([BLK, KT, width])).then_inc(w_loaded[g], 16)

            load(0, [0])
            for k in range(3):
                sp.dma_start(brow[k * HEADS:(k + 1) * HEADS, :],
                             bias_rows[k].rearrange("(h f) -> h f", f=HD)).then_inc(b_loaded, 16)
            load(0, [1, 2, 3])
            sp.wait_ge(zeros_ready, 1)
            sp.dma_start(table.rearrange("(p a) e -> p (a e)", p=P), zeros).then_inc(table_zeroed, 16)
            with sp.Fori(1, PAIRS) as p:
                load(p)
            sp.wait_ge(o_stored, PAIRS * STEPS)

        @block.gpsimd
        def _(pool):
            pool.memset(ident[:, :], 0.0).then_inc(ident_ready, 1)
            pool.wait_ge(ident_ready, 1)
            pool.affine_select(out=ident[:, :], in_=ident[:, :], compare_op=ALU.not_equal, fill=1.0,
                               base=0, pattern=[[-1, P]], channel_multiplier=1).then_inc(ident_ready, 1)

            for dst, src in ((idx_16, idx.rearrange("(t s) -> t s", s=P)), (mix, expert_atoms),
                             (idx_row, idx.rearrange("(a n) -> a n", a=1).broadcast_to([P, NS])),
                             (imp_sb, importance), (atoms_sb, atoms)):
                pool.dma_start(dst, src).then_inc(setup_loaded, 16)

            pool.memset(before, 1.0).then_inc(masks_ready, 1)
            pool.iota(spare_i, pattern=[[0, 1]], base=D * D, channel_multiplier=1).then_inc(masks_ready, 1)
            pool.wait_ge(masks_ready, 2)
            pool.affine_select(out=before, in_=before, compare_op=ALU.is_gt, fill=0.0, base=0,
                               pattern=[[-1, P]], channel_multiplier=1).then_inc(masks_ready, 1)

            def scatter(i, half):
                n = 2 * i + half
                if isinstance(i, int) and n == 0:
                    pool.wait_ge(table_zeroed, 16)
                    pool.wait_ge(setup_dve, SETUP_DONE)
                else:
                    hold(pool, scattered, 16 * n, pool_passed)
                pool.tensor_copy(tile_rows[:, :], summed[:, bass.ds(n * EXPERTS, EXPERTS)]).then_inc(tile_staged, 1)
                pool.tensor_copy(tile_place[:, :], place[:, bass.ds(n, 1)]).then_inc(tile_staged, 1)
                hold(pool, tile_staged, 2 * (n + 1), pool_passed)
                pool.indirect_dma_start(
                    out=table, out_offset=bass.IndirectOffsetOnAxis(ap=tile_place[:, 0:1], axis=0),
                    in_=tile_rows[:, :], in_offset=None, compute_op=ALU.add).then_inc(scattered, 16)

            def multiply(g, i):
                pool.wait_ge(w_loaded[g], 16 * LOADS[g] * (i + 2))
                pool.tensor_tensor(code[g][:, :], code[g][:, :], scal[g][:, :], ALU.mult).then_inc(w_made[g], 1)

            def make_low(g, i):
                hi, lo = weight_parts(g, i)
                hold(pool, w_hi[g], i + 2, pool_passed)
                pool.tensor_tensor(lo, code[g][:, :], hi.bitcast(F32), ALU.subtract).then_inc(w_lo[g], 1)

            def step(i, t):
                n = STEPS * i + t
                last = isinstance(i, int) and i == PAIRS - 1
                if isinstance(i, int) and i == -1:
                    if t == 3:
                        multiply(0, i)
                    if t < 7:
                        make_low(t - 3, i)
                    if t < 6:
                        multiply(t - 2, i)
                elif not last and t % 2 == 0:
                    multiply(t // 2, i)
                elif not last:
                    make_low(t // 2, i)
                if t in (3, 7) and not (isinstance(i, int) and i < 0):
                    scatter(i, t // 4)
                if within(i, t, 1):
                    hold(pool, rinv_ready, n + 2, pool_passed)
                    k = (t + 1) % 2
                    for q in range(2):
                        pool.tensor_scalar(prob[k][:, q, :], prob[k][:, q, :], rinv[k][:, q:q + 1], 1.0,
                                           ALU.mult, ALU.mult).then_inc(prob_ready, 1)

            def setup(t):
                if t == 4:
                    pool.memset(zeros, 0.0).then_inc(zeros_ready, 1)

            passes(pool, step, setup)
            pool.wait_ge(scattered, 16 * NS_TILES)

        @block.tensor
        def _(pe):
            pe.wait_ge(ident_ready, 2)
            pe.wait_ge(x_loaded, 16)
            for u in range(4):
                k, half = u % 2, u // 2
                if u >= 2:
                    pe.wait_ge(xt_split, u - 1)
                for j in range(4):
                    last = pe.transpose(proj[u % 2][:, j * P:(j + 1) * P],
                                        xrow[:, half * 4 + j, k * P:(k + 1) * P], ident[:, :])
                last.then_inc(xt_ready, 1)
            pe.wait_ge(b_loaded, 48)
            pe.transpose(op[0][:, 0:3 * HEADS], brow, ident[0:3 * HEADS, 0:3 * HEADS]).then_inc(bias_turned, 1)
            pe.wait_ge(xt_split, 4)
            pe.wait_ge(bias_ready, 1)

            pe.wait_ge(idx_float, 1)
            pe.transpose(op[1][:, 0:NS_TILES], idx_16f, ident[0:NS_TILES, 0:NS_TILES]).then_inc(setup_pe, 1)

            def setup(t):
                if t == 3:
                    pe.wait_ge(mix_ready, 1)
                    pe.transpose(ptp[1][0:ATOMS, 0, 0:EXPERTS], mix, ident[0:EXPERTS, 0:EXPERTS])\
                        .then_inc(setup_pe, 1)
                    for t in range(NS_TILES):
                        last = pe.transpose(ptp[0][:, 0, t * EXPERTS:(t + 1) * EXPERTS],
                                            imp_sb[:, t * P:(t + 1) * P], ident[96:96 + EXPERTS, 96:96 + EXPERTS])
                    last.then_inc(setup_pe, 1)
                elif t == 4:
                    pe.wait_ge(setup_dve, 1)
                    for t in range(NS_TILES):
                        last = pe.matmul(op[0][:, t * EXPERTS:(t + 1) * EXPERTS],
                                         atoms_sb[:, t * P:(t + 1) * P], mix_t, start=True, stop=True)
                    last.then_inc(setup_pe, 1)
                elif t == 6:
                    pe.wait_ge(setup_dve, 2)
                    for t in range(NS_TILES):
                        last = pe.matmul(op[1][:, t * EXPERTS:(t + 1) * EXPERTS],
                                         same[:, t, :], scaled[:, t * EXPERTS:(t + 1) * EXPERTS],
                                         start=True, stop=True)
                    last.then_inc(setup_pe, 1)
                elif t == 7:
                    pe.wait_ge(setup_dve, SETUP_DONE)

            def three(out, lh, ll, rh, rl, k, n):
                pe.matmul(out, lh, rh, start=(k == 0), stop=False)
                pe.matmul(out, lh, rl, start=False, stop=False)
                return pe.matmul(out, ll, rh, start=False, stop=(k == n - 1))

            def step(i, t):
                n = STEPS * i + t
                if within(i, t, 2):
                    m = n + 2
                    c = t + 2
                    par, b = (c // 4) % 2, c % 4
                    pe.wait_ge(proj_lo, qk_seq(i, 4 * (c // 4) + 2 * (b // 2) + 1) + 1)
                    positive(pe, exp_done, m - 1)
                    lo, hi = qk_lo[par], qk_hi[par]
                    keys = slice(b * S, (b + 1) * S)
                    for q in range(2):
                        rows = slice(b * S + q * P, b * S + (q + 1) * P)
                        last = three(score[c % 2][:, q, :], hi[:, 0, rows], lo[:, 0, rows],
                                     hi[:, 1, keys], lo[:, 1, keys], 0, 1)
                    last.then_inc(score_ready, 1)
                if within(i, t, 5):
                    c = t + 5
                    par, part = (c // 4) % 2, c % 4
                    pair = i + c // 8
                    seq = qk_seq(i, c)
                    bank = proj[QK_SLOT[t] % 2]
                    pe.wait_ge(w_lo[2 * par], pair + 1)
                    positive(pe, proj_lo, seq - 1)
                    m, half = part % 2, part // 2
                    cols = slice(half * 512, (half + 1) * 512)
                    for k in range(KT):
                        last = three(bank[:, :], wqk_hi[par][:, m, k, :], wqk_lo[par][:, m, k, :],
                                     xt_hi[:, k, cols], xt_lo[:, k, cols], k, KT)
                    last.then_inc(proj_ready, 1)
                if within(i, t, 0):
                    pe.wait_ge(prob_ready, 2 * (n + 1))
                    positive(pe, pt_lo_ready, n - 1)
                    for k in range(2):
                        for q in range(2):
                            last = pe.transpose(ptp[t % 2][:, k, q * P:(q + 1) * P],
                                                prob[t % 2][:, q, k * P:(k + 1) * P], ident[:, :])
                    last.then_inc(pt_ready, 1)
                if within(i, t, -1):
                    m, c = n - 1, (t - 1) % 8
                    weigh(i, t, m, c)
                if t in V_SLOT and not (isinstance(i, int) and (i == PAIRS - 1 and t > 0 or i == -1 and t == 0)):
                    b = 3 if t == 0 else t - 5
                    pair = i if t == 0 else i + 1
                    seq = v_seq(pair, b)
                    bank = proj[V_SLOT[t] % 2]
                    pe.wait_ge(w_lo[1], pair + 1)
                    positive(pe, proj_lo, seq - 1)
                    for j in range(2):
                        rows = slice(b * S + j * P, b * S + (j + 1) * P)
                        for k in range(KT):
                            last = three(bank[:, j * 256:(j + 1) * 256], xt_hi[:, k, rows], xt_lo[:, k, rows],
                                         wv_hi[:, k, :], wv_lo[:, k, :], k, KT)
                    last.then_inc(proj_ready, 1)

            def weigh(i, t, m, c):
                par, b = c // 4, c % 4
                pair = i - 1 if t == 0 else i
                pe.wait_ge(pt_lo_ready, m + 1)
                pe.wait_ge(proj_lo, v_seq(pair, b) + 1)
                positive(pe, o_stored, m - 1)
                for k in range(2):
                    cols = slice(par * P, (par + 1) * P)
                    last = three(op[c % 2][:, 0:S], v_hi[:, 2 * b + k, cols], v_lo[:, 2 * b + k, cols],
                                 pt_hi[c % 2][:, k, :], pt_lo[c % 2][:, k, :], k, 2)
                last.then_inc(o_ready, 1)

            passes(pe, step, setup)
            weigh(PAIRS, 0, STEPS * PAIRS - 1, 7)

        @block.scalar
        def _(act):
            for u in range(4):
                k, half = u % 2, u // 2
                act.wait_ge(xt_ready, u + 1)
                act.copy(xt_hi[:, k, half * 512:(half + 1) * 512], proj[u % 2][:, :]).then_inc(xt_copied, 1)
            act.wait_ge(bias_turned, 1)
            act.copy(bias[:, :], op[0][:, 0:3 * HEADS]).then_inc(bias_ready, 1)
            act.wait_ge(bias_ready, 1)
            act.wait_ge(setup_act, 1)
            act.activation(mix, mix, ACT.Exp, bias=mix_s[:, 0:1], accum_out=mix_s[:, 1:2]).then_inc(setup_act, 1)

            def setup(t):
                if t == 4:
                    act.wait_ge(setup_pe, 3)
                    act.activation(gates, ptp[0][:, 0, 0:NS_TILES * EXPERTS], ACT.Exp, scale=-1.0)\
                       .then_inc(setup_act, 1)

            def make_high(g, i):
                hi, lo = weight_parts(g, i)
                if g < 3:
                    positive(act, proj_ready, (qk_seq(i, 3), v_seq(i, 3), qk_seq(i, 7))[g] + 1)
                hold(act, w_made[g], i + 2, act_passed)
                act.copy(hi, code[g][:, :]).then_inc(w_hi[g], 1)

            def step(i, t):
                n = STEPS * i + t
                if within(i, t, 5):
                    c = t + 5
                    par, part = (c // 4) % 2, c % 4
                    m, half = part % 2, part // 2
                    head = 2 * (i + c // 8) + par
                    seq = qk_seq(i, c)
                    hold(act, proj_ready, seq + 1, act_passed)
                    act.activation(qk_hi[par][:, m, half * 512:(half + 1) * 512], proj[QK_SLOT[t] % 2][:, :],
                                   ACT.Identity, bias=bias[:, bass.ds(m * HEADS + head, 1)]).then_inc(proj_hi, 1)
                if within(i, t, 0):
                    act.wait_ge(pt_ready, n + 1)
                    positive(act, o_ready, n - 1)
                    act.copy(pt_hi[t % 2][:, :, :], ptp[t % 2][:, :, :]).then_inc(pt_hi_ready, 1)
                if t in V_SLOT and not (isinstance(i, int) and (i == PAIRS - 1 and t > 0 or i == -1 and t == 0)):
                    b = 3 if t == 0 else t - 5
                    pair = i if t == 0 else i + 1
                    act.wait_ge(proj_ready, v_seq(pair, b) + 1)
                    act.copy(v_hi[:, 2 * b:2 * b + 2, :],
                             proj[V_SLOT[t] % 2][:, :].rearrange("p (j f) -> p j f", j=2)).then_inc(proj_hi, 1)
                if within(i, t, 2):
                    k = t % 2
                    act.wait_ge(negmax_ready, n + 3)
                    positive(act, pt_ready, n + 1)
                    for q in range(2):
                        last = act.activation(prob[k][:, q, :], score[k][:, q, :], ACT.Exp,
                                              bias=negmax[k][:, q:q + 1], scale=SCALE,
                                              accum_out=rowsum[k][:, q:q + 1])
                    last.then_inc(exp_done, 1)

            def step_and_weights(i, t):
                first = isinstance(i, int) and i == -1
                if first and t == 3:
                    make_high(0, i)
                step(i, t)
                if first and t < 6:
                    make_high(t - 2, i)
                if not first and t % 2 == 0 and not (isinstance(i, int) and i == PAIRS - 1):
                    make_high(t // 2, i)

            passes(act, step_and_weights, setup)

        @block.vector
        def _(dve):
            for u in range(4):
                k, half = u % 2, u // 2
                dve.wait_ge(xt_copied, u + 1)
                cols = slice(half * 512, (half + 1) * 512)
                dve.tensor_tensor(xt_lo[:, k, cols], proj[u % 2][:, :], xt_hi[:, k, cols].bitcast(F32),
                                  ALU.subtract).then_inc(xt_split, 1)
            dve.wait_ge(bias_ready, 1)
            small = sem("small")
            setup_small = sem("setup_small")
            count = [0]

            def then(ins):
                count[0] += 1
                ins.then_inc(setup_small, 1)
                dve.wait_ge(setup_small, count[0])

            dve.wait_ge(setup_loaded, 80)
            dve.tensor_copy(idx_16f, idx_16).then_inc(idx_float, 1)
            dve.tensor_reduce(mix_s[:, 0:1], mix, AX.X, ALU.max, negate=True).then_inc(setup_act, 1)
            dve.wait_ge(setup_pe, 1)
            then(dve.tensor_copy(idx_f, op[1][:, 0:NS_TILES]))
            then(dve.tensor_copy(idx_i, idx_f))
            dve.tensor_scalar(row_i, idx_i, 8, None, ALU.logical_shift_right)
            then(dve.tensor_scalar(col_i, idx_i, D - 1, 8, ALU.bitwise_and, ALU.logical_shift_left))
            then(dve.tensor_tensor(place_f, col_i, row_i, ALU.add))
            then(dve.tensor_tensor(same, idx_row.rearrange("p (t s) -> p t s", t=NS_TILES),
                                   idx_f.unsqueeze(2).broadcast_to([P, NS_TILES, P]), ALU.is_equal))
            dve.wait_ge(setup_act, 2)
            then(dve.reciprocal(mix_s[:, 2:3], mix_s[:, 1:2]))
            dve.tensor_scalar(mix, mix, mix_s[:, 2:3], None, ALU.mult).then_inc(mix_ready, 1)

            def duplicates_first():
                then(dve.tensor_tensor(earlier, same, before.unsqueeze(1).broadcast_to([P, NS_TILES, P]), ALU.mult))

            def duplicates_second():
                then(dve.tensor_reduce(dup, earlier, AX.X, ALU.max))
                then(dve.tensor_copy(idx_f, spare_i.broadcast_to([P, NS_TILES])))
                then(dve.tensor_tensor(idx_f, idx_f, place_f, ALU.subtract))
                then(dve.tensor_tensor(idx_f, idx_f, dup, ALU.mult))
                then(dve.tensor_tensor(place[:, :], place_f, idx_f, ALU.add))

            def setup(t):
                if t == 3:
                    dve.wait_ge(setup_pe, 2)
                    dve.tensor_copy(mix_t, ptp[1][0:ATOMS, 0, 0:EXPERTS]).then_inc(setup_dve, 1)
                    dve.wait_ge(masks_ready, 3)
                    duplicates_first()
                elif t == 4:
                    dve.wait_ge(setup_act, 3)
                    then(dve.tensor_scalar(gates, gates, 1.0, None, ALU.add))
                    then(dve.reciprocal(gates, gates))
                    duplicates_second()
                elif t == 5:
                    dve.wait_ge(setup_pe, 4)
                    dve.tensor_tensor(scaled, op[0][:, 0:NS_TILES * EXPERTS], gates, ALU.mult)\
                       .then_inc(setup_dve, 1)
                elif t == 7:
                    dve.wait_ge(setup_pe, 5)
                    dve.tensor_copy(summed[:, :], op[1][:, 0:NS_TILES * EXPERTS]).then_inc(setup_dve, 1)

            def store_o(i, t, m, c):
                par, b = c // 4, c % 4
                head = 2 * (i - 1 if t == 0 else i) + par
                dve.wait_ge(o_ready, m + 1)
                dve.tensor_scalar(ot[:, bass.ds(head * T + b * S, S)], op[c % 2][:, 0:S],
                                  bias[:, bass.ds(2 * HEADS + head, 1)], None, ALU.add).then_inc(o_stored, 1)

            def step(i, t):
                n = STEPS * i + t
                if within(i, t, 2):
                    k = t % 2
                    dve.wait_ge(score_ready, n + 3)
                    dve.tensor_reduce(rowmax[k][:, :], score[k][:, :, :], AX.X, ALU.max).then_inc(small, 1)
                    dve.wait_ge(small, n + 3)
                    dve.tensor_scalar(negmax[k][:, :], rowmax[k][:, :], -SCALE, None, ALU.mult)\
                       .then_inc(negmax_ready, 1)
                if within(i, t, 5):
                    c = t + 5
                    par, part = (c // 4) % 2, c % 4
                    m, half = part % 2, part // 2
                    head = 2 * (i + c // 8) + par
                    cols = slice(half * 512, (half + 1) * 512)
                    dve.wait_ge(proj_hi, qk_seq(i, c) + 1)
                    dve.scalar_tensor_tensor(qk_lo[par][:, m, cols], proj[QK_SLOT[t] % 2][:, :],
                                             bias[:, bass.ds(m * HEADS + head, 1)],
                                             qk_hi[par][:, m, cols].bitcast(F32),
                                             ALU.add, ALU.subtract).then_inc(proj_lo, 1)
                if within(i, t, 1):
                    k = (t + 1) % 2
                    dve.wait_ge(exp_done, n + 2)
                    dve.reciprocal(rinv[k][:, :], rowsum[k][:, :]).then_inc(rinv_ready, 1)
                if within(i, t, 0):
                    dve.wait_ge(pt_hi_ready, n + 1)
                    dve.tensor_tensor(pt_lo[t % 2][:, :, :], ptp[t % 2][:, :, :],
                                      pt_hi[t % 2][:, :, :].bitcast(F32), ALU.subtract).then_inc(pt_lo_ready, 1)
                if within(i, t, -1):
                    store_o(i, t, n - 1, (t - 1) % 8)
                if t in V_SLOT and not (isinstance(i, int) and (i == PAIRS - 1 and t > 0 or i == -1 and t == 0)):
                    b = 3 if t == 0 else t - 5
                    pair = i if t == 0 else i + 1
                    dve.wait_ge(proj_hi, v_seq(pair, b) + 1)
                    dve.tensor_tensor(v_lo[:, 2 * b:2 * b + 2, :],
                                      proj[V_SLOT[t] % 2][:, :].rearrange("p (j f) -> p j f", j=2),
                                      v_hi[:, 2 * b:2 * b + 2, :].bitcast(F32), ALU.subtract)\
                       .then_inc(proj_lo, 1)

            def step_and_zeros(i, t):
                if isinstance(i, int) and i == 0 and t == 7:
                    dve.wait_ge(table_zeroed, 16)
                step(i, t)

            passes(dve, step_and_zeros, setup)
            store_o(PAIRS, 0, STEPS * PAIRS - 1, 7)


EPS_LN, EPS_Q, QMAX = 1e-5, 1e-6, 127.0
ROUND = 1.5 * 2.0 ** 23
INNER = 128
TB = S // P
NB = 2
NT = NB * TB
GROUPS = B // NB
HG, RING = 4, 4
UPB = TB * HEADS // HG
WIDE = EXPERTS * D
CHUNKS = 1 + WIDE // 512
CLIP = 50.0

LINKS = [("prep", None, "dve", 1), ("prepd", None, "dve", 1), ("x1", "dve", "dve", 0),
         ("scale", "dve", "dve", 1), ("xq", "dve", "act", 0), ("wq", "dve", "act", 1),
         ("mm1", "act", "dve", 0), ("row1", "dve", "act", 1), ("act", "dve", "dve", 0),
         ("scale2", "dve", "dve", 1), ("q2", "dve", "act", 0), ("mm2", "act", "dve", 1),
         ("row2", "dve", "act", 0), ("x2", "dve", "act", 1), ("gate", "act", "dve", 0)]


def link_tables():
    table, feeds, reads, held = {}, {"dve": 0, "act": 0}, {"dve": 0, "act": 0}, [None, None]
    for k, (name, feeder, reader, half) in enumerate(LINKS):
        if feeder:
            feeds[feeder] += 1
        reads[reader] += 1
        table[name] = dict(number=k, half=half, before=held[half], feeder=feeder,
                           fed=feeds[feeder] if feeder else 0, reader=reader, read=reads[reader])
        held[half] = name
    return table


def unit_of(u):
    b, j, q = u // UPB, u % UPB * TB // UPB, u % (UPB // TB)
    return slice(HG * q, HG * (q + 1)), slice(b * S + j * P, b * S + (j + 1) * P)


def layers(nc, x, bo, guw, dw, gate_w, w_ffn, table, out, kept):
    ident, ot, wo_hi, wo_lo = kept
    links = link_tables()
    with ExitStack() as ctx:
        def sb(name, shape, dt=F32):
            return ctx.enter_context(nc.sbuf_tensor(name, shape, dt))

        def sem(name):
            return ctx.enter_context(nc.semaphore(name))

        o_hi = [sb(f"o_hi{k}", [P, HG, P], F32R) for k in range(RING)]
        o_lo = [sb(f"o_lo{k}", [P, HG, P], F32R) for k in range(RING)]
        bo_row = sb("bo_row", [P, D])
        ones = sb("ones", [P, P])
        half_power = sb("half_power", [P, 8])
        iota8 = sb("iota8", [P, EXPERTS])
        wall_hi = sb("wall_hi", [P, KT, WIDE + D + EXPERTS], F32R)
        wall_lo = sb("wall_lo", [P, KT, WIDE + D + EXPERTS], F32R)
        free = [0]

        def region(cols):
            free[0] += cols
            assert free[0] <= HEADS * T
            return ot[:, free[0] - cols:free[0]]

        raw = [region(WIDE) for k in range(KT)]

        def per_group(name, count, width, dt=F32):
            size = count * width * (2 if dt is BF16 else 4) // 4
            late = [region(size) for g in range(1, GROUPS)]
            late = [(a.bitcast(dt) if dt is not F32 else a).rearrange("p (n d) -> p n d", n=count) for a in late]
            return [sb(name, [P, count, width], dt)[:, :, :]] + late

        def small(name, width, dt=F32):
            return [sb(f"{name}{g}", [P, width], dt)[:, :] for g in range(GROUPS)]

        xb = [sb(f"xb{g}", [P, NT, D])[:, :, :] for g in range(GROUPS)]
        gu_sb = [sb(f"gu_sb{g}", [P, NT, D])[:, :, :] for g in range(GROUPS)]
        dw_sb = [sb(f"dw_sb{g}", [P, NT, INNER])[:, :, :] for g in range(GROUPS)]
        scaled, y1 = per_group("scaled", NT, D), per_group("y1", NT, D)
        x1, x2 = per_group("x1", NT, D), per_group("x2", NT, D)
        diag = per_group("diag", 4 * NB, P)
        xq_t, wq_t = per_group("xq_t", NB * KT, S, BF16), per_group("wq_t", NB * KT, S, BF16)
        row = per_group("row", NB, D)
        hidden = per_group("hidden", NT, 2 * INNER)
        gate, act_sb = per_group("gate", NT, INNER), per_group("act_sb", NT, INNER)
        x2t_hi, x2t_lo = wo_hi[:, 0:NB * KT, :], wo_lo[:, 0:NB * KT, :]
        result = xb
        w_rows, g_rows = hidden[0], row[0][0:EXPERTS, 0, :]
        amax_w, amax_d, amax_x = small("amax_w", NB * KT), small("amax_d", NB), small("amax_x", NB * KT)
        smooth, unsmooth = small("smooth", NB * KT), small("unsmooth", NB * KT)
        x_scale, w_scale, inv = small("x_scale", NT), small("w_scale", NT), small("inv", NT)
        st = sb("st", [P, NT, 6])
        mv = sb("mv", [P, NT, 2])
        base, root = sb("base", [P, 8]), sb("root", [P, 8])
        logit, top = sb("logit", [P, NT, EXPERTS]), sb("top", [P, NT, EXPERTS])
        top_at = sb("top_at", [P, NT, EXPERTS], U32)
        top_f = sb("top_f", [P, NT, 2])
        gap, share = sb("gap", [P, NT]), sb("share", [P, NT, 2])
        weight = [sb(f"weight{g}", [P, NT, EXPERTS]) for g in range(GROUPS)]
        second = sb("second", [P, NT, EXPERTS])

        banks = [ctx.enter_context(nc.psum_tensor(f"banks{g}", [P, 4, 512], F32)) for g in range(GROUPS)]

        w_in, bo_in = sem("w_in"), sem("bo_in")
        x_in, q_in = [sem(f"x_in{g}") for g in range(GROUPS)], [sem(f"q_in{g}") for g in range(GROUPS)]
        raw_in = [sem(f"raw_in{k}") for k in range(KT)]
        wt_ready, wt_used = sem("wt_ready"), sem("wt_used")
        consts = sem("consts")
        wall_hi_ready, wall_ready = sem("wall_hi_ready"), sem("wall_ready")
        o_hi_ready, o_used = sem("o_hi_ready"), sem("o_used")
        o_lo_pool, o_lo_dve = sem("o_lo_pool"), sem("o_lo_dve")
        xb_ready = sem("xb_ready")
        link_ready = [sem(f"link_ready{g}") for g in range(GROUPS)]
        link_fed = [{e: sem(f"fed_by_{e}{g}") for e in ("dve", "act")} for g in range(GROUPS)]
        link_read = [{e: sem(f"read_by_{e}{g}") for e in ("dve", "act")} for g in range(GROUPS)]
        exp_in, exp_out = sem("exp_in"), sem("exp_out")
        pow_in, pow_out = sem("pow_in"), sem("pow_out")
        x2t_hi_ready, x2t_ready = sem("x2t_hi_ready"), sem("x2t_ready")
        f_ready = [sem(f"f_ready{g}") for g in range(GROUPS)]
        f_used = [sem(f"f_used{g}") for g in range(GROUPS)]
        result_ready = sem("result_ready")
        stored = [sem(f"stored{g}") for g in range(GROUPS)]
        chain = sem("chain")

        def low_by_dve(u):
            return u < NB * UPB and u % 2 == 1

        def low_count(u):
            return sum(low_by_dve(v) == low_by_dve(u) for v in range(u + 1))

        def low_part(eng, u, ready):
            heads, rows = unit_of(u)
            eng.wait_ge(o_hi_ready, u + 1)
            eng.tensor_tensor(o_lo[u % RING][:, :, :], ot_view[:, heads, rows],
                              o_hi[u % RING][:, :, :].bitcast(F32), ALU.subtract).then_inc(ready, 1)

        ot_view = ot[:, :].rearrange("p (h t) -> p h t", h=HEADS)

        def half_of(g, name):
            h = links[name]["half"]
            return banks[g][:, 2 * h:2 * h + 2, :].rearrange("p k n -> p (k n)")

        def flat(a):
            return a.rearrange("p n d -> p (n d)")

        GIVEN = [NB * UPB + n for n in (5, 8, 12, 14)]

        block = ctx.enter_context(nc.Block())

        @block.sync
        def _(sp):
            def load(g):
                bs = slice(NB * g, NB * (g + 1))
                sp.dma_start(gu_sb[g], guw[bs].rearrange("b (j p) d -> p (b j) d", p=P)).then_inc(q_in[g], 16)
                sp.dma_start(dw_sb[g], dw[bs].rearrange("b (j p) d -> p (b j) d", p=P)).then_inc(q_in[g], 16)
                sp.dma_start(xb[g], x[bs].rearrange("b (j p) d -> p (b j) d", p=P)).then_inc(x_in[g], 16)

            sp.dma_start(w_rows[:, 0:TB, :], w_ffn.rearrange("(j p) d -> p j d", p=P)).then_inc(w_in, 16)
            sp.dma_start(g_rows, gate_w).then_inc(w_in, 16)
            load(0)
            sp.dma_start(bo_row[:, :], bo.rearrange("(a n) -> a n", a=1).broadcast_to([P, D])).then_inc(bo_in, 16)
            for g in range(1, GROUPS):
                load(g)
            rows = table[0:D * D, :].rearrange("(k p r) e -> k p (r e)", k=KT, p=P)
            sp.wait_ge(o_used, B * UPB)
            for k in range(KT):
                sp.dma_start(raw[k], rows[k]).then_inc(raw_in[k], 16)
            for g in range(GROUPS):
                for n in range(NT):
                    sp.wait_ge(result_ready, NT * g + n + 1)
                    b, j = NB * g + n // TB, n % TB
                    sp.dma_start(out[b, j * P:(j + 1) * P, :], result[g][:, n, :]).then_inc(stored[g], 16)
            for g in range(GROUPS):
                sp.wait_ge(stored[g], 16 * NT)

        @block.gpsimd
        def _(pool):
            pool.memset(ones[:, :], 1.0).then_inc(consts, 1)
            pool.memset(half_power[:, 0:4], -0.5).then_inc(consts, 1)
            pool.memset(half_power[:, 4:8], 0.5).then_inc(consts, 1)
            pool.iota(iota8[:, :], pattern=[[1, EXPERTS]], base=0, channel_multiplier=0,
                      allow_small_or_imprecise_dtypes=True).then_inc(consts, 1)
            pool.wait_ge(consts, 4)
            powers = [0]

            def power(width, sign):
                powers[0] += 1
                pool.wait_ge(pow_in, powers[0])
                e = half_power[:, 4:4 + width] if sign > 0 else half_power[:, 0:width]
                pool.tensor_tensor(root[:, 0:width], base[:, 0:width], e, ALU.pow).then_inc(pow_out, 1)

            def low_parts(first, last):
                for u in range(first, last):
                    if not low_by_dve(u):
                        low_part(pool, u, o_lo_pool)

            def add_bias(g):
                pool.wait_ge(x_in[g], 16)
                pool.tensor_tensor(xb[g], xb[g], bo_row[:, :].unsqueeze(1).broadcast_to([P, NT, D]), ALU.add)\
                    .then_inc(xb_ready, 1)

            def experts_low(k):
                pool.wait_ge(wall_hi_ready, KT + k + 1)
                pool.tensor_tensor(wall_lo[:, k, 0:WIDE].rearrange("p (e r) -> p e r", e=EXPERTS),
                                   raw[k].rearrange("p (r e) -> p e r", e=EXPERTS),
                                   wall_hi[:, k, 0:WIDE].bitcast(F32).rearrange("p (e r) -> p e r", e=EXPERTS),
                                   ALU.subtract).then_inc(wall_ready, 1)

            low_parts(0, UPB)
            pool.wait_ge(bo_in, 16)
            add_bias(0)
            low_parts(UPB, GIVEN[0])
            power(NT, -1)
            low_parts(GIVEN[0], GIVEN[1])
            power(NB * KT, 1)
            low_parts(GIVEN[1], B * UPB)
            add_bias(1)
            power(NT, -1)
            power(NB * KT, 1)
            power(NB, 1)
            experts_low(0)
            power(NT, -1)
            experts_low(1)
            power(NB, 1)
            power(NT, -1)
            for g in range(GROUPS):
                power(NT, -1)

        @block.tensor
        def _(pe):
            def three(out, lh, ll, rh, rl, k, n):
                pe.matmul(out, lh, rh, start=(k == 0), stop=False)
                pe.matmul(out, lh, rl, start=False, stop=False)
                return pe.matmul(out, ll, rh, start=False, stop=(k == n - 1))

            def link(g, name):
                this = links[name]
                if this["feeder"]:
                    pe.wait_ge(link_fed[g][this["feeder"]], this["fed"])
                if this["before"]:
                    before = links[this["before"]]
                    pe.wait_ge(link_read[g][before["reader"]], before["read"])
                return half_of(g, name)

            def turn_rows(bank, src, width=D):
                for b in range(NB):
                    for k in range(width // P):
                        for j in range(TB):
                            at = (b * (width // P) + k) * S + j * P
                            last = pe.transpose(bank[:, at:at + P], src[:, b * TB + j, k * P:(k + 1) * P],
                                                ident[:, :])
                return last

            def spread(bank, diag, cols):
                for n, c in enumerate(cols):
                    last = pe.matmul(bank[:, n * P:(n + 1) * P], ones[:, :], diag[:, c, :], start=True, stop=True)
                return last

            def project(first, last_unit):
                for u in range(first, last_unit):
                    heads, rows = unit_of(u)
                    pe.wait_ge(o_lo_dve if low_by_dve(u) else o_lo_pool, low_count(u))
                    b, j = u // UPB, u % UPB * TB // UPB
                    for k, h in enumerate(range(heads.start, heads.stop)):
                        last = three(banks[b // NB][:, b % NB, j * D:(j + 1) * D], o_hi[u % RING][:, k, :], o_lo[u % RING][:, k, :],
                                     wo_hi[:, h, :], wo_lo[:, h, :], h, HEADS)
                    last.then_inc(o_used, 1)

            def made(g, ins):
                ins.then_inc(link_ready[g], 1)

            def prepare(g):
                pe.wait_ge(q_in[g], 32)
                made(g, turn_rows(link(g, "prep"), gu_sb[g]))

            def prepare_second(g):
                made(g, turn_rows(link(g, "prepd"), dw_sb[g], INNER))

            def turn_x1(g):
                made(g, turn_rows(link(g, "x1"), x1[g]))

            def spread_scales(g):
                made(g, spread(link(g, "scale"), diag[g], range(4 * NB)))

            def turn_xq(g):
                made(g, turn_rows(link(g, "xq"), scaled[g]))

            def turn_wq(g):
                made(g, turn_rows(link(g, "wq"), hidden[g]))

            def first_layer(g):
                bank = link(g, "mm1")
                for n in range(NT):
                    b, j = n // TB, n % TB
                    for k in range(KT):
                        last = pe.matmul(bank[:, n * S:(n + 1) * S], xq_t[g][:, b * KT + k, j * P:(j + 1) * P],
                                         wq_t[g][:, b * KT + k, :], start=(k == 0), stop=(k == KT - 1))
                made(g, last)
                made(g, spread(link(g, "row1"), diag[g], range(NT)))

            def turn_act(g):
                made(g, turn_rows(link(g, "act"), act_sb[g], INNER))

            def spread_second(g):
                made(g, spread(link(g, "scale2"), diag[g], range(NT, NT + 2 * NB)))

            def turn_q2(g):
                bank = link(g, "q2")
                turn_rows(bank[:, 0:NB * S], act_sb[g], INNER)
                made(g, turn_rows(bank[:, NB * S:2 * NB * S], gate[g], INNER))

            def second_layer(g):
                bank = link(g, "mm2")
                for n in range(NT):
                    b, j = n // TB, n % TB
                    last = pe.matmul(bank[:, n * D:(n + 1) * D], xq_t[g][:, b, j * P:(j + 1) * P],
                                     wq_t[g][:, b, :], start=True, stop=True)
                made(g, last)
                made(g, spread(link(g, "row2"), diag[g], range(NT)))

            def turn_x2(g):
                made(g, turn_rows(link(g, "x2"), x2[g]))

            def route(g):
                bank = link(g, "gate")
                pe.wait_ge(x2t_ready, g + 1)
                for n in range(NT):
                    b, rows = n // TB, slice(n % TB * P, (n % TB + 1) * P)
                    for k in range(KT):
                        last = three(bank[:, n * EXPERTS:(n + 1) * EXPERTS], x2t_hi[:, b * KT + k, rows],
                                     x2t_lo[:, b * KT + k, rows], wall_hi[:, k, WIDE + D:], wall_lo[:, k, WIDE + D:],
                                     k, KT)
                made(g, last)

            def experts(g, first, last_chunk):
                for f in range(first, last_chunk):
                    n, c = f // CHUNKS, f % CHUNKS
                    b, rows = n // TB, slice(n % TB * P, (n % TB + 1) * P)
                    if f == 2:
                        pe.wait_ge(link_read[g]["dve"], links["gate"]["read"])
                    if f == 0:
                        pe.wait_ge(wall_ready, KT)
                    if f >= 4:
                        pe.wait_ge(f_used[g], f - 3)
                    cols = slice(WIDE, WIDE + D) if c == 0 else slice((c - 1) * 512, c * 512)
                    for k in range(KT):
                        last = three(banks[g][:, (f + 2) % 4, 0:cols.stop - cols.start], x2t_hi[:, b * KT + k, rows],
                                     x2t_lo[:, b * KT + k, rows], wall_hi[:, k, cols], wall_lo[:, k, cols], k, KT)
                    last.then_inc(f_ready[g], 1)

            pe.wait_ge(w_in, 32)
            for k in range(KT):
                for j in range(TB):
                    pe.transpose(banks[1][:, 2 + k, j * P:(j + 1) * P], w_rows[:, j, k * P:(k + 1) * P], ident[:, :])
                last = pe.transpose(banks[1][:, 2 + k, D:D + EXPERTS], g_rows[:, k * P:(k + 1) * P],
                                    ident[0:EXPERTS, 0:EXPERTS])
            last.then_inc(wt_ready, 1)
            prepare(0)
            pe.wait_ge(consts, 4)
            project(0, 6)
            prepare_second(0)
            project(6, GIVEN[0])
            turn_x1(0)
            pe.wait_ge(wt_used, 1)
            prepare(1)
            project(GIVEN[0], GIVEN[1])
            spread_scales(0)
            prepare_second(1)
            project(GIVEN[1], GIVEN[2])
            turn_xq(0)
            project(GIVEN[2], GIVEN[3])
            turn_wq(0)
            project(GIVEN[3], B * UPB)
            first_layer(0)
            turn_x1(1)
            turn_act(0)
            spread_scales(1)
            spread_second(0)
            turn_xq(1)
            turn_q2(0)
            second_layer(0)
            turn_wq(1)
            first_layer(1)
            turn_x2(0)
            turn_act(1)
            route(0)
            experts(0, 0, 4)
            spread_second(1)
            experts(0, 4, 8)
            turn_q2(1)
            experts(0, 8, 10)
            second_layer(1)
            experts(0, 10, 14)
            experts(0, 14, NT * CHUNKS)
            turn_x2(1)
            route(1)
            experts(1, 0, NT * CHUNKS)

        @block.scalar
        def _(act):
            def high_parts(first, last):
                for u in range(first, last):
                    heads, rows = unit_of(u)
                    if u >= RING:
                        act.wait_ge(o_used, u - RING + 1)
                    act.copy(o_hi[u % RING][:, :, :], ot_view[:, heads, rows]).then_inc(o_hi_ready, 1)

            def arrived(g, name):
                act.wait_ge(link_ready[g], links[name]["number"] + 1)
                return half_of(g, name)

            def row_of(g, name):
                act.copy(flat(row[g]), arrived(g, name)[:, 0:NB * D]).then_inc(link_read[g]["act"], 1)

            def unround(dst, src):
                return act.activation(dst, src, ACT.Copy, bias=-ROUND)

            exps = [0]

            def exponential(dst, src, scale=1.0):
                exps[0] += 1
                act.wait_ge(exp_in, exps[0])
                act.activation(dst, src, ACT.Exp, scale=scale).then_inc(exp_out, 1)

            def fed_operands(g, name):
                act.wait_ge(link_read[g]["act"], links[name]["read"])
                act.sem_inc(link_fed[g]["act"], 1)

            def rows_operand(g):
                unround(flat(xq_t[g]), arrived(g, "xq")).then_inc(link_read[g]["act"], 1)

            def weights_operand(g):
                unround(flat(wq_t[g]), arrived(g, "wq")).then_inc(link_read[g]["act"], 1)
                fed_operands(g, "wq")

            def hidden_row(g):
                row_of(g, "row1")
                exponential(gate[g], hidden[g][:, :, 0:INNER], -1.0)

            def second_operands(g):
                bank = arrived(g, "q2")
                unround(flat(xq_t[g][:, 0:NB, :]), bank[:, 0:NB * S])
                unround(flat(wq_t[g][:, 0:NB, :]), bank[:, NB * S:2 * NB * S]).then_inc(link_read[g]["act"], 1)
                fed_operands(g, "q2")

            def split_x2(g):
                bank = arrived(g, "x2")
                if g:
                    act.wait_ge(f_ready[g - 1], NT * CHUNKS)
                act.copy(flat(x2t_hi[:, :, :]), bank).then_inc(x2t_hi_ready, 1)
                act.wait_ge(x2t_ready, g + 1)
                act.sem_inc(link_read[g]["act"], 1)
                act.sem_inc(link_fed[g]["act"], 1)
                exponential(gap[:, :], gap[:, :])

            def experts_high(k):
                act.wait_ge(raw_in[k], 16)
                act.copy(wall_hi[:, k, 0:WIDE].rearrange("p (e r) -> p e r", e=EXPERTS),
                         raw[k].rearrange("p (r e) -> p e r", e=EXPERTS)).then_inc(wall_hi_ready, 1)

            high_parts(0, RING)
            act.wait_ge(wt_ready, 1)
            for k in range(KT):
                act.copy(wall_hi[:, k, WIDE:], banks[1][:, 2 + k, 0:D + EXPERTS]).then_inc(wall_hi_ready, 1)
            high_parts(RING, GIVEN[2] + RING)
            rows_operand(0)
            high_parts(GIVEN[2] + RING, min(GIVEN[3] + RING, B * UPB))
            weights_operand(0)
            high_parts(min(GIVEN[3] + RING, B * UPB), B * UPB)
            hidden_row(0)
            experts_high(0)
            rows_operand(1)
            second_operands(0)
            row_of(0, "row2")
            weights_operand(1)
            experts_high(1)
            hidden_row(1)
            split_x2(0)
            second_operands(1)
            row_of(1, "row2")
            split_x2(1)

        @block.vector
        def _(dve):
            count = [0]

            def then(ins):
                count[0] += 1
                ins.then_inc(chain, 1)
                dve.wait_ge(chain, count[0])

            exps, powers = [0], [0]

            def arrived(g, name):
                dve.wait_ge(link_ready[g], links[name]["number"] + 1)
                return half_of(g, name)

            def was_read(g, name, ins):
                ins.then_inc(link_read[g]["dve"], 1)
                dve.wait_ge(link_read[g]["dve"], links[name]["read"])

            def feed(g, ins):
                ins.then_inc(link_fed[g]["dve"], 1)

            def fed_now(g, name):
                dve.wait_ge(link_fed[g]["dve"], links[name]["fed"])

            def exponential(ins):
                exps[0] += 1
                ins.then_inc(exp_in, 1)

            def exp_made():
                dve.wait_ge(exp_out, exps[0])

            def power(ins):
                powers[0] += 1
                ins.then_inc(pow_in, 1)
                dve.wait_ge(pow_out, powers[0])

            def normalise(src, dst):
                for n in range(NT):
                    ins = dve.bn_stats(st[:, n, :], src[:, n, :])
                then(ins)
                for n in range(NT):
                    ins = dve.bn_aggr(mv[:, n, :], st[:, n, :])
                then(ins)
                power(dve.tensor_scalar(base[:, 0:NT], mv[:, :, 1], EPS_LN, None, ALU.add))
                for n in range(NT):
                    yield dve.tensor_scalar(dst[:, n, :], src[:, n, :], mv[:, n, 0:1], root[:, n:n + 1],
                                            ALU.subtract, ALU.mult)

            def quantise(g, src, scales):
                then(dve.tensor_reduce(scales, src, AX.X, ALU.max, apply_absolute_value=True))
                then(dve.tensor_scalar(scales, scales, EPS_Q, 1.0 / QMAX, ALU.max, ALU.mult))
                then(dve.reciprocal(inv[g], scales))
                for n in range(NT):
                    ins = dve.tensor_scalar(src[:, n, :], src[:, n, :], inv[g][:, n:n + 1], ROUND,
                                            ALU.mult, ALU.add)
                then(ins)
                return dve.tensor_scalar(src, src, ROUND + QMAX, ROUND - QMAX, ALU.min, ALU.max)

            def balance(g, amax_weight, n):
                s, u = smooth[g][:, 0:n], unsmooth[g][:, 0:n]
                then(dve.tensor_scalar(s, amax_weight, EPS_Q, None, ALU.max))
                then(dve.reciprocal(s, s))
                power(dve.scalar_tensor_tensor(base[:, 0:n], amax_x[g][:, 0:n], EPS_Q, s, ALU.max, ALU.mult))
                then(dve.tensor_scalar(s, root[:, 0:n], EPS_Q, None, ALU.max))
                then(dve.reciprocal(u, s))
                return s, u

            def diagonal(g, at, values, n):
                return dve.tensor_tensor(diag[g][:, at:at + n, :],
                                         ident[:, :].unsqueeze(1).broadcast_to([P, n, P]),
                                         values.unsqueeze(2).broadcast_to([P, n, P]), ALU.mult)

            def largest(dst, src, n):
                return dve.tensor_reduce(dst, src.rearrange("p (n t) -> p n t", n=n), AX.X, ALU.max,
                                         apply_absolute_value=True)

            def prepare(g):
                was_read(g, "prep", largest(amax_w[g], arrived(g, "prep"), NB * KT))

            def prepare_second(g):
                was_read(g, "prepd", largest(amax_d[g], arrived(g, "prepd")[:, 0:NB * S], NB))

            def wide(a, n):
                return a.rearrange("p (b n) -> p b n", b=NB).unsqueeze(2).broadcast_to([P, NB, TB, n])

            def tiles(a):
                return a.rearrange("p (b j) d -> p b j d", b=NB)

            def start(g):
                dve.wait_ge(xb_ready, g + 1)
                dve.wait_ge(o_used, NB * UPB * (g + 1))
                y = banks[g][:, 0:NB, :].rearrange("p b (j d) -> p (b j) d", j=TB)
                then(dve.tensor_tensor(y1[g], y, xb[g], ALU.add))
                for n, ins in enumerate(normalise(y1[g], x1[g])):
                    if n == NT - 1:
                        feed(g, ins)
                fed_now(g, "x1")

            def balance_first(g):
                was_read(g, "x1", largest(amax_x[g], arrived(g, "x1"), NB * KT))
                s, u = balance(g, amax_w[g], NB * KT)
                diagonal(g, 0, u, NB * KT)
                feed(g, diagonal(g, NB * KT, s, NB * KT))

            def quantise_rows(g):
                bank = arrived(g, "scale")
                then(dve.tensor_tensor(tiles(scaled[g]), tiles(x1[g]), wide(bank[:, 0:NB * D], D), ALU.mult))
                feed(g, quantise(g, scaled[g], x_scale[g]))

            def quantise_weights(g):
                bank = half_of(g, "scale")
                was_read(g, "scale", dve.tensor_tensor(tiles(hidden[g]), tiles(gu_sb[g]),
                                                       wide(bank[:, NB * D:2 * NB * D], D), ALU.mult))
                feed(g, quantise(g, hidden[g], w_scale[g]))
                feed(g, diagonal(g, 0, w_scale[g], NT))

            def dequantise(g, name, row_name, dst):
                bank = arrived(g, name)
                dve.wait_ge(link_read[g]["act"], links[row_name]["read"])
                for n in range(NT):
                    ins = dve.scalar_tensor_tensor(dst[:, n, :], bank[:, n * D:(n + 1) * D],
                                                   x_scale[g][:, n:n + 1], row[g][:, n // TB, :], ALU.mult, ALU.mult)
                was_read(g, name, ins)

            def first_layer(g):
                dequantise(g, "mm1", "row1", hidden[g])
                dve.sem_inc(exp_in, 1)
                exps[0] += 1
                then(dve.tensor_tensor(act_sb[g], hidden[g][:, :, 0:INNER], hidden[g][:, :, INNER:], ALU.mult))

            def activate(g):
                exp_made()
                then(dve.tensor_scalar(gate[g], gate[g], 1.0, None, ALU.add))
                then(dve.reciprocal(gate[g], gate[g]))
                feed(g, dve.tensor_tensor(act_sb[g], act_sb[g], gate[g], ALU.mult))
                fed_now(g, "act")

            def balance_second(g):
                was_read(g, "act", largest(amax_x[g][:, 0:NB], arrived(g, "act")[:, 0:NB * S], NB))
                s, u = balance(g, amax_d[g], NB)
                diagonal(g, NT, u, NB)
                feed(g, diagonal(g, NT + NB, s, NB))

            def quantise_second(g):
                bank = arrived(g, "scale2")
                then(dve.tensor_tensor(tiles(act_sb[g]), tiles(act_sb[g]), wide(bank[:, 0:NB * P], P), ALU.mult))
                was_read(g, "scale2", dve.tensor_tensor(tiles(gate[g]), tiles(dw_sb[g]),
                                                        wide(bank[:, NB * P:2 * NB * P], P), ALU.mult))
                then(quantise(g, act_sb[g], x_scale[g]))
                feed(g, quantise(g, gate[g], w_scale[g]))
                feed(g, diagonal(g, 0, w_scale[g], NT))

            def second_layer(g):
                dequantise(g, "mm2", "row2", y1[g])
                then(dve.tensor_tensor(y1[g], y1[g], x1[g], ALU.add))
                for n, ins in enumerate(normalise(y1[g], x2[g])):
                    if n == NT - 1:
                        feed(g, ins)
                fed_now(g, "x2")

            def split_x2(g):
                bank = arrived(g, "x2")
                dve.wait_ge(x2t_hi_ready, g + 1)
                dve.tensor_tensor(flat(x2t_lo[:, :, :]), bank, flat(x2t_hi[:, :, :]).bitcast(F32),
                                  ALU.subtract).then_inc(x2t_ready, 1)

            def route(g):
                bank = arrived(g, "gate")
                was_read(g, "gate", dve.tensor_scalar(flat(logit[:, :, :]), bank[:, 0:NT * EXPERTS],
                                                      CLIP, -CLIP, ALU.min, ALU.max))
                for n in range(NT):
                    ins = dve.max(top[:, n, :], logit[:, n, :])
                then(ins)
                exponential(dve.tensor_tensor(gap[:, :], top[:, :, 1], top[:, :, 0], ALU.subtract))
                for n in range(NT):
                    ins = dve.max_index(top_at[:, n, :], top[:, n, :], logit[:, n, :])
                then(ins)
                then(dve.tensor_copy(top_f[:, :, :], top_at[:, :, 0:2]))
                exp_made()
                then(dve.tensor_scalar(share[:, :, 0], gap[:, :], 1.0, None, ALU.add))
                then(dve.reciprocal(share[:, :, 0], share[:, :, 0]))
                then(dve.tensor_tensor(share[:, :, 1], gap[:, :], share[:, :, 0], ALU.mult))
                for k, dst in enumerate((weight[g], second)):
                    every = iota8[:, :].unsqueeze(1).broadcast_to([P, NT, EXPERTS])
                    then(dve.tensor_tensor(dst[:, :, :], every,
                                           top_f[:, :, k:k + 1].broadcast_to([P, NT, EXPERTS]), ALU.is_equal))
                    then(dve.tensor_tensor(dst[:, :, :], dst[:, :, :],
                                           share[:, :, k:k + 1].broadcast_to([P, NT, EXPERTS]), ALU.mult))
                then(dve.tensor_tensor(weight[g][:, :, :], weight[g][:, :, :], second[:, :, :], ALU.add))

            def mix(g, first, last):
                for f in range(first, last):
                    n, c = f // CHUNKS, f % CHUNKS
                    dst, bank = x2[g][:, n, :], banks[g][:, (f + 2) % 4, :]
                    dve.wait_ge(f_ready[g], f + 1)
                    if c == 0:
                        ins = dve.tensor_tensor(dst, bank[:, 0:D], dst, ALU.add)
                    else:
                        for h in range(2):
                            e = 2 * (c - 1) + h
                            ins = dve.scalar_tensor_tensor(dst, bank[:, h * D:(h + 1) * D],
                                                           weight[g][:, n, e:e + 1], dst, ALU.mult, ALU.add)
                            if h == 0:
                                then(ins)
                    ins.then_inc(f_used[g], 1)
                    dve.wait_ge(f_used[g], f + 1)

            def finish(g):
                for ins in normalise(x2[g], result[g]):
                    ins.then_inc(result_ready, 1)

            def low_parts(first, last):
                for u in range(first, last):
                    if low_by_dve(u):
                        low_part(dve, u, o_lo_dve)

            low_parts(0, 2)
            for k in range(KT):
                dve.wait_ge(wall_hi_ready, k + 1)
                ins = dve.tensor_tensor(wall_lo[:, k, WIDE:], banks[1][:, 2 + k, 0:D + EXPERTS],
                                        wall_hi[:, k, WIDE:].bitcast(F32), ALU.subtract)
            ins.then_inc(wt_used, 1)
            low_parts(2, 4)
            prepare(0)
            low_parts(4, 10)
            prepare_second(0)
            low_parts(10, NB * UPB)
            start(0)
            balance_first(0)
            prepare(1)
            prepare_second(1)
            quantise_rows(0)
            quantise_weights(0)
            first_layer(0)
            start(1)
            activate(0)
            balance_first(1)
            balance_second(0)
            quantise_rows(1)
            quantise_second(0)
            quantise_weights(1)
            second_layer(0)
            first_layer(1)
            split_x2(0)
            activate(1)
            route(0)
            balance_second(1)
            mix(0, 0, 4)
            quantise_second(1)
            mix(0, 4, 10)
            second_layer(1)
            mix(0, 10, NT * CHUNKS)
            split_x2(1)
            finish(0)
            route(1)
            mix(1, 0, NT * CHUNKS)
            finish(1)


def program(nc, inputs, out):
    a = inputs
    table = nc.dram_tensor("table", (TABLE_ROWS, EXPERTS), F32, kind="Internal").ap()
    with ExitStack() as ctx:
        def sb(name, shape, dt=F32):
            return ctx.enter_context(nc.sbuf_tensor(name, shape, dt))

        kept = (sb("ident", [P, P]), sb("ot", [P, HEADS * T]), sb("wo_hi", [P, HEADS, D], F32R),
                sb("wo_lo", [P, HEADS, D], F32R))
        w = [a[f"L0_attn_w{m}_{part}"] for m in "qkvo" for part in ("codes", "scales")]
        attention(nc, a["x"], w, [a[f"L0_attn_b{m}"] for m in "qkv"],
                  [a["L0_ffn_mask_idx"], a["L0_ffn_importance"], a["L0_ffn_atoms"],
                   a["L0_ffn_expert_atom_weights"], table], kept)
        layers(nc, a["x"], a["L0_attn_bo"], a["fside_BxS2xS2_0"], a["ctx_1024"], a["L0_ffn_gate_w"],
               a["L0_ffn_W"], table, out, kept)


_INS = ["x", "fside_BxS2xS2_0", "ctx_1024",
        "L0_attn_wq_codes", "L0_attn_wq_scales", "L0_attn_bq", "L0_attn_wk_codes", "L0_attn_wk_scales",
        "L0_attn_bk", "L0_attn_wv_codes", "L0_attn_wv_scales", "L0_attn_bv", "L0_attn_wo_codes",
        "L0_attn_wo_scales", "L0_attn_bo", "L0_ffn_gate_w", "L0_ffn_W", "L0_ffn_atoms",
        "L0_ffn_expert_atom_weights", "L0_ffn_importance", "L0_ffn_mask_idx"]


def kernel(**inputs):
    import numpy as np
    import concourse.bacc as bacc
    from concourse.bass_utils import run_bass_kernel_spmd

    nc = bacc.Bacc("TRN2", target_bir_lowering=False, num_devices=1)
    arrays, args = {}, {}
    for name in _INS:
        a = np.ascontiguousarray(inputs[name])
        arrays["in_" + name] = a
        args[name] = nc.dram_tensor("in_" + name, a.shape, mybir.dt.from_np(a.dtype), kind="ExternalInput").ap()
    out = nc.dram_tensor("out_0", (B, S, D), F32, kind="ExternalOutput").ap()
    program(nc, args, out)
    r = run_bass_kernel_spmd(nc, [arrays], core_ids=[0])
    return r.results[0]["out_0"]
```

```python
from contextlib import ExitStack

import concourse.bass as bass
from concourse import mybir

F32 = mybir.dt.float32
F32R = mybir.dt.float32r
ALU = mybir.AluOpType
ACT = mybir.ActivationFunctionType
AX = mybir.AxisListType
P = 128

B, S, D = 4, 256, 256
HEADS, HD, BLK = 16, 128, 32
T = B * S
TILES = T // P
KT = D // P
PAIRS = HEADS // 2
STEPS = 2 * B
SCALE = float(HD) ** -0.5
I32, U32, BF16 = mybir.dt.int32, mybir.dt.uint32, mybir.dt.bfloat16
EXPERTS, ATOMS, NS = 8, 64, 2048
NS_TILES = NS // P
TABLE_ROWS = D * D + P
SETUP_DONE = 3

QK_SLOT = [0, 2, 3, 4, 5, 6, 8, 10]
V_SLOT = {0: 1, 5: 7, 6: 9, 7: 11}
UNITS = 12


def qk_seq(i, c):
    return (i + (c - 5) // 8) * UNITS + 8 + QK_SLOT[(c - 5) % 8]


def v_seq(i, b):
    return i * UNITS + 8 + V_SLOT[0] if b == 3 else (i - 1) * UNITS + 8 + V_SLOT[5 + b]


def positive(eng, sem, value):
    if not isinstance(value, int) or value > 0:
        eng.wait_ge(sem, value)


def hold(eng, sem, value, passed):
    eng.wait_ge(sem, value)
    if not isinstance(value, int):
        eng.sem_inc(passed, 1)


def attention(nc, x, w, bias_rows, moe, kept):
    with ExitStack() as ctx:
        def sb(name, shape, dt=F32):
            return ctx.enter_context(nc.sbuf_tensor(name, shape, dt))

        def ps(name, shape, dt=F32):
            return ctx.enter_context(nc.psum_tensor(name, shape, dt))

        def sem(name):
            return ctx.enter_context(nc.semaphore(name))

        ident, ot, wo_hi, wo_lo = kept
        xt_hi = sb("xt_hi", [P, KT, T], F32R)
        xt_lo = sb("xt_lo", [P, KT, T], F32R)
        bias = sb("bias", [P, 3 * HEADS])
        code = [sb(f"code{g}", [P, 512]) for g in range(4)]
        scal = [sb(f"scal{g}", [P, 512]) for g in range(4)]
        wqk_hi = [sb(f"wqk_hi{p}", [P, 2, KT, P], F32R) for p in range(2)]
        wqk_lo = [sb(f"wqk_lo{p}", [P, 2, KT, P], F32R) for p in range(2)]
        wv_hi = sb("wv_hi", [P, KT, 256], F32R)
        wv_lo = sb("wv_lo", [P, KT, 256], F32R)
        qk_hi = [sb(f"qk_hi{p}", [P, 2, T], F32R) for p in range(2)]
        qk_lo = [sb(f"qk_lo{p}", [P, 2, T], F32R) for p in range(2)]
        v_hi = sb("v_hi", [P, TILES, 256], F32R)
        v_lo = sb("v_lo", [P, TILES, 256], F32R)
        prob = [sb(f"prob{p}", [P, 2, S]) for p in range(2)]
        pt_hi = [sb(f"pt_hi{p}", [P, 2, S], F32R) for p in range(2)]
        pt_lo = [sb(f"pt_lo{p}", [P, 2, S], F32R) for p in range(2)]
        xrow = ot[:, 0:TILES * D].rearrange("p (t d) -> p t d", t=TILES)
        brow = ot[0:3 * HEADS, TILES * D:TILES * D + P]
        idx, importance, atoms, expert_atoms, table = moe
        taken = [TILES * D + P]

        def region(cols, dt=F32):
            taken[0] += cols
            assert taken[0] <= HEADS * T
            cols_of_ot = ot[:, taken[0] - cols:taken[0]]
            return cols_of_ot if dt is F32 else cols_of_ot.bitcast(dt)

        zeros = region(TABLE_ROWS * EXPERTS // P)
        idx_row = region(NS, I32)
        same = region(NS).rearrange("p (t s) -> p t s", t=NS_TILES)
        earlier = region(NS).rearrange("p (t s) -> p t s", t=NS_TILES)
        atoms_imp = region(NS)
        atoms_sb, imp_sb = atoms_imp[0:ATOMS, :], atoms_imp[96:96 + EXPERTS, :]
        before = region(P)
        idx_16 = region(P, I32)[0:NS_TILES, :]
        idx_16f = region(P)[0:NS_TILES, :]
        mix = region(ATOMS)[0:EXPERTS, :]
        mix_t = region(EXPERTS)[0:ATOMS, :]
        mix_s = region(4)[0:EXPERTS, :]
        idx_f = region(NS_TILES)
        idx_i = region(NS_TILES, I32)
        col_i = region(NS_TILES, I32)
        row_i = region(NS_TILES, I32)
        dup = region(NS_TILES)
        place_f = region(NS_TILES)
        spare_i = region(1, I32)
        gates = region(NS_TILES * EXPERTS)
        scaled = region(NS_TILES * EXPERTS)
        summed = sb("summed", [P, NS_TILES * EXPERTS])
        place = sb("place", [P, NS_TILES], U32)
        tile_rows = sb("tile_rows", [P, EXPERTS])
        tile_place = sb("tile_place", [P, 1], U32)
        negmax = [sb(f"negmax{p}", [P, 2]) for p in range(2)]
        rowsum = [sb(f"rowsum{p}", [P, 2]) for p in range(2)]
        rowmax = [sb(f"rowmax{p}", [P, 2]) for p in range(2)]
        rinv = [sb(f"rinv{p}", [P, 2]) for p in range(2)]

        proj = [ps(f"proj{p}", [P, 512]) for p in range(2)]
        score = [ps(f"score{p}", [P, 2, S]) for p in range(2)]
        ptp = [ps(f"ptp{p}", [P, 2, S]) for p in range(2)]
        op = [ps(f"op{p}", [P, 512]) for p in range(2)]

        x_loaded, b_loaded = sem("x_loaded"), sem("b_loaded")
        ident_ready = sem("ident_ready")
        xt_ready, xt_copied, xt_split = sem("xt_ready"), sem("xt_copied"), sem("xt_split")
        bias_turned, bias_ready = sem("bias_turned"), sem("bias_ready")
        w_loaded = [sem(f"w_loaded{g}") for g in range(4)]
        w_made = [sem(f"w_made{g}") for g in range(4)]
        w_hi = [sem(f"w_hi{g}") for g in range(4)]
        w_lo = [sem(f"w_lo{g}") for g in range(4)]
        proj_ready, proj_hi, proj_lo = sem("proj_ready"), sem("proj_hi"), sem("proj_lo")
        score_ready, negmax_ready, exp_done = sem("score_ready"), sem("negmax_ready"), sem("exp_done")
        rinv_ready, prob_ready = sem("rinv_ready"), sem("prob_ready")
        pt_ready, pt_hi_ready, pt_lo_ready = sem("pt_ready"), sem("pt_hi_ready"), sem("pt_lo_ready")
        o_ready, o_stored = sem("o_ready"), sem("o_stored")
        importance_loaded, small_loaded = sem("importance_loaded"), sem("small_loaded")
        setup_loaded, zeros_ready, table_zeroed = sem("setup_loaded"), sem("zeros_ready"), sem("table_zeroed")
        masks_ready, idx_float, mix_ready = sem("masks_ready"), sem("idx_float"), sem("mix_ready")
        setup_pe, setup_dve, setup_act = sem("setup_pe"), sem("setup_dve"), sem("setup_act")
        pool_passed, act_passed = sem("pool_passed"), sem("act_passed")
        tile_staged, scattered = sem("tile_staged"), sem("scattered")
        rowmax_ready, setup_step = sem("rowmax_ready"), sem("setup_step")

        def passes(eng, body, setup):
            for t in range(3, STEPS):
                body(-1, t)
                setup(t)
            for t in range(STEPS):
                body(0, t)
            with eng.Fori(1, PAIRS - 1) as i:
                for t in range(STEPS):
                    body(i, t)
            for t in range(STEPS):
                body(PAIRS - 1, t)

        def no_setup(t):
            pass

        LOADS = [10, 5, 10, 5]

        def weight_parts(g, i):
            if g == 3:
                return (z[:, bass.ds(2 * (i + 1), 2), :].rearrange("p a b -> p (a b)") for z in (wo_hi, wo_lo))
            if g == 1:
                return (z[:, :, :].rearrange("p a b -> p (a b)") for z in (wv_hi, wv_lo))
            return (z[g // 2][:, :, :, :].rearrange("p a b c -> p (a b c)") for z in (wqk_hi, wqk_lo))

        def within(i, t, ahead, count=STEPS * PAIRS):
            return not isinstance(i, int) or 0 <= STEPS * i + t + ahead < count

        def value_unit(i, t):
            if t not in V_SLOT or isinstance(i, int) and (i == PAIRS - 1 and t > 0 or i == -1 and t == 0):
                return None
            return (3, i) if t == 0 else (t - 5, i + 1)

        block = ctx.enter_context(nc.Block())

        @block.sync
        def _(sp):
            sp.dma_start(xrow, x.rearrange("b (s p) d -> p (b s) d", p=P)).then_inc(x_loaded, 16)

            def load(p, blocks=range(4)):
                for g in blocks:
                    if not isinstance(p, int) or p > 0:
                        sp.wait_ge(w_lo[g], p)
                    if g == 3:
                        codes, scales = w[6], w[7]
                        src = codes[bass.ds(p * 256, 256), :].rearrange("(k p) f -> p k f", p=P)
                        sp.dma_start(code[g][:, :].rearrange("p (k f) -> p k f", k=2), src).then_inc(w_loaded[g], 16)
                        rows = scales[bass.ds(p * 8, 8), :].rearrange("(k b) f -> b k f", k=2)
                        for b in range(4):
                            sp.dma_start(scal[g][b * BLK:(b + 1) * BLK, :].rearrange("p (k f) -> p k f", k=2),
                                         rows[b:b + 1].broadcast_to([BLK, 2, 256])).then_inc(w_loaded[g], 16)
                        continue
                    width = 256 if g == 1 else P
                    col = p * 256 + (P if g == 2 else 0)
                    for m in range(1 if g == 1 else 2):
                        codes, scales = (w[4], w[5]) if g == 1 else (w[2 * m], w[2 * m + 1])
                        span = slice(m * 256, m * 256 + KT * width)
                        src = codes.rearrange("(k p) f -> p k f", p=P)[:, :, bass.ds(col, width)]
                        sp.dma_start(code[g][:, span].rearrange("p (k f) -> p k f", k=KT), src)\
                          .then_inc(w_loaded[g], 16)
                        rows = scales.rearrange("(k b) f -> b k f", k=KT)[:, :, bass.ds(col, width)]
                        for b in range(4):
                            sp.dma_start(scal[g][b * BLK:(b + 1) * BLK, span].rearrange("p (k f) -> p k f", k=KT),
                                         rows[b:b + 1].broadcast_to([BLK, KT, width])).then_inc(w_loaded[g], 16)

            load(0, [0])
            for k in range(3):
                sp.dma_start(brow[k * HEADS:(k + 1) * HEADS, :],
                             bias_rows[k].rearrange("(h f) -> h f", f=HD)).then_inc(b_loaded, 16)
            load(0, [1, 2, 3])
            sp.wait_ge(zeros_ready, 1)
            sp.dma_start(table.rearrange("(p a) e -> p (a e)", p=P), zeros).then_inc(table_zeroed, 16)
            with sp.Fori(1, PAIRS) as p:
                load(p)
            sp.wait_ge(o_stored, PAIRS * STEPS)

        @block.gpsimd
        def _(pool):
            pool.memset(ident[:, :], 0.0).then_inc(ident_ready, 1)
            pool.wait_ge(ident_ready, 1)
            pool.affine_select(out=ident[:, :], in_=ident[:, :], compare_op=ALU.not_equal, fill=1.0,
                               base=0, pattern=[[-1, P]], channel_multiplier=1).then_inc(ident_ready, 1)

            pool.dma_start(imp_sb, importance).then_inc(importance_loaded, 16)
            for dst, src in ((idx_16, idx.rearrange("(t s) -> t s", s=P)), (mix, expert_atoms)):
                pool.dma_start(dst, src).then_inc(small_loaded, 16)
            for dst, src in ((idx_row, idx.rearrange("(a n) -> a n", a=1).broadcast_to([P, NS])),
                             (atoms_sb, atoms)):
                pool.dma_start(dst, src).then_inc(setup_loaded, 16)

            pool.memset(before, 1.0).then_inc(masks_ready, 1)
            pool.iota(spare_i, pattern=[[0, 1]], base=D * D, channel_multiplier=1).then_inc(masks_ready, 1)
            pool.wait_ge(masks_ready, 2)
            pool.affine_select(out=before, in_=before, compare_op=ALU.is_gt, fill=0.0, base=0,
                               pattern=[[-1, P]], channel_multiplier=1).then_inc(masks_ready, 1)

            def scatter(i, half):
                n = 2 * i + half
                if isinstance(i, int) and n == 0:
                    pool.wait_ge(table_zeroed, 16)
                    pool.wait_ge(setup_dve, SETUP_DONE)
                else:
                    hold(pool, scattered, 16 * n, pool_passed)
                pool.tensor_copy(tile_rows[:, :], summed[:, bass.ds(n * EXPERTS, EXPERTS)]).then_inc(tile_staged, 1)
                pool.tensor_copy(tile_place[:, :], place[:, bass.ds(n, 1)]).then_inc(tile_staged, 1)
                hold(pool, tile_staged, 2 * (n + 1), pool_passed)
                pool.indirect_dma_start(
                    out=table, out_offset=bass.IndirectOffsetOnAxis(ap=tile_place[:, 0:1], axis=0),
                    in_=tile_rows[:, :], in_offset=None, compute_op=ALU.add).then_inc(scattered, 16)

            def multiply(g, i):
                pool.wait_ge(w_loaded[g], 16 * LOADS[g] * (i + 2))
                pool.tensor_tensor(code[g][:, :], code[g][:, :], scal[g][:, :], ALU.mult).then_inc(w_made[g], 1)

            def make_low(g, i):
                hi, lo = weight_parts(g, i)
                hold(pool, w_hi[g], i + 2, pool_passed)
                pool.tensor_tensor(lo, code[g][:, :], hi.bitcast(F32), ALU.subtract).then_inc(w_lo[g], 1)

            def step(i, t):
                n = STEPS * i + t
                last = isinstance(i, int) and i == PAIRS - 1
                if isinstance(i, int) and i == -1:
                    if t == 3:
                        multiply(0, i)
                    if t < 7:
                        make_low(t - 3, i)
                    if t < 6:
                        multiply(t - 2, i)
                elif not last and t % 2 == 0:
                    multiply(t // 2, i)
                elif not last:
                    make_low(t // 2, i)
                if t in (3, 7) and not (isinstance(i, int) and i < 0):
                    scatter(i, t // 4)
                if within(i, t, 1):
                    hold(pool, rinv_ready, n + 2, pool_passed)
                    k = (t + 1) % 2
                    for q in range(2):
                        pool.tensor_scalar(prob[k][:, q, :], prob[k][:, q, :], rinv[k][:, q:q + 1], 1.0,
                                           ALU.mult, ALU.mult).then_inc(prob_ready, 1)

            def setup(t):
                if t == 4:
                    pool.memset(zeros, 0.0).then_inc(zeros_ready, 1)

            passes(pool, step, setup)
            pool.wait_ge(scattered, 16 * NS_TILES)

        @block.tensor
        def _(pe):
            pe.wait_ge(ident_ready, 2)
            pe.wait_ge(x_loaded, 16)
            for u in range(4):
                k, half = u % 2, u // 2
                if u >= 2:
                    pe.wait_ge(xt_split, u - 1)
                for j in range(4):
                    last = pe.transpose(proj[u % 2][:, j * P:(j + 1) * P],
                                        xrow[:, half * 4 + j, k * P:(k + 1) * P], ident[:, :])
                last.then_inc(xt_ready, 1)
            pe.wait_ge(b_loaded, 48)
            pe.transpose(op[0][:, 0:3 * HEADS], brow, ident[0:3 * HEADS, 0:3 * HEADS]).then_inc(bias_turned, 1)
            pe.wait_ge(xt_split, 4)
            pe.wait_ge(bias_ready, 1)

            pe.wait_ge(idx_float, 1)
            pe.transpose(op[1][:, 0:NS_TILES], idx_16f, ident[0:NS_TILES, 0:NS_TILES]).then_inc(setup_pe, 1)
            pe.wait_ge(importance_loaded, 16)
            for t in range(NS_TILES):
                last = pe.transpose(ptp[0][:, 0, t * EXPERTS:(t + 1) * EXPERTS],
                                    imp_sb[:, t * P:(t + 1) * P], ident[96:96 + EXPERTS, 96:96 + EXPERTS])
            last.then_inc(setup_pe, 1)

            def setup(t):
                if t == 3:
                    pe.wait_ge(mix_ready, 1)
                    pe.transpose(ptp[1][0:ATOMS, 0, 0:EXPERTS], mix, ident[0:EXPERTS, 0:EXPERTS])\
                        .then_inc(setup_pe, 1)
                elif t == 4:
                    pe.wait_ge(setup_loaded, 32)
                    pe.wait_ge(setup_dve, 1)
                    for t in range(NS_TILES):
                        last = pe.matmul(op[0][:, t * EXPERTS:(t + 1) * EXPERTS],
                                         atoms_sb[:, t * P:(t + 1) * P], mix_t, start=True, stop=True)
                    last.then_inc(setup_pe, 1)
                elif t == 6:
                    pe.wait_ge(setup_dve, 2)
                    for t in range(NS_TILES):
                        last = pe.matmul(op[1][:, t * EXPERTS:(t + 1) * EXPERTS],
                                         same[:, t, :], scaled[:, t * EXPERTS:(t + 1) * EXPERTS],
                                         start=True, stop=True)
                    last.then_inc(setup_pe, 1)
                elif t == 7:
                    pe.wait_ge(setup_dve, SETUP_DONE)

            def three(out, lh, ll, rh, rl, k, n):
                pe.matmul(out, lh, rh, start=(k == 0), stop=False)
                pe.matmul(out, lh, rl, start=False, stop=False)
                return pe.matmul(out, ll, rh, start=False, stop=(k == n - 1))

            def step(i, t):
                n = STEPS * i + t
                if within(i, t, 2):
                    m = n + 2
                    c = t + 2
                    par, b = (c // 4) % 2, c % 4
                    pe.wait_ge(proj_lo, qk_seq(i, 4 * (c // 4) + 2 * (b // 2) + 1) + 1)
                    positive(pe, exp_done, m - 1)
                    lo, hi = qk_lo[par], qk_hi[par]
                    keys = slice(b * S, (b + 1) * S)
                    for q in range(2):
                        rows = slice(b * S + q * P, b * S + (q + 1) * P)
                        last = three(score[c % 2][:, q, :], hi[:, 0, rows], lo[:, 0, rows],
                                     hi[:, 1, keys], lo[:, 1, keys], 0, 1)
                    last.then_inc(score_ready, 1)
                if within(i, t, 5):
                    c = t + 5
                    par, part = (c // 4) % 2, c % 4
                    pair = i + c // 8
                    seq = qk_seq(i, c)
                    bank = proj[QK_SLOT[t] % 2]
                    pe.wait_ge(w_lo[2 * par], pair + 1)
                    positive(pe, proj_lo, seq - 1)
                    m, half = part % 2, part // 2
                    cols = slice(half * 512, (half + 1) * 512)
                    for k in range(KT):
                        last = three(bank[:, :], wqk_hi[par][:, m, k, :], wqk_lo[par][:, m, k, :],
                                     xt_hi[:, k, cols], xt_lo[:, k, cols], k, KT)
                    last.then_inc(proj_ready, 1)
                if within(i, t, 0):
                    pe.wait_ge(prob_ready, 2 * (n + 1))
                    positive(pe, pt_lo_ready, n - 1)
                    for k in range(2):
                        for q in range(2):
                            last = pe.transpose(ptp[t % 2][:, k, q * P:(q + 1) * P],
                                                prob[t % 2][:, q, k * P:(k + 1) * P], ident[:, :])
                    last.then_inc(pt_ready, 1)
                if within(i, t, -1):
                    m, c = n - 1, (t - 1) % 8
                    weigh(i, t, m, c)
                if value_unit(i, t):
                    b, pair = value_unit(i, t)
                    seq = v_seq(pair, b)
                    bank = proj[V_SLOT[t] % 2]
                    pe.wait_ge(w_lo[1], pair + 1)
                    positive(pe, proj_lo, seq - 1)
                    for j in range(2):
                        rows = slice(b * S + j * P, b * S + (j + 1) * P)
                        for k in range(KT):
                            last = three(bank[:, j * 256:(j + 1) * 256], xt_hi[:, k, rows], xt_lo[:, k, rows],
                                         wv_hi[:, k, :], wv_lo[:, k, :], k, KT)
                    last.then_inc(proj_ready, 1)

            def weigh(i, t, m, c):
                par, b = c // 4, c % 4
                pair = i - 1 if t == 0 else i
                pe.wait_ge(pt_lo_ready, m + 1)
                pe.wait_ge(proj_lo, v_seq(pair, b) + 1)
                positive(pe, o_stored, m - 1)
                for k in range(2):
                    cols = slice(par * P, (par + 1) * P)
                    last = three(op[c % 2][:, 0:S], v_hi[:, 2 * b + k, cols], v_lo[:, 2 * b + k, cols],
                                 pt_hi[c % 2][:, k, :], pt_lo[c % 2][:, k, :], k, 2)
                last.then_inc(o_ready, 1)

            passes(pe, step, setup)
            weigh(PAIRS, 0, STEPS * PAIRS - 1, 7)

        @block.scalar
        def _(act):
            def make_high(g, i):
                hi, lo = weight_parts(g, i)
                if g < 3:
                    positive(act, proj_ready, (qk_seq(i, 3), v_seq(i, 3), qk_seq(i, 7))[g] + 1)
                hold(act, w_made[g], i + 2, act_passed)
                act.copy(hi, code[g][:, :]).then_inc(w_hi[g], 1)

            for u in range(4):
                k, half = u % 2, u // 2
                act.wait_ge(xt_ready, u + 1)
                act.copy(xt_hi[:, k, half * 512:(half + 1) * 512], proj[u % 2][:, :]).then_inc(xt_copied, 1)
            act.wait_ge(bias_turned, 1)
            act.copy(bias[:, :], op[0][:, 0:3 * HEADS]).then_inc(bias_ready, 1)
            act.wait_ge(bias_ready, 1)
            make_high(0, -1)
            act.wait_ge(setup_act, 1)
            act.activation(mix, mix, ACT.Exp, bias=mix_s[:, 0:1], accum_out=mix_s[:, 1:2]).then_inc(setup_act, 1)

            act.wait_ge(setup_pe, 2)
            act.activation(gates, ptp[0][:, 0, 0:NS_TILES * EXPERTS], ACT.Exp, scale=-1.0).then_inc(setup_act, 1)

            def step(i, t):
                n = STEPS * i + t
                if within(i, t, 5):
                    c = t + 5
                    par, part = (c // 4) % 2, c % 4
                    m, half = part % 2, part // 2
                    head = 2 * (i + c // 8) + par
                    seq = qk_seq(i, c)
                    hold(act, proj_ready, seq + 1, act_passed)
                    act.activation(qk_hi[par][:, m, half * 512:(half + 1) * 512], proj[QK_SLOT[t] % 2][:, :],
                                   ACT.Identity, bias=bias[:, bass.ds(m * HEADS + head, 1)]).then_inc(proj_hi, 1)
                if within(i, t, 0):
                    act.wait_ge(pt_ready, n + 1)
                    positive(act, o_ready, n - 1)
                    act.copy(pt_hi[t % 2][:, :, :], ptp[t % 2][:, :, :]).then_inc(pt_hi_ready, 1)
                if value_unit(i, t):
                    b, pair = value_unit(i, t)
                    act.wait_ge(proj_ready, v_seq(pair, b) + 1)
                    act.copy(v_hi[:, 2 * b:2 * b + 2, :],
                             proj[V_SLOT[t] % 2][:, :].rearrange("p (j f) -> p j f", j=2)).then_inc(proj_hi, 1)
                if within(i, t, 2):
                    k = t % 2
                    act.wait_ge(negmax_ready, n + 3)
                    positive(act, pt_ready, n + 1)
                    for q in range(2):
                        last = act.activation(prob[k][:, q, :], score[k][:, q, :], ACT.Exp,
                                              bias=negmax[k][:, q:q + 1], scale=SCALE,
                                              accum_out=rowsum[k][:, q:q + 1])
                    last.then_inc(exp_done, 1)

            def step_and_weights(i, t):
                first = isinstance(i, int) and i == -1
                step(i, t)
                if first and t < 6:
                    make_high(t - 2, i)
                if not first and t % 2 == 0 and not (isinstance(i, int) and i == PAIRS - 1):
                    make_high(t // 2, i)

            passes(act, step_and_weights, no_setup)

        @block.vector
        def _(dve):
            for u in range(4):
                k, half = u % 2, u // 2
                dve.wait_ge(xt_copied, u + 1)
                cols = slice(half * 512, (half + 1) * 512)
                dve.tensor_tensor(xt_lo[:, k, cols], proj[u % 2][:, :], xt_hi[:, k, cols].bitcast(F32),
                                  ALU.subtract).then_inc(xt_split, 1)
            dve.wait_ge(bias_ready, 1)
            count = [0]

            def then(ins):
                count[0] += 1
                ins.then_inc(setup_step, 1)
                dve.wait_ge(setup_step, count[0])

            dve.wait_ge(small_loaded, 32)
            dve.tensor_copy(idx_16f, idx_16).then_inc(idx_float, 1)
            dve.tensor_reduce(mix_s[:, 0:1], mix, AX.X, ALU.max, negate=True).then_inc(setup_act, 1)
            dve.wait_ge(setup_pe, 1)
            then(dve.tensor_copy(idx_f, op[1][:, 0:NS_TILES]))
            then(dve.tensor_copy(idx_i, idx_f))
            dve.tensor_scalar(row_i, idx_i, 8, None, ALU.logical_shift_right)
            then(dve.tensor_scalar(col_i, idx_i, D - 1, 8, ALU.bitwise_and, ALU.logical_shift_left))
            then(dve.tensor_tensor(place_f, col_i, row_i, ALU.add))
            dve.wait_ge(setup_loaded, 32)
            then(dve.tensor_tensor(same, idx_row.rearrange("p (t s) -> p t s", t=NS_TILES),
                                   idx_f.unsqueeze(2).broadcast_to([P, NS_TILES, P]), ALU.is_equal))
            dve.wait_ge(setup_act, 2)
            then(dve.reciprocal(mix_s[:, 2:3], mix_s[:, 1:2]))
            dve.tensor_scalar(mix, mix, mix_s[:, 2:3], None, ALU.mult).then_inc(mix_ready, 1)

            def duplicates_first():
                then(dve.tensor_tensor(earlier, same, before.unsqueeze(1).broadcast_to([P, NS_TILES, P]), ALU.mult))

            def duplicates_second():
                then(dve.tensor_reduce(dup, earlier, AX.X, ALU.max))
                then(dve.tensor_copy(idx_f, spare_i.broadcast_to([P, NS_TILES])))
                then(dve.tensor_tensor(idx_f, idx_f, place_f, ALU.subtract))
                then(dve.tensor_tensor(idx_f, idx_f, dup, ALU.mult))
                then(dve.tensor_tensor(place[:, :], place_f, idx_f, ALU.add))

            def setup(t):
                if t == 3:
                    dve.wait_ge(setup_pe, 3)
                    dve.tensor_copy(mix_t, ptp[1][0:ATOMS, 0, 0:EXPERTS]).then_inc(setup_dve, 1)
                    dve.wait_ge(masks_ready, 3)
                    duplicates_first()
                elif t == 4:
                    dve.wait_ge(setup_act, 3)
                    then(dve.tensor_scalar(gates, gates, 1.0, None, ALU.add))
                    then(dve.reciprocal(gates, gates))
                    duplicates_second()
                elif t == 5:
                    dve.wait_ge(setup_pe, 4)
                    dve.tensor_tensor(scaled, op[0][:, 0:NS_TILES * EXPERTS], gates, ALU.mult)\
                       .then_inc(setup_dve, 1)
                elif t == 7:
                    dve.wait_ge(setup_pe, 5)
                    dve.tensor_copy(summed[:, :], op[1][:, 0:NS_TILES * EXPERTS]).then_inc(setup_dve, 1)

            def store_o(i, t, m, c):
                par, b = c // 4, c % 4
                head = 2 * (i - 1 if t == 0 else i) + par
                dve.wait_ge(o_ready, m + 1)
                dve.tensor_scalar(ot[:, bass.ds(head * T + b * S, S)], op[c % 2][:, 0:S],
                                  bias[:, bass.ds(2 * HEADS + head, 1)], None, ALU.add).then_inc(o_stored, 1)

            def step(i, t):
                n = STEPS * i + t
                if within(i, t, 2):
                    k = t % 2
                    dve.wait_ge(score_ready, n + 3)
                    dve.tensor_reduce(rowmax[k][:, :], score[k][:, :, :], AX.X, ALU.max).then_inc(rowmax_ready, 1)
                    dve.wait_ge(rowmax_ready, n + 3)
                    dve.tensor_scalar(negmax[k][:, :], rowmax[k][:, :], -SCALE, None, ALU.mult)\
                       .then_inc(negmax_ready, 1)
                if within(i, t, 5):
                    c = t + 5
                    par, part = (c // 4) % 2, c % 4
                    m, half = part % 2, part // 2
                    head = 2 * (i + c // 8) + par
                    cols = slice(half * 512, (half + 1) * 512)
                    dve.wait_ge(proj_hi, qk_seq(i, c) + 1)
                    dve.scalar_tensor_tensor(qk_lo[par][:, m, cols], proj[QK_SLOT[t] % 2][:, :],
                                             bias[:, bass.ds(m * HEADS + head, 1)],
                                             qk_hi[par][:, m, cols].bitcast(F32),
                                             ALU.add, ALU.subtract).then_inc(proj_lo, 1)
                if within(i, t, 1):
                    k = (t + 1) % 2
                    dve.wait_ge(exp_done, n + 2)
                    dve.reciprocal(rinv[k][:, :], rowsum[k][:, :]).then_inc(rinv_ready, 1)
                if within(i, t, 0):
                    dve.wait_ge(pt_hi_ready, n + 1)
                    dve.tensor_tensor(pt_lo[t % 2][:, :, :], ptp[t % 2][:, :, :],
                                      pt_hi[t % 2][:, :, :].bitcast(F32), ALU.subtract).then_inc(pt_lo_ready, 1)
                if within(i, t, -1):
                    store_o(i, t, n - 1, (t - 1) % 8)
                if value_unit(i, t):
                    b, pair = value_unit(i, t)
                    dve.wait_ge(proj_hi, v_seq(pair, b) + 1)
                    dve.tensor_tensor(v_lo[:, 2 * b:2 * b + 2, :],
                                      proj[V_SLOT[t] % 2][:, :].rearrange("p (j f) -> p j f", j=2),
                                      v_hi[:, 2 * b:2 * b + 2, :].bitcast(F32), ALU.subtract)\
                       .then_inc(proj_lo, 1)

            def step_and_zeros(i, t):
                if isinstance(i, int) and i == 0 and t == 7:
                    dve.wait_ge(table_zeroed, 16)
                step(i, t)

            passes(dve, step_and_zeros, setup)
            store_o(PAIRS, 0, STEPS * PAIRS - 1, 7)


EPS_LN, EPS_Q, QMAX = 1e-5, 1e-6, 127.0
ROUND = 1.5 * 2.0 ** 23
INNER = 128
TB = S // P
NB = 2
NT = NB * TB
GROUPS = B // NB
HG, RING = 4, 4
UPB = TB * HEADS // HG
WIDE = EXPERTS * D
CHUNKS = WIDE // 512
CLIP = 50.0

LINKS = [("prep", None, "dve", (2, 3), ()),
         ("prepd", None, "dve", (2,), ("prep",)),
         ("x1", "dve", "dve", (0, 1), ()),
         ("scale", "dve", "dve", (2, 3), ("prepd",)),
         ("xq", "dve", "dve", (0,), ("x1",)),
         ("wq", "dve", "dve", (1,), ("x1",)),
         ("row1", "dve", "act", (2,), ("scale",)),
         ("mm1", "dve", "dve", (0, 1), ("wq",)),
         ("act", "dve", "dve", (3,), ("scale",)),
         ("scale2", "dve", "dve", (2,), ("row1",)),
         ("q2", "dve", "dve", (3,), ("act",)),
         ("row2", "dve", "act", (2,), ("scale2",)),
         ("mm2", "dve", "dve", (0, 1), ("mm1",)),
         ("x2", "dve", "act", (2, 3), ("q2", "row2")),
         ("gate", "act", "dve", (0, 1, 2, 3), ("mm2", "x2"))]


def count_links():
    counted, feeds, reads = {}, {"dve": 0, "act": 0}, {"dve": 0, "act": 0}
    for k, (name, feeder, reader, banks, before) in enumerate(LINKS):
        if feeder:
            feeds[feeder] += 1
        reads[reader] += 1
        counted[name] = dict(number=k, banks=banks, before=before, feeder=feeder,
                             fed=feeds[feeder] if feeder else 0, reader=reader, read=reads[reader])
    return counted


def unit_of(u):
    b, j, q = u // UPB, u % UPB * TB // UPB, u % (UPB // TB)
    return slice(HG * q, HG * (q + 1)), slice(b * S + j * P, b * S + (j + 1) * P)


def layers(nc, x, bo, guw, dw, gate_w, w_ffn, table, out, kept):
    ident, ot, wo_hi, wo_lo = kept
    links = count_links()
    with ExitStack() as ctx:
        def sb(name, shape, dt=F32):
            return ctx.enter_context(nc.sbuf_tensor(name, shape, dt))

        def sem(name):
            return ctx.enter_context(nc.semaphore(name))

        o_hi = [sb(f"o_hi{k}", [P, HG, P], F32R) for k in range(RING)]
        o_lo = [sb(f"o_lo{k}", [P, HG, P], F32R) for k in range(RING)]
        bo_row = sb("bo_row", [P, D])
        ones = sb("ones", [P, P])
        half_power = sb("half_power", [P, 8])
        iota8 = sb("iota8", [P, EXPERTS])
        wall_hi = sb("wall_hi", [P, KT, WIDE + D + EXPERTS], F32R)
        wall_lo = sb("wall_lo", [P, KT, WIDE + D + EXPERTS], F32R)
        free = [0]

        def region(cols):
            free[0] += cols
            assert free[0] <= HEADS * T
            return ot[:, free[0] - cols:free[0]]

        raw = [region(WIDE) for k in range(KT)]

        def per_group(name, count, width, dt=F32):
            size = count * width * (2 if dt is BF16 else 4) // 4
            late = [region(size) for g in range(1, GROUPS)]
            late = [(a.bitcast(dt) if dt is not F32 else a).rearrange("p (n d) -> p n d", n=count) for a in late]
            return [sb(name, [P, count, width], dt)[:, :, :]] + late

        def small(name, width, dt=F32):
            return [sb(f"{name}{g}", [P, width], dt)[:, :] for g in range(GROUPS)]

        xb = [sb(f"xb{g}", [P, NT, D])[:, :, :] for g in range(GROUPS)]
        gu_sb = [sb(f"gu_sb{g}", [P, NT, D])[:, :, :] for g in range(GROUPS)]
        dw_sb = [sb(f"dw_sb{g}", [P, NT, INNER])[:, :, :] for g in range(GROUPS)]
        scaled, y1 = per_group("scaled", NT, D), per_group("y1", NT, D)
        x1, x2 = per_group("x1", NT, D), per_group("x2", NT, D)
        diag = per_group("diag", 4 * NB, P)
        q_rows = [a.rearrange("p n d -> p (n d)").bitcast(BF16).rearrange("p (n d) -> p n d", n=2 * NT) for a in y1]
        parts = [region(4 * D) for k in range(2)]
        q_t = per_group("q_t", 2 * NB * KT, S, BF16)
        ident_16 = sb("ident_16", [P, P], BF16)
        row = per_group("row", NB, D)
        hidden = per_group("hidden", NT, 2 * INNER)
        gate, act_sb = per_group("gate", NT, INNER), per_group("act_sb", NT, INNER)
        x2t_hi, x2t_lo = ([z[:, g * NB * KT:(g + 1) * NB * KT, :] for g in range(GROUPS)] for z in (wo_hi, wo_lo))
        result = xb
        w_rows, g_rows = hidden[0], row[0][0:EXPERTS, 0, :]
        amax_w, amax_d, amax_x = small("amax_w", NB * KT), small("amax_d", NB), small("amax_x", NB * KT)
        inv_amax_w, inv_amax_d = small("inv_amax_w", NB * KT), small("inv_amax_d", NB)
        smooth, unsmooth = small("smooth", NB * KT), small("unsmooth", NB * KT)
        x_scale, w_scale = small("x_scale", NT), small("w_scale", NT)
        inv = [[sb(f"inv{g}_{k}", [P, NT])[:, :] for k in range(2)] for g in range(GROUPS)]
        round_bias = sb("round_bias", [P, 1])
        st = [sb(f"st{g}", [P, NT, 6]) for g in range(GROUPS)]
        mv = [sb(f"mv{g}", [P, NT, 2]) for g in range(GROUPS)]
        base, root = small("base", 4), small("root", 4)
        logit, top = sb("logit", [P, NT, EXPERTS]), sb("top", [P, NT, EXPERTS])
        top_at = sb("top_at", [P, NT, EXPERTS], U32)
        top_f = sb("top_f", [P, NT, 2])
        gap, share = sb("gap", [P, NT]), sb("share", [P, NT, 2])
        weight = [sb(f"weight{g}", [P, NT, EXPERTS]) for g in range(GROUPS)]
        second = sb("second", [P, NT, EXPERTS])

        banks = [ctx.enter_context(nc.psum_tensor(f"banks{g}", [P, 4, 512], F32)) for g in range(GROUPS)]

        w_in, bo_in = sem("w_in"), sem("bo_in")
        x_in, q_in = [sem(f"x_in{g}") for g in range(GROUPS)], [sem(f"q_in{g}") for g in range(GROUPS)]
        raw_in = [sem(f"raw_in{k}") for k in range(KT)]
        wt_ready, wt_used = sem("wt_ready"), sem("wt_used")
        consts = sem("consts")
        wall_hi_ready, wall_ready = sem("wall_hi_ready"), sem("wall_ready")
        o_hi_ready, o_used = sem("o_hi_ready"), sem("o_used")
        o_lo_pool, o_lo_dve = sem("o_lo_pool"), sem("o_lo_dve")
        xb_ready = sem("xb_ready")
        link_ready = [sem(f"link_ready{g}") for g in range(GROUPS)]
        link_fed = [{e: sem(f"fed_by_{e}{g}") for e in ("dve", "act")} for g in range(GROUPS)]
        link_read = [{e: sem(f"read_by_{e}{g}") for e in ("dve", "act")} for g in range(GROUPS)]
        exp_in, exp_out = sem("exp_in"), sem("exp_out")
        pow_in, pow_out = sem("pow_in"), sem("pow_out")
        round_in, round_out = sem("round_in"), sem("round_out")
        x2t_hi_ready, x2t_ready = sem("x2t_hi_ready"), sem("x2t_ready")
        f_ready = [sem(f"f_ready{g}") for g in range(GROUPS)]
        f_used = [{e: sem(f"f_used_by_{e}{g}") for e in ("dve", "act")} for g in range(GROUPS)]
        weights_ready, fold = sem("weights_ready"), sem("fold")
        scaled_ready = [sem(f"scaled_ready{g}") for g in range(GROUPS)]
        sums_ready, sums_used = [sem(f"sums_ready{g}") for g in range(GROUPS)], sem("sums_used")
        result_ready = sem("result_ready")
        stored = [sem(f"stored{g}") for g in range(GROUPS)]
        chain = sem("chain")

        def low_by_dve(u):
            return u < NB * UPB and u % 2 == 0

        def low_count(u):
            return sum(low_by_dve(v) == low_by_dve(u) for v in range(u + 1))

        def low_part(eng, u, ready):
            heads, rows = unit_of(u)
            eng.wait_ge(o_hi_ready, u + 1)
            eng.tensor_tensor(o_lo[u % RING][:, :, :], ot_view[:, heads, rows],
                              o_hi[u % RING][:, :, :].bitcast(F32), ALU.subtract).then_inc(ready, 1)

        ot_view = ot[:, :].rearrange("p (h t) -> p h t", h=HEADS)

        def banks_of(g, name):
            b = links[name]["banks"]
            return banks[g][:, b[0]:b[-1] + 1, :].rearrange("p k n -> p (k n)")

        BY_ACT = [CHUNKS] * (GROUPS - 1) + [CHUNKS // 2]

        def weighted_by(g, f):
            n, c = f // CHUNKS, f % CHUNKS
            return ("act", BY_ACT[g] * n + c + 1) if c < BY_ACT[g] else \
                ("dve", (CHUNKS - BY_ACT[g]) * n + c - BY_ACT[g] + 1)

        def part_of(g, n):
            return raw[n % 2] if g < GROUPS - 1 else parts[n % 2]

        def flat(a):
            return a.rearrange("p n d -> p (n d)")

        OWN = 1
        CONSTS = 6
        GIVEN = [NB * UPB + n for n in (5, 8, 12, 12)]

        block = ctx.enter_context(nc.Block())

        @block.sync
        def _(sp):
            def load(g):
                bs = slice(NB * g, NB * (g + 1))
                sp.dma_start(gu_sb[g], guw[bs].rearrange("b (j p) d -> p (b j) d", p=P)).then_inc(q_in[g], 16)
                sp.dma_start(dw_sb[g], dw[bs].rearrange("b (j p) d -> p (b j) d", p=P)).then_inc(q_in[g], 16)
                sp.dma_start(xb[g], x[bs].rearrange("b (j p) d -> p (b j) d", p=P)).then_inc(x_in[g], 16)

            sp.dma_start(w_rows[:, 0:TB, :], w_ffn.rearrange("(j p) d -> p j d", p=P)).then_inc(w_in, 16)
            sp.dma_start(g_rows, gate_w).then_inc(w_in, 16)
            load(0)
            sp.dma_start(bo_row[:, :], bo.rearrange("(a n) -> a n", a=1).broadcast_to([P, D])).then_inc(bo_in, 16)
            for g in range(1, GROUPS):
                load(g)
            rows = table[0:D * D, :].rearrange("(k p r) e -> k p (r e)", k=KT, p=P)
            sp.wait_ge(o_used, B * UPB)
            for k in range(KT):
                sp.dma_start(raw[k], rows[k]).then_inc(raw_in[k], 16)
            for g in range(GROUPS):
                for n in range(NT):
                    sp.wait_ge(result_ready, NT * g + n + 1)
                    b, j = NB * g + n // TB, n % TB
                    sp.dma_start(out[b, j * P:(j + 1) * P, :], result[g][:, n, :]).then_inc(stored[g], 16)
            for g in range(GROUPS):
                sp.wait_ge(stored[g], 16 * NT)

        @block.gpsimd
        def _(pool):
            pool.memset(ones[:, :], 1.0).then_inc(consts, 1)
            pool.memset(round_bias[:, :], ROUND).then_inc(consts, 1)
            pool.memset(half_power[:, 0:4], -0.5).then_inc(consts, 1)
            pool.memset(half_power[:, 4:8], 0.5).then_inc(consts, 1)
            pool.iota(iota8[:, :], pattern=[[1, EXPERTS]], base=0, channel_multiplier=0,
                      allow_small_or_imprecise_dtypes=True).then_inc(consts, 1)
            pool.tensor_copy(ident_16[:, :], ident[:, :]).then_inc(consts, 1)
            pool.wait_ge(consts, CONSTS)
            powers = [0]

            def power(g, width, sign):
                powers[0] += 1
                pool.wait_ge(pow_in, powers[0])
                e = half_power[:, 4:4 + width] if sign > 0 else half_power[:, 0:width]
                pool.tensor_tensor(root[g][:, 0:width], base[g][:, 0:width], e, ALU.pow).then_inc(pow_out, 1)

            def low_parts(first, last):
                for u in range(first, last):
                    if not low_by_dve(u):
                        low_part(pool, u, o_lo_pool)

            def add_bias(g):
                pool.wait_ge(x_in[g], 16)
                pool.tensor_tensor(xb[g], xb[g], bo_row[:, :].unsqueeze(1).broadcast_to([P, NT, D]), ALU.add)\
                    .then_inc(xb_ready, 1)

            def experts_low(k):
                pool.wait_ge(wall_hi_ready, KT + k + 1)
                pool.tensor_tensor(wall_lo[:, k, 0:WIDE].rearrange("p (e r) -> p e r", e=EXPERTS),
                                   raw[k].rearrange("p (r e) -> p e r", e=EXPERTS),
                                   wall_hi[:, k, 0:WIDE].bitcast(F32).rearrange("p (e r) -> p e r", e=EXPERTS),
                                   ALU.subtract).then_inc(wall_ready, 1)

            folds = [0]

            def sum_parts(g, n):
                part, width = part_of(g, n), 2 * BY_ACT[g] * D
                pool.wait_ge(scaled_ready[g], BY_ACT[g] * (n + 1))
                while width > 2 * D:
                    width //= 2
                    folds[0] += 1
                    pool.tensor_tensor(part[:, 0:width], part[:, 0:width], part[:, width:2 * width], ALU.add)\
                        .then_inc(fold, 1)
                    pool.wait_ge(fold, folds[0])
                last = pool.tensor_tensor(part[:, 0:D], part[:, 0:D], part[:, D:2 * D], ALU.add)
                if g < GROUPS - 1:
                    folds[0] += 1
                    last.then_inc(fold, 1)
                    pool.wait_ge(fold, folds[0])
                    last = pool.tensor_tensor(x2[g][:, n, :], x2[g][:, n, :], part[:, 0:D], ALU.add)
                last.then_inc(sums_ready[g], 1)

            low_parts(0, UPB)
            pool.wait_ge(bo_in, 16)
            add_bias(0)
            low_parts(UPB, GIVEN[0])
            power(0, NT, -1)
            low_parts(GIVEN[0], GIVEN[1])
            power(0, NB * KT, 1)
            low_parts(GIVEN[1], B * UPB)
            add_bias(1)
            power(1, NT, -1)
            power(0, NB, 1)
            power(1, NB * KT, 1)
            experts_low(0)
            experts_low(1)
            power(0, NT, -1)
            power(1, NB, 1)
            sum_parts(0, 0)
            sum_parts(0, 1)
            power(1, NT, -1)
            sum_parts(0, 2)
            sum_parts(0, 3)
            power(0, NT, -1)
            for n in range(NT):
                sum_parts(1, n)
                power(1, 1, -1)

        @block.tensor
        def _(pe):
            def three(out, lh, ll, rh, rl, k, n):
                pe.matmul(out, lh, rh, start=(k == 0), stop=False)
                pe.matmul(out, lh, rl, start=False, stop=False)
                return pe.matmul(out, ll, rh, start=False, stop=(k == n - 1))

            def link(g, name):
                this = links[name]
                if this["feeder"]:
                    pe.wait_ge(link_fed[g][this["feeder"]], this["fed"])
                for before in this["before"]:
                    pe.wait_ge(link_read[g][links[before]["reader"]], links[before]["read"])
                return banks_of(g, name)

            def turn_rows(bank, src, width=D, eye=ident):
                for b in range(NB):
                    for k in range(width // P):
                        for j in range(TB):
                            at = (b * (width // P) + k) * S + j * P
                            last = pe.transpose(bank[:, at:at + P], src[:, b * TB + j, k * P:(k + 1) * P],
                                                eye[:, :])
                return last

            def spread(bank, diag, cols):
                for n, c in enumerate(cols):
                    last = pe.matmul(bank[:, n * P:(n + 1) * P], ones[:, :], diag[:, c, :], start=True, stop=True)
                return last

            def project(first, last_unit):
                for u in range(first, last_unit):
                    heads, rows = unit_of(u)
                    pe.wait_ge(o_lo_dve if low_by_dve(u) else o_lo_pool, low_count(u))
                    b, j = u // UPB, u % UPB * TB // UPB
                    for k, h in enumerate(range(heads.start, heads.stop)):
                        last = three(banks[b // NB][:, b % NB, j * D:(j + 1) * D], o_hi[u % RING][:, k, :],
                                     o_lo[u % RING][:, k, :], wo_hi[:, h, :], wo_lo[:, h, :], h, HEADS)
                    last.then_inc(o_used, 1)

            def made(g, ins):
                ins.then_inc(link_ready[g], 1)

            def prepare(g):
                pe.wait_ge(q_in[g], 32)
                made(g, turn_rows(link(g, "prep"), gu_sb[g]))

            def prepare_second(g):
                made(g, turn_rows(link(g, "prepd"), dw_sb[g], INNER))

            def turn_x1(g):
                made(g, turn_rows(link(g, "x1"), x1[g]))

            def spread_scales(g):
                made(g, spread(link(g, "scale"), diag[g], range(4 * NB)))

            def turn_xq(g):
                made(g, turn_rows(link(g, "xq").bitcast(BF16), q_rows[g][:, 0:NT, :], D, ident_16))

            def turn_wq(g):
                made(g, turn_rows(link(g, "wq").bitcast(BF16), q_rows[g][:, NT:2 * NT, :], D, ident_16))

            def spread_row(g, name):
                made(g, spread(link(g, name), diag[g], range(NT)))

            def first_layer(g):
                bank = link(g, "mm1")
                for n in range(NT):
                    b, j = n // TB, n % TB
                    for k in range(KT):
                        last = pe.matmul(bank[:, n * S:(n + 1) * S], q_t[g][:, b * KT + k, j * P:(j + 1) * P],
                                         q_t[g][:, (NB + b) * KT + k, :], start=(k == 0), stop=(k == KT - 1))
                made(g, last)

            def turn_act(g):
                made(g, turn_rows(link(g, "act"), act_sb[g], INNER))

            def spread_second(g):
                made(g, spread(link(g, "scale2"), diag[g], range(NT, NT + 2 * NB)))

            def turn_q2(g):
                bank = link(g, "q2").bitcast(BF16)
                turn_rows(bank[:, 0:NB * S], q_rows[g][:, 0:NT, 0:INNER], INNER, ident_16)
                made(g, turn_rows(bank[:, NB * S:2 * NB * S], q_rows[g][:, NT:2 * NT, 0:INNER], INNER, ident_16))

            def second_layer(g):
                bank = link(g, "mm2")
                for n in range(NT):
                    b, j = n // TB, n % TB
                    last = pe.matmul(bank[:, n * D:(n + 1) * D], q_t[g][:, b, j * P:(j + 1) * P],
                                     q_t[g][:, NB + b, :], start=True, stop=True)
                made(g, last)

            def turn_x2(g):
                made(g, turn_rows(link(g, "x2"), x2[g]))

            def route(g):
                link(g, "gate")
                for n in range(NT):
                    b, rows = n // TB, slice(n % TB * P, (n % TB + 1) * P)
                    for k in range(KT):
                        last = three(banks[g][:, n, 0:D + EXPERTS], x2t_hi[g][:, b * KT + k, rows],
                                     x2t_lo[g][:, b * KT + k, rows], wall_hi[:, k, WIDE:], wall_lo[:, k, WIDE:],
                                     k, KT)
                made(g, last)

            def experts(g, n):
                for c in range(CHUNKS):
                    f = n * CHUNKS + c
                    b, rows = n // TB, slice(n % TB * P, (n % TB + 1) * P)
                    if f == 0:
                        pe.wait_ge(link_read[g]["dve"], links["gate"]["read"])
                        pe.wait_ge(wall_ready, KT)
                    if f >= CHUNKS:
                        engine, count = weighted_by(g, f - CHUNKS)
                        pe.wait_ge(f_used[g][engine], count)
                    cols = slice(c * 512, (c + 1) * 512)
                    for k in range(KT):
                        last = three(banks[g][:, c, :], x2t_hi[g][:, b * KT + k, rows],
                                     x2t_lo[g][:, b * KT + k, rows], wall_hi[:, k, cols], wall_lo[:, k, cols], k, KT)
                    last.then_inc(f_ready[g], 1)

            project(0, RING)
            pe.wait_ge(w_in, 32)
            for k in range(KT):
                for j in range(TB):
                    pe.transpose(banks[1][:, 2 + k, j * P:(j + 1) * P], w_rows[:, j, k * P:(k + 1) * P], ident[:, :])
                last = pe.transpose(banks[1][:, 2 + k, D:D + EXPERTS], g_rows[:, k * P:(k + 1) * P],
                                    ident[0:EXPERTS, 0:EXPERTS])
            last.then_inc(wt_ready, 1)
            project(RING, 7)
            prepare(0)
            project(7, 10)
            prepare_second(0)
            pe.wait_ge(consts, CONSTS)
            project(10, GIVEN[0])
            turn_x1(0)
            pe.wait_ge(wt_used, 1)
            prepare(1)
            project(GIVEN[0], GIVEN[1])
            spread_scales(0)
            prepare_second(1)
            project(GIVEN[1], GIVEN[2])
            turn_xq(0)
            turn_wq(0)
            spread_row(0, "row1")
            project(GIVEN[2], GIVEN[3])
            first_layer(0)
            project(GIVEN[3], B * UPB)
            turn_act(0)
            turn_x1(1)
            spread_second(0)
            spread_scales(1)
            turn_q2(0)
            spread_row(0, "row2")
            turn_xq(1)
            turn_wq(1)
            spread_row(1, "row1")
            second_layer(0)
            first_layer(1)
            turn_x2(0)
            route(0)
            turn_act(1)
            experts(0, 0)
            spread_second(1)
            experts(0, 1)
            turn_q2(1)
            spread_row(1, "row2")
            second_layer(1)
            experts(0, 2)
            experts(0, 3)
            turn_x2(1)
            route(1)
            for n in range(NT):
                experts(1, n)

        @block.scalar
        def _(act):
            def high_parts(first, last):
                for u in range(first, last):
                    heads, rows = unit_of(u)
                    if u >= RING:
                        act.wait_ge(o_used, u - RING + 1)
                    act.copy(o_hi[u % RING][:, :, :], ot_view[:, heads, rows]).then_inc(o_hi_ready, 1)

            def arrived(g, name):
                act.wait_ge(link_ready[g], links[name]["number"] + 1)
                return banks_of(g, name)

            def row_of(g, name):
                act.copy(flat(row[g]), arrived(g, name)[:, 0:NB * D]).then_inc(link_read[g]["act"], 1)

            def rounded(g, src, first=0):
                rounds[0] += 1
                act.wait_ge(round_in, rounds[0])
                k = rounds[0] % 2
                for n in range(first, NT):
                    last = act.activation(src[:, n, :], src[:, n, :], ACT.Identity, scale=inv[g][k][:, n:n + 1],
                                          bias=round_bias[:, 0:1])
                last.then_inc(round_out, 1)

            rounds = [0]
            exps = [0]

            def exponential(dst, src, scale=1.0):
                exps[0] += 1
                act.wait_ge(exp_in, exps[0])
                act.activation(dst, src, ACT.Exp, scale=scale).then_inc(exp_out, 1)

            def hidden_exp(g):
                exponential(gate[g], hidden[g][:, :, 0:INNER], -1.0)

            def split_x2(g):
                bank = arrived(g, "x2")
                act.copy(flat(x2t_hi[g]), bank).then_inc(x2t_hi_ready, 1)
                act.wait_ge(x2t_ready, g + 1)
                act.sem_inc(link_read[g]["act"], 1)
                act.sem_inc(link_fed[g]["act"], 1)

            def weight_chunks(g, n):
                if n == 0:
                    act.wait_ge(weights_ready, g + 1)
                if n >= 2:
                    if g < GROUPS - 1:
                        act.wait_ge(sums_ready[g], n - 1)
                    else:
                        act.wait_ge(sums_used, n - 1)
                for c in range(BY_ACT[g]):
                    f = n * CHUNKS + c
                    act.wait_ge(f_ready[g], f + 1)
                    for h in range(2):
                        e = 2 * c + h
                        last = act.activation(part_of(g, n)[:, e * D:(e + 1) * D],
                                              banks[g][:, c, h * D:(h + 1) * D], ACT.Copy,
                                              scale=weight[g][:, n, e:e + 1])
                    last.then_inc(f_used[g]["act"], 1)
                    act.wait_ge(f_used[g]["act"], weighted_by(g, f)[1])
                    act.sem_inc(scaled_ready[g], 1)

            def route_exp(g):
                exponential(gap[:, :], gap[:, :])

            def experts_high(k):
                act.wait_ge(raw_in[k], 16)
                act.copy(wall_hi[:, k, 0:WIDE].rearrange("p (e r) -> p e r", e=EXPERTS),
                         raw[k].rearrange("p (r e) -> p e r", e=EXPERTS)).then_inc(wall_hi_ready, 1)

            high_parts(0, 7)
            act.wait_ge(wt_ready, 1)
            for k in range(KT):
                act.copy(wall_hi[:, k, WIDE:], banks[1][:, 2 + k, 0:D + EXPERTS]).then_inc(wall_hi_ready, 1)
            high_parts(7, GIVEN[1] + RING)
            rounded(0, scaled[0])
            rounded(0, hidden[0], OWN)
            high_parts(GIVEN[1] + RING, B * UPB)
            row_of(0, "row1")
            hidden_exp(0)
            experts_high(0)
            rounded(0, act_sb[0])
            rounded(0, gate[0], OWN)
            rounded(1, scaled[1])
            rounded(1, hidden[1], OWN)
            row_of(0, "row2")
            experts_high(1)
            row_of(1, "row1")
            hidden_exp(1)
            split_x2(0)
            route_exp(0)
            weight_chunks(0, 0)
            rounded(1, act_sb[1])
            rounded(1, gate[1], OWN)
            weight_chunks(0, 1)
            row_of(1, "row2")
            weight_chunks(0, 2)
            weight_chunks(0, 3)
            split_x2(1)
            route_exp(1)
            for n in range(NT):
                weight_chunks(1, n)

        @block.vector
        def _(dve):
            count = [0]

            def then(ins):
                count[0] += 1
                ins.then_inc(chain, 1)
                dve.wait_ge(chain, count[0])

            exps, powers = [0], [0]

            def arrived(g, name):
                dve.wait_ge(link_ready[g], links[name]["number"] + 1)
                return banks_of(g, name)

            def was_read(g, name, ins):
                ins.then_inc(link_read[g]["dve"], 1)
                dve.wait_ge(link_read[g]["dve"], links[name]["read"])

            def feed(g, ins):
                ins.then_inc(link_fed[g]["dve"], 1)

            def fed_now(g, name):
                dve.wait_ge(link_fed[g]["dve"], links[name]["fed"])

            def exponential(ins):
                exps[0] += 1
                ins.then_inc(exp_in, 1)

            def exp_made():
                dve.wait_ge(exp_out, exps[0])

            def ask_power(ins):
                powers[0] += 1
                ins.then_inc(pow_in, 1)
                return powers[0]

            def statistics(g, src, tiles=range(NT)):
                for n in tiles:
                    ins = dve.bn_stats(st[g][:, n, :], src[:, n, :])
                then(ins)
                for n in tiles:
                    ins = dve.bn_aggr(mv[g][:, n, :], st[g][:, n, :])
                then(ins)
                return ask_power(dve.tensor_scalar(base[g][:, 0:len(tiles)], mv[g][:, tiles[0]:tiles[-1] + 1, 1],
                                                   EPS_LN, None, ALU.add))

            def normalise(g, src, dst, answer, tiles=range(NT)):
                dve.wait_ge(pow_out, answer)
                for k, n in enumerate(tiles):
                    yield dve.tensor_scalar(dst[:, n, :], src[:, n, :], mv[g][:, n, 0:1], root[g][:, k:k + 1],
                                            ALU.subtract, ALU.mult)

            def row_scales(g, src, scales, own=0):
                rounds[0] += 1
                then(dve.tensor_reduce(scales, src, AX.X, ALU.max, apply_absolute_value=True))
                then(dve.tensor_scalar(scales, scales, EPS_Q, 1.0 / QMAX, ALU.max, ALU.mult))
                inverse = inv[g][rounds[0] % 2]
                dve.reciprocal(inverse, scales).then_inc(round_in, 1)
                if own:
                    dve.wait_ge(round_in, rounds[0])
                    for n in range(own):
                        ins = dve.tensor_scalar(src[:, n, :], src[:, n, :], inverse[:, n:n + 1], ROUND,
                                                ALU.mult, ALU.add)
                    count[0] += 1
                    ins.then_inc(chain, 1)
                return rounds[0]

            def integers(dst, src, count):
                dve.wait_ge(round_out, count)
                return dve.tensor_scalar(dst, src, ROUND, QMAX, ALU.subtract, ALU.min)

            def turned(g, name, dst):
                src = arrived(g, name).bitcast(BF16)
                was_read(g, name, dve.tensor_scalar(flat(dst), src, -QMAX, None, ALU.max))

            rounds = [0]

            def ask_balance(g, inv_amax_weight, n):
                return ask_power(dve.scalar_tensor_tensor(base[g][:, 0:n], amax_x[g][:, 0:n], EPS_Q, inv_amax_weight,
                                                          ALU.max, ALU.mult))

            def balance(g, answer, n):
                s, u = smooth[g][:, 0:n], unsmooth[g][:, 0:n]
                dve.wait_ge(pow_out, answer)
                then(dve.tensor_scalar(s, root[g][:, 0:n], EPS_Q, None, ALU.max))
                then(dve.reciprocal(u, s))
                return s, u

            def diagonal(g, at, values, n):
                return dve.tensor_tensor(diag[g][:, at:at + n, :],
                                         ident[:, :].unsqueeze(1).broadcast_to([P, n, P]),
                                         values.unsqueeze(2).broadcast_to([P, n, P]), ALU.mult)

            def largest(dst, src, n):
                return dve.tensor_reduce(dst, src.rearrange("p (n t) -> p n t", n=n), AX.X, ALU.max,
                                         apply_absolute_value=True)

            def prepare(g):
                was_read(g, "prep", largest(amax_w[g], arrived(g, "prep"), NB * KT))
                then(dve.tensor_scalar(amax_w[g], amax_w[g], EPS_Q, None, ALU.max))
                then(dve.reciprocal(inv_amax_w[g], amax_w[g]))

            def prepare_second(g):
                was_read(g, "prepd", largest(amax_d[g], arrived(g, "prepd")[:, 0:NB * S], NB))
                then(dve.tensor_scalar(amax_d[g], amax_d[g], EPS_Q, None, ALU.max))
                then(dve.reciprocal(inv_amax_d[g], amax_d[g]))

            def wide(a, n):
                return a.rearrange("p (b n) -> p b n", b=NB).unsqueeze(2).broadcast_to([P, NB, TB, n])

            def tiles(a):
                return a.rearrange("p (b j) d -> p b j d", b=NB)

            def start(g):
                dve.wait_ge(xb_ready, g + 1)
                dve.wait_ge(o_used, NB * UPB * (g + 1))
                y = banks[g][:, 0:NB, :].rearrange("p b (j d) -> p (b j) d", j=TB)
                then(dve.tensor_tensor(y1[g], y, xb[g], ALU.add))
                return statistics(g, y1[g])

            def normalise_first(g, answer):
                for n, ins in enumerate(normalise(g, y1[g], x1[g], answer)):
                    if n == NT - 1:
                        feed(g, ins)
                fed_now(g, "x1")

            def ask_balance_first(g):
                was_read(g, "x1", largest(amax_x[g], arrived(g, "x1"), NB * KT))
                return ask_balance(g, inv_amax_w[g], NB * KT)

            def balance_first(g, answer):
                s, u = balance(g, answer, NB * KT)
                diagonal(g, 0, u, NB * KT)
                feed(g, diagonal(g, NB * KT, s, NB * KT))

            def quantise_first(g):
                bank = arrived(g, "scale")
                then(dve.tensor_tensor(tiles(scaled[g]), tiles(x1[g]), wide(bank[:, 0:NB * D], D), ALU.mult))
                x_round = row_scales(g, scaled[g], x_scale[g])
                was_read(g, "scale", dve.tensor_tensor(tiles(hidden[g]), tiles(gu_sb[g]),
                                                       wide(bank[:, NB * D:2 * NB * D], D), ALU.mult))
                w_round = row_scales(g, hidden[g], w_scale[g], OWN)
                feed(g, integers(q_rows[g][:, 0:NT, :], scaled[g], x_round))
                dve.wait_ge(chain, count[0])
                feed(g, integers(q_rows[g][:, NT:2 * NT, :], hidden[g], w_round))
                feed(g, diagonal(g, 0, w_scale[g], NT))

            def operands_first(g):
                turned(g, "xq", q_t[g][:, 0:NB * KT, :])
                turned(g, "wq", q_t[g][:, NB * KT:2 * NB * KT, :])
                dve.sem_inc(link_fed[g]["dve"], 1)

            def dequantise(g, name, row_name, dst):
                bank = arrived(g, name)
                dve.wait_ge(link_read[g]["act"], links[row_name]["read"])
                for n in range(NT):
                    ins = dve.scalar_tensor_tensor(dst[:, n, :], bank[:, n * D:(n + 1) * D],
                                                   x_scale[g][:, n:n + 1], row[g][:, n // TB, :], ALU.mult, ALU.mult)
                was_read(g, name, ins)

            def first_layer(g):
                dequantise(g, "mm1", "row1", hidden[g])
                dve.sem_inc(exp_in, 1)
                exps[0] += 1
                then(dve.tensor_tensor(act_sb[g], hidden[g][:, :, 0:INNER], hidden[g][:, :, INNER:], ALU.mult))

            def activate(g):
                exp_made()
                then(dve.tensor_scalar(gate[g], gate[g], 1.0, None, ALU.add))
                then(dve.reciprocal(gate[g], gate[g]))
                feed(g, dve.tensor_tensor(act_sb[g], act_sb[g], gate[g], ALU.mult))
                fed_now(g, "act")

            def ask_balance_second(g):
                was_read(g, "act", largest(amax_x[g][:, 0:NB], arrived(g, "act")[:, 0:NB * S], NB))
                return ask_balance(g, inv_amax_d[g], NB)

            def balance_second(g, answer):
                s, u = balance(g, answer, NB)
                diagonal(g, NT, u, NB)
                feed(g, diagonal(g, NT + NB, s, NB))

            def quantise_second(g):
                bank = arrived(g, "scale2")
                then(dve.tensor_tensor(tiles(act_sb[g]), tiles(act_sb[g]), wide(bank[:, 0:NB * P], P), ALU.mult))
                x_round = row_scales(g, act_sb[g], x_scale[g])
                was_read(g, "scale2", dve.tensor_tensor(tiles(gate[g]), tiles(dw_sb[g]),
                                                        wide(bank[:, NB * P:2 * NB * P], P), ALU.mult))
                w_round = row_scales(g, gate[g], w_scale[g], OWN)
                integers(q_rows[g][:, 0:NT, 0:INNER], act_sb[g], x_round)
                dve.wait_ge(chain, count[0])
                feed(g, integers(q_rows[g][:, NT:2 * NT, 0:INNER], gate[g], w_round))
                feed(g, diagonal(g, 0, w_scale[g], NT))

            def operands_second(g):
                turned(g, "q2", q_t[g][:, 0:2 * NB, :])
                dve.sem_inc(link_fed[g]["dve"], 1)

            def second_layer(g):
                dequantise(g, "mm2", "row2", y1[g])
                then(dve.tensor_tensor(y1[g], y1[g], x1[g], ALU.add))
                return statistics(g, y1[g])

            def normalise_second(g, answer):
                for n, ins in enumerate(normalise(g, y1[g], x2[g], answer)):
                    if n == NT - 1:
                        feed(g, ins)
                fed_now(g, "x2")

            def split_x2(g):
                bank = arrived(g, "x2")
                dve.wait_ge(x2t_hi_ready, g + 1)
                dve.tensor_tensor(flat(x2t_lo[g]), bank, flat(x2t_hi[g]).bitcast(F32),
                                  ALU.subtract).then_inc(x2t_ready, 1)

            def read_logits(g):
                arrived(g, "gate")
                then(dve.tensor_scalar(logit[:, :, :], banks[g][:, :, D:D + EXPERTS], CLIP, -CLIP, ALU.min, ALU.max))
                was_read(g, "gate", dve.tensor_tensor(x2[g], banks[g][:, :, 0:D], x2[g], ALU.add))

            def route(g):
                for n in range(NT):
                    ins = dve.max(top[:, n, :], logit[:, n, :])
                then(ins)
                exponential(dve.tensor_tensor(gap[:, :], top[:, :, 1], top[:, :, 0], ALU.subtract))
                for n in range(NT):
                    ins = dve.max_index(top_at[:, n, :], top[:, n, :], logit[:, n, :])
                then(ins)
                then(dve.tensor_copy(top_f[:, :, :], top_at[:, :, 0:2]))
                exp_made()
                then(dve.tensor_scalar(share[:, :, 0], gap[:, :], 1.0, None, ALU.add))
                then(dve.reciprocal(share[:, :, 0], share[:, :, 0]))
                then(dve.tensor_tensor(share[:, :, 1], gap[:, :], share[:, :, 0], ALU.mult))
                for k, dst in enumerate((weight[g], second)):
                    every = iota8[:, :].unsqueeze(1).broadcast_to([P, NT, EXPERTS])
                    then(dve.tensor_tensor(dst[:, :, :], every,
                                           top_f[:, :, k:k + 1].broadcast_to([P, NT, EXPERTS]), ALU.is_equal))
                    then(dve.tensor_tensor(dst[:, :, :], dst[:, :, :],
                                           share[:, :, k:k + 1].broadcast_to([P, NT, EXPERTS]), ALU.mult))
                dve.tensor_tensor(weight[g][:, :, :], weight[g][:, :, :], second[:, :, :], ALU.add)\
                   .then_inc(weights_ready, 1)
                dve.wait_ge(weights_ready, g + 1)

            def mix(g, n):
                dst = x2[g][:, n, :]
                for c in range(BY_ACT[g], CHUNKS):
                    f = n * CHUNKS + c
                    dve.wait_ge(f_ready[g], f + 1)
                    for h in range(2):
                        e = 2 * c + h
                        ins = dve.scalar_tensor_tensor(dst, banks[g][:, c, h * D:(h + 1) * D],
                                                       weight[g][:, n, e:e + 1], dst, ALU.mult, ALU.add)
                        if h == 0:
                            then(ins)
                    ins.then_inc(f_used[g]["dve"], 1)
                    dve.wait_ge(f_used[g]["dve"], weighted_by(g, f)[1])
                dve.wait_ge(sums_ready[g], n + 1)
                dve.tensor_tensor(dst, part_of(g, n)[:, 0:D], dst, ALU.add).then_inc(sums_used, 1)
                dve.wait_ge(sums_used, n + 1)

            def finish(g, tiles=range(NT)):
                for ins in normalise(g, x2[g], result[g], statistics(g, x2[g], tiles), tiles):
                    ins.then_inc(result_ready, 1)

            def low_parts(first, last):
                for u in range(first, last):
                    if low_by_dve(u):
                        low_part(dve, u, o_lo_dve)

            low_parts(0, 7)
            for k in range(KT):
                dve.wait_ge(wall_hi_ready, k + 1)
                ins = dve.tensor_tensor(wall_lo[:, k, WIDE:], banks[1][:, 2 + k, 0:D + EXPERTS],
                                        wall_hi[:, k, WIDE:].bitcast(F32), ALU.subtract)
            ins.then_inc(wt_used, 1)
            low_parts(7, 10)
            prepare(0)
            low_parts(10, 13)
            prepare_second(0)
            low_parts(13, NB * UPB)
            normalise_first(0, start(0))
            balance_first(0, ask_balance_first(0))
            prepare(1)
            quantise_first(0)
            prepare_second(1)
            operands_first(0)
            first_layer(0)
            activate(0)
            norm = start(1)
            balanced = ask_balance_second(0)
            normalise_first(1, norm)
            balance_second(0, balanced)
            balance_first(1, ask_balance_first(1))
            quantise_second(0)
            quantise_first(1)
            operands_second(0)
            operands_first(1)
            normalise_second(0, second_layer(0))
            first_layer(1)
            split_x2(0)
            activate(1)
            read_logits(0)
            balance_second(1, ask_balance_second(1))
            route(0)
            quantise_second(1)
            operands_second(1)
            norm = second_layer(1)
            normalise_second(1, norm)
            split_x2(1)
            read_logits(1)
            route(1)
            dve.wait_ge(sums_ready[0], NT)
            finish(0)
            for n in range(NT):
                mix(1, n)
                finish(1, [n])


def program(nc, inputs, out):
    a = inputs
    table = nc.dram_tensor("table", (TABLE_ROWS, EXPERTS), F32, kind="Internal").ap()
    with ExitStack() as ctx:
        def sb(name, shape, dt=F32):
            return ctx.enter_context(nc.sbuf_tensor(name, shape, dt))

        kept = (sb("ident", [P, P]), sb("ot", [P, HEADS * T]), sb("wo_hi", [P, HEADS, D], F32R),
                sb("wo_lo", [P, HEADS, D], F32R))
        w = [a[f"L0_attn_w{m}_{part}"] for m in "qkvo" for part in ("codes", "scales")]
        attention(nc, a["x"], w, [a[f"L0_attn_b{m}"] for m in "qkv"],
                  [a["L0_ffn_mask_idx"], a["L0_ffn_importance"], a["L0_ffn_atoms"],
                   a["L0_ffn_expert_atom_weights"], table], kept)
        layers(nc, a["x"], a["L0_attn_bo"], a["fside_BxS2xS2_0"], a["ctx_1024"], a["L0_ffn_gate_w"],
               a["L0_ffn_W"], table, out, kept)


_INS = ["x", "fside_BxS2xS2_0", "ctx_1024",
        "L0_attn_wq_codes", "L0_attn_wq_scales", "L0_attn_bq", "L0_attn_wk_codes", "L0_attn_wk_scales",
        "L0_attn_bk", "L0_attn_wv_codes", "L0_attn_wv_scales", "L0_attn_bv", "L0_attn_wo_codes",
        "L0_attn_wo_scales", "L0_attn_bo", "L0_ffn_gate_w", "L0_ffn_W", "L0_ffn_atoms",
        "L0_ffn_expert_atom_weights", "L0_ffn_importance", "L0_ffn_mask_idx"]


def kernel(**inputs):
    import numpy as np
    import concourse.bacc as bacc
    from concourse.bass_utils import run_bass_kernel_spmd

    nc = bacc.Bacc("TRN2", target_bir_lowering=False, num_devices=1)
    arrays, args = {}, {}
    for name in _INS:
        a = np.ascontiguousarray(inputs[name])
        arrays["in_" + name] = a
        args[name] = nc.dram_tensor("in_" + name, a.shape, mybir.dt.from_np(a.dtype), kind="ExternalInput").ap()
    out = nc.dram_tensor("out_0", (B, S, D), F32, kind="ExternalOutput").ap()
    program(nc, args, out)
    r = run_bass_kernel_spmd(nc, [arrays], core_ids=[0])
    return r.results[0]["out_0"]
```
